# Optimizing a Trainium2 kernel written in Bass

```python
import numpy as np
import jax
import jax.numpy as jnp

def _softmax(x, axis=-1):
    return jax.nn.softmax(x, axis=axis)

def _gelu(x):
    return jax.nn.gelu(x, approximate=True)

def _silu(x):
    return jax.nn.silu(x)

def _sigmoid(x):
    return jax.nn.sigmoid(x)

def _layernorm(x, axis=-1, eps=1e-05):
    m = jnp.mean(x, axis=axis, keepdims=True)
    v = jnp.var(x, axis=axis, keepdims=True)
    return (x - m) / jnp.sqrt(v + eps)

def _scatter_add(tgt, idx, src, axis=0):
    return tgt.at[idx].add(src)

def _segment_sum(src, seg, n):
    return jax.ops.segment_sum(src, seg, n)
kernel_name = 'mk_seq_preln_d2_jaxref_r8_3043c1'

def setup_inputs(seed: int=0):
    np.random.seed(seed)
    _w = jnp.asarray

    def _L0_attn_setup():
        import jax, jax.numpy as jnp
        import numpy as np
        DIM = 128
        C = 128
        B = 8
        T = 256
        key = jax.random.key(seed)
        ks = jax.random.split(key, 16)
        s = 0.02
        inp = {'x': jax.random.normal(ks[0], (B, T, DIM), dtype=jnp.float32), 'Wq': jax.random.normal(ks[1], (DIM, C), dtype=jnp.float32) * s, 'bq': jnp.zeros((C,), dtype=jnp.float32), 'Wk': jax.random.normal(ks[2], (DIM, C), dtype=jnp.float32) * s, 'bk': jnp.zeros((C,), dtype=jnp.float32), 'Wv': jax.random.normal(ks[3], (DIM, C), dtype=jnp.float32) * s, 'bv': jnp.zeros((C,), dtype=jnp.float32), 'Wa': jax.random.normal(ks[4], (DIM, 1), dtype=jnp.float32) * s, 'ba': jnp.zeros((1,), dtype=jnp.float32), 'Wb': jax.random.normal(ks[5], (DIM, 1), dtype=jnp.float32) * s, 'bb': jnp.zeros((1,), dtype=jnp.float32), 'Wg': jax.random.normal(ks[6], (DIM, C), dtype=jnp.float32) * s, 'bg': jnp.zeros((C,), dtype=jnp.float32), 'Wo': jax.random.normal(ks[7], (C, DIM), dtype=jnp.float32) * s, 'bo': jnp.zeros((DIM,), dtype=jnp.float32)}
        return inp
    _L0_attn_in = _L0_attn_setup()

    def _L0_ffn_setup():
        import jax, jax.numpy as jnp
        import numpy as np
        H, E, DFF = (128, 8, 512)
        key = jax.random.key(seed)
        ks = jax.random.split(key, 7)
        s = lambda *shape: 1.0 / np.sqrt(shape[-2] if len(shape) > 1 else shape[-1])
        x = jax.random.normal(ks[0], (2, 256, H), dtype=jnp.float32)
        Wr = jax.random.normal(ks[1], (H, E), dtype=jnp.float32) * (1.0 / np.sqrt(H))
        br = jnp.zeros((E,), dtype=jnp.float32)
        W1 = jax.random.normal(ks[2], (E, H, DFF), dtype=jnp.float32) * (1.0 / np.sqrt(H))
        b1 = jnp.zeros((E, DFF), dtype=jnp.float32)
        W2 = jax.random.normal(ks[3], (E, DFF, H), dtype=jnp.float32) * (1.0 / np.sqrt(DFF))
        b2 = jnp.zeros((E, H), dtype=jnp.float32)
        return {'x': x, 'Wr': Wr, 'br': br, 'W1': W1, 'b1': b1, 'W2': W2, 'b2': b2}
    _L0_ffn_in = _L0_ffn_setup()

    def _L1_attn_setup():
        import jax, jax.numpy as jnp
        import numpy as np
        HEADS = 8
        DIM_HEAD = 128
        ATTN_MATRIX_SCALE = 1.5
        SCALE = DIM_HEAD ** (-0.5)

        def _split_heads(t):
            b, n, _ = t.shape
            t = t.reshape(b, n, HEADS, DIM_HEAD)
            return t.transpose(2, 0, 1, 3).reshape(HEADS, b * n, DIM_HEAD)
        key = jax.random.key(seed)
        ks = jax.random.split(key, 7)
        b, n, m = (2, 256, 256)
        qd, cd, inner = (128, 96, HEADS * DIM_HEAD)
        x = jax.random.normal(ks[0], (b, n, qd), dtype=jnp.float32)
        context = jax.random.normal(ks[1], (b, m, cd), dtype=jnp.float32)
        Wq = jax.random.normal(ks[2], (qd, inner), dtype=jnp.float32) * qd ** (-0.5)
        Wk = jax.random.normal(ks[3], (cd, inner), dtype=jnp.float32) * cd ** (-0.5)
        Wv = jax.random.normal(ks[4], (cd, inner), dtype=jnp.float32) * cd ** (-0.5)
        Wout = jax.random.normal(ks[5], (inner, qd), dtype=jnp.float32) * inner ** (-0.5)
        bout = jnp.zeros((qd,), dtype=jnp.float32)
        return {'x': x, 'context': context, 'Wq': Wq, 'Wk': Wk, 'Wv': Wv, 'Wout': Wout, 'bout': bout}
    _L1_attn_in = _L1_attn_setup()

    def _L1_ffn_setup():
        import jax, jax.numpy as jnp
        import numpy as np
        B, S, D, F, E, K = (4, 256, 128, 512, 8, 2)
        key = jax.random.key(seed)
        ks = jax.random.split(key, 8)
        x = jax.random.normal(ks[0], (B, S, D), dtype=jnp.float32)
        router_w = jax.random.normal(ks[1], (E, D), dtype=jnp.float32) * 0.02
        w1_w = jax.random.normal(ks[2], (E, F, D), dtype=jnp.float32) * 0.02
        w1_b = jax.random.normal(ks[3], (E, F), dtype=jnp.float32) * 0.02
        w2_w = jax.random.normal(ks[4], (E, D, F), dtype=jnp.float32) * 0.02
        w2_b = jax.random.normal(ks[5], (E, D), dtype=jnp.float32) * 0.02
        wg_w = jax.random.normal(ks[6], (E, F, D), dtype=jnp.float32) * 0.02
        wg_b = jax.random.normal(ks[7], (E, F), dtype=jnp.float32) * 0.02
        return {'x': x, 'router_w': router_w, 'w1_w': w1_w, 'w1_b': w1_b, 'w2_w': w2_w, 'w2_b': w2_b, 'wg_w': wg_w, 'wg_b': wg_b}
    _L1_ffn_in = _L1_ffn_setup()
    _d = {'L0_attn_x': _L0_attn_in['x'], 'L0_attn_Wq': _L0_attn_in['Wq'], 'L0_attn_bq': _L0_attn_in['bq'], 'L0_attn_Wk': _L0_attn_in['Wk'], 'L0_attn_bk': _L0_attn_in['bk'], 'L0_attn_Wv': _L0_attn_in['Wv'], 'L0_attn_bv': _L0_attn_in['bv'], 'L0_attn_Wa': _L0_attn_in['Wa'], 'L0_attn_ba': _L0_attn_in['ba'], 'L0_attn_Wb': _L0_attn_in['Wb'], 'L0_attn_bb': _L0_attn_in['bb'], 'L0_attn_Wg': _L0_attn_in['Wg'], 'L0_attn_bg': _L0_attn_in['bg'], 'L0_attn_Wo': _L0_attn_in['Wo'], 'L0_attn_bo': _L0_attn_in['bo'], 'L0_ffn_Wr': _L0_ffn_in['Wr'], 'L0_ffn_br': _L0_ffn_in['br'], 'L0_ffn_W1': _L0_ffn_in['W1'], 'L0_ffn_b1': _L0_ffn_in['b1'], 'L0_ffn_W2': _L0_ffn_in['W2'], 'L0_ffn_b2': _L0_ffn_in['b2'], 'L1_attn_context': _L1_attn_in['context'], 'L1_attn_Wq': _L1_attn_in['Wq'], 'L1_attn_Wk': _L1_attn_in['Wk'], 'L1_attn_Wv': _L1_attn_in['Wv'], 'L1_attn_Wout': _L1_attn_in['Wout'], 'L1_attn_bout': _L1_attn_in['bout'], 'L1_ffn_router_w': _L1_ffn_in['router_w'], 'L1_ffn_w1_w': _L1_ffn_in['w1_w'], 'L1_ffn_w1_b': _L1_ffn_in['w1_b'], 'L1_ffn_w2_w': _L1_ffn_in['w2_w'], 'L1_ffn_w2_b': _L1_ffn_in['w2_b'], 'L1_ffn_wg_w': _L1_ffn_in['wg_w'], 'L1_ffn_wg_b': _L1_ffn_in['wg_b']}
    _x0 = _d['L0_attn_x']
    _d['L0_attn_x'] = jax.random.normal(jax.random.fold_in(jax.random.key(seed), 1), (4, 512, 128), dtype=_x0.dtype)
    del _x0
    return _d

def reference(L0_attn_x, L0_attn_Wq, L0_attn_bq, L0_attn_Wk, L0_attn_bk, L0_attn_Wv, L0_attn_bv, L0_attn_Wa, L0_attn_ba, L0_attn_Wb, L0_attn_bb, L0_attn_Wg, L0_attn_bg, L0_attn_Wo, L0_attn_bo, L0_ffn_Wr, L0_ffn_br, L0_ffn_W1, L0_ffn_b1, L0_ffn_W2, L0_ffn_b2, L1_attn_context, L1_attn_Wq, L1_attn_Wk, L1_attn_Wv, L1_attn_Wout, L1_attn_bout, L1_ffn_router_w, L1_ffn_w1_w, L1_ffn_w1_b, L1_ffn_w2_w, L1_ffn_w2_b, L1_ffn_wg_w, L1_ffn_wg_b):

    def _L0_attn_ref(x, Wq, bq, Wk, bk, Wv, bv, Wa, ba, Wb, bb, Wg, bg, Wo, bo):
        import jax, jax.numpy as jnp
        import numpy as np
        DIM = 128
        C = 128
        B = 8
        T = 256
        q = x @ Wq + bq
        kr = x @ Wk + bk
        k = kr / jnp.maximum(jnp.linalg.norm(kr, axis=-1, keepdims=True), 1e-12)
        v = x @ Wv + bv
        alpha = jax.nn.sigmoid(x @ Wa + ba)
        beta = jax.nn.sigmoid(x @ Wb + bb)
        gate = jax.nn.sigmoid(x @ Wg + bg)

        def step(S, inp):
            q_t, k_t, v_t, a_t, b_t, g_t = inp
            Sk = jnp.einsum('bij,bj->bi', S, k_t)
            a = a_t[:, :, None]
            b = b_t[:, :, None]
            S_new = a * (S - b * (Sk[:, :, None] * k_t[:, None, :])) + b * (v_t[:, :, None] * k_t[:, None, :])
            o = jnp.einsum('bi,bij->bj', q_t, S_new) * g_t
            return (S_new, o)
        seq = (jnp.swapaxes(q, 0, 1), jnp.swapaxes(k, 0, 1), jnp.swapaxes(v, 0, 1), jnp.swapaxes(alpha, 0, 1), jnp.swapaxes(beta, 0, 1), jnp.swapaxes(gate, 0, 1))
        S0 = jnp.zeros((x.shape[0], C, C), dtype=x.dtype)
        _, outs = jax.lax.scan(step, S0, seq)
        o = jnp.swapaxes(outs, 0, 1)
        return o @ Wo + bo

    def _L0_ffn_ref(x, Wr, br, W1, b1, W2, b2):
        import jax, jax.numpy as jnp
        import numpy as np
        H, E, DFF = (128, 8, 512)
        B, S, Hd = x.shape
        n_exp = W1.shape[0]
        xt = x.reshape(-1, Hd)
        logits = xt @ Wr + br
        probs = jax.nn.softmax(logits, axis=-1)
        gate = jnp.max(probs, axis=-1)
        idx = jnp.argmax(probs, axis=-1)
        h1 = jnp.maximum(jnp.einsum('th,ehf->etf', xt, W1) + b1[:, None, :], 0.0)
        ye = jnp.einsum('etf,efh->eth', h1, W2) + b2[:, None, :]
        onehot = jax.nn.one_hot(idx, n_exp, dtype=xt.dtype)
        y = jnp.einsum('te,eth->th', onehot, ye) * gate[:, None]
        return y.reshape(B, S, Hd)

    def _L1_attn_ref(x, context, Wq, Wk, Wv, Wout, bout):
        import jax, jax.numpy as jnp
        import numpy as np
        HEADS = 8
        DIM_HEAD = 128
        ATTN_MATRIX_SCALE = 1.5
        SCALE = DIM_HEAD ** (-0.5)

        def _split_heads(t):
            b, n, _ = t.shape
            t = t.reshape(b, n, HEADS, DIM_HEAD)
            return t.transpose(2, 0, 1, 3).reshape(HEADS, b * n, DIM_HEAD)
        b, n, _ = x.shape
        qh = _split_heads(jnp.einsum('bnq,qi->bni', x, Wq))
        kh = _split_heads(jnp.einsum('bmc,ci->bmi', context, Wk))
        vh = _split_heads(jnp.einsum('bmc,ci->bmi', context, Wv))
        sim = jnp.einsum('hid,hjd->hij', qh, kh) * SCALE
        mean = jnp.mean(sim, axis=-1, keepdims=True)
        sim = (sim - mean) * ATTN_MATRIX_SCALE + mean
        attn = jax.nn.softmax(sim, axis=-1)
        out = jnp.einsum('hij,hjd->hid', attn, vh)
        out = out.reshape(HEADS, b, n, DIM_HEAD).transpose(1, 2, 0, 3)
        out = out.reshape(b, n, HEADS * DIM_HEAD)
        return jnp.einsum('bni,iq->bnq', out, Wout) + bout

    def _L1_ffn_ref(x, router_w, w1_w, w1_b, w2_w, w2_b, wg_w, wg_b):
        import jax, jax.numpy as jnp
        import numpy as np
        B, S, D, F, E, K = (4, 256, 128, 512, 8, 2)
        probs = jax.nn.softmax(jnp.einsum('bsd,ed->bse', x, router_w), axis=-1)
        token_probs, probs_idx = jax.lax.top_k(probs, K)
        gates = jnp.sum(token_probs[..., None] * jax.nn.one_hot(probs_idx, E, dtype=x.dtype), axis=-2)
        gates_e = jnp.moveaxis(gates, -1, 0)

        def body(acc, params):
            w1w, w1b, w2w, w2b, wgw, wgb, g = params
            y = jax.nn.gelu(jnp.einsum('bsd,fd->bsf', x, wgw) + wgb, approximate=False)
            h = y * (jnp.einsum('bsd,fd->bsf', x, w1w) + w1b)
            out = jnp.einsum('bsf,df->bsd', h, w2w) + w2b
            return (acc + out * g[..., None], None)
        acc0 = jnp.zeros_like(x)
        out, _ = jax.lax.scan(body, acc0, (w1_w, w1_b, w2_w, w2_b, wg_w, wg_b, gates_e))
        return out
    x = L0_attn_x
    x = x + _L0_attn_ref(_layernorm(x, axis=-1), L0_attn_Wq, L0_attn_bq, L0_attn_Wk, L0_attn_bk, L0_attn_Wv, L0_attn_bv, L0_attn_Wa, L0_attn_ba, L0_attn_Wb, L0_attn_bb, L0_attn_Wg, L0_attn_bg, L0_attn_Wo, L0_attn_bo)
    x = x + _L0_ffn_ref(_layernorm(x, axis=-1), L0_ffn_Wr, L0_ffn_br, L0_ffn_W1, L0_ffn_b1, L0_ffn_W2, L0_ffn_b2)
    x = x + _L1_attn_ref(_layernorm(x, axis=-1), L1_attn_context, L1_attn_Wq, L1_attn_Wk, L1_attn_Wv, L1_attn_Wout, L1_attn_bout)
    x = x + _L1_ffn_ref(_layernorm(x, axis=-1), L1_ffn_router_w, L1_ffn_w1_w, L1_ffn_w1_b, L1_ffn_w2_w, L1_ffn_w2_b, L1_ffn_wg_w, L1_ffn_wg_b)
    return x

_drawn_inputs = setup_inputs


def setup_inputs(seed=0):
    import zlib

    import numpy as np

    out = dict(_drawn_inputs(seed))
    spreads = {'L0_attn_bq': (0.0, 0.8),
     'L0_attn_bk': (0.0, 0.8),
     'L0_attn_bv': (0.0, 0.8),
     'L0_attn_bg': (0.0, 0.8),
     'L0_attn_bo': (0.0, 0.1),
     'L0_ffn_br': (0.0, 0.1),
     'L0_ffn_b1': (0.0, 0.303),
     'L0_ffn_b2': (0.0, 0.1),
     'L1_attn_bout': (0.0, 0.1)}
    factors = {'L0_attn_Wq': 5.786,
     'L0_attn_Wk': 4.792,
     'L0_attn_Wv': 3.79,
     'L0_attn_Wa': 8.0,
     'L0_attn_Wb': 8.0,
     'L0_attn_Wg': 8.0,
     'L0_attn_Wo': 4.679,
     'L1_ffn_router_w': 8.0,
     'L1_ffn_w1_w': 8.0,
     'L1_ffn_w1_b': 8.0,
     'L1_ffn_w2_w': 8.0,
     'L1_ffn_w2_b': 23.226,
     'L1_ffn_wg_w': 8.0,
     'L1_ffn_wg_b': 8.0}
    for name, (base, spread) in spreads.items():
        noise = np.random.default_rng([zlib.crc32(name.encode()), seed]).standard_normal(out[name].shape)
        drawn = base * np.exp(spread * noise) if base else spread * noise
        out[name] = jnp.asarray(drawn.astype(out[name].dtype))
    for name, factor in factors.items():
        out[name] = (out[name] * factor).astype(out[name].dtype)
    return out
```

```python
from contextlib import ExitStack

import concourse.bass as bass
from concourse import mybir

F32 = mybir.dt.float32
I32 = mybir.dt.int32
U32 = mybir.dt.uint32
ALU = mybir.AluOpType
ACT = mybir.ActivationFunctionType
AX = mybir.AxisListType

STAGE = 4
P = 128
SEQS, CHUNKS = 4, 4
TILES = SEQS * CHUNKS
D = 128
E = 8
F = 512
FT = F // P
HEADS = 8
KEYS = 512
KT_N = KEYS // P
CTX = 96
LEVELS = 7
ROW = 130
DEST, GATE = 128, 129
FAR = 1.0e6
SIM_SCALE = 128 ** -0.5
MATRIX_SCALE = 1.5
EPS = 1e-5
IDENT, TRI_INC, LOW_STRICT, UP_STRICT, ONES, PAIRS = 0, 1, 2, 3, 4, 5
V_EM8, V_KTH, V_TILE, V_ROW, V_SCAN, V_END = 0, 8, 24, 64, 80, 208


def slot_tiles(choices):
    return choices * TILES + E - 1


def last_col(ap, n):
    return ap.unsqueeze(2).broadcast_to([ap.shape[0], ap.shape[1], n])


def mid_col(ap, n):
    return ap.unsqueeze(1).broadcast_to([ap.shape[0], n, ap.shape[1]])


class Chain:

    def __init__(self, sem):
        self.sem, self.n = sem, 0

    def run(self, eng, ins):
        self.n += 1
        ins.then_inc(self.sem, 1)
        eng.wait_ge(self.sem, self.n)


def rsqrt(dve, chain, v, y, t):
    chain.run(dve, dve.tensor_scalar(y.bitcast(I32), v.bitcast(I32), 1, None, ALU.logical_shift_right))
    chain.run(dve, dve.tensor_scalar(y.bitcast(I32), y.bitcast(I32), -1.0, float(0x5F3759DF), ALU.mult, ALU.add))
    for _ in range(3):
        chain.run(dve, dve.tensor_tensor(t, y, y, ALU.mult))
        chain.run(dve, dve.scalar_tensor_tensor(t, t, -0.5, v, ALU.mult, ALU.mult))
        chain.run(dve, dve.scalar_tensor_tensor(y, t, 1.5, y, ALU.add, ALU.mult))


def layernorm_stats(dve, chain, X, st6, mv, var, rstd, tmp):
    for j in range(TILES):
        last = dve.bn_stats(st6[:, j, :], X[:, j, :])
    chain.run(dve, last)
    for j in range(TILES):
        last = dve.bn_aggr(mv[:, j, :], st6[:, j, :])
    chain.run(dve, last)
    chain.run(dve, dve.tensor_scalar(var[:, :], mv[:, :, 1], EPS, None, ALU.add))
    rsqrt(dve, chain, var[:, :], rstd[:, :], tmp[:, :])


def build(nc, a, out):
    with ExitStack() as top:
        def alloc(ctx):
            return lambda name, shape, dt=F32: ctx.enter_context(nc.sbuf_tensor(name, shape, dt))

        def sem(name):
            return top.enter_context(nc.semaphore(name))

        sb = alloc(top)
        bank = [top.enter_context(nc.psum_tensor(f"bank{i}", [P, 512], F32)) for i in range(8)]

        def quad(ap):
            return ap.rearrange("p (a n) -> p a n", a=4)

        X = sb("X", [P, TILES, D])
        C = sb("C", [P, 5 + LEVELS, P])
        V = sb("V", [P, V_END])
        ident = C[:, IDENT, :]
        mv = sb("mv", [P, TILES, 2])
        st6 = sb("st6", [P, TILES, 6])
        var = sb("var", [P, TILES])
        rstd = sb("rstd", [P, TILES])
        tmp = sb("tmp", [P, TILES])
        bo_b = sb("bo_b", [P, D])
        bout_b = sb("bout_b", [P, D])
        wr0 = sb("wr0", [P, E])
        br0 = sb("br0", [P, E])
        wr1 = sb("wr1", [P, E])
        fill = sb("fill", [P, ROW])
        plan_i = sb("plan_i", [P, TILES * 2], I32)
        expert_i = sb("expert_i", [1, 40], I32)

        slots = [nc.dram_tensor(f"slots{n}", [slot_tiles(n + 1) * P, ROW], F32, kind="Internal").ap()
                 for n in range(2)]
        byrow = [nc.dram_tensor(f"byrow{n}", [(n + 1) * TILES * P, D], F32, kind="Internal").ap()
                 for n in range(2)]

        chain = Chain(sem("s_chain"))
        s_x = sem("s_x")
        s_const = sem("s_const")
        s_w0 = sem("s_w0")
        s_ffn0 = sem("s_ffn0")
        s_fillz = sem("s_fillz")
        s_fill = sem("s_fill")
        s_attnw = sem("s_attnw")
        s_ffn1 = sem("s_ffn1")

        ffn = ExitStack()
        sf = alloc(ffn)
        w1a = sf("w1a", [P, E * F])
        w2a = sf("w2a", [P, E * F])
        b1a = sf("b1a", [P, E * F])
        b2a = sf("b2a", [P, E * D])

        ab = ExitStack()
        sa = alloc(ab)
        kvqg = sa("kvqg", [P, TILES, 4, D])
        dec = sa("dec", [P, 3, TILES])
        beta = sa("beta", [P, TILES])
        la = sa("la", [P, TILES])
        rn = sa("rn", [P, TILES])
        wo = sa("wo", [P, D])

        with ExitStack() as ctx:
            s1 = alloc(ctx)
            wcat = s1("wcat", [P, 512])
            bcat = s1("bcat", [P, 512])
            wab = s1("wab", [P, 2])
            bab = s1("bab", [P, 2])
            xn = [s1(f"xn{i}", [P, 4, D]) for i in range(2)]
            xnT = [s1(f"xnT{i}", [P, 512]) for i in range(2)]
            z = s1("z", [P, TILES, 2])
            az = s1("az", [P, TILES, 2])
            ez = s1("ez", [P, TILES, 2])
            lz = s1("lz", [P, TILES, 2])
            lb = s1("lb", [P, TILES])
            junk = s1("junk", [P, D])
            ss = s1("ss", [P, TILES])
            s_act = sem("a_act")
            s_xn = sem("a_xn")
            s_tr = sem("a_tr")
            s_xT = sem("a_xT")
            s_pj = sem("a_pj")
            s_ev = sem("a_ev")
            s_az = sem("a_az")
            s_lz = sem("a_lz")
            s_la = sem("a_la")
            s_cum = sem("a_cum")
            s_sq = sem("a_sq")
            block = ctx.enter_context(nc.Block())

            @block.sync
            def _(sp):
                sp.dma_start(X[:, :, :], a["x"]).then_inc(s_x, 16)
                sp.dma_start(C[:, :, :], a["consts"]).then_inc(s_const, 16)
                sp.dma_start(V[:, :], a["vecs"]).then_inc(s_const, 16)
                sp.dma_start(wcat[:, :], a["wcat"]).then_inc(s_w0, 16)
                sp.dma_start(bcat[:, :], a["bcat"].partition_broadcast(P)).then_inc(s_w0, 16)
                sp.dma_start(wab[:, :], a["wab"]).then_inc(s_w0, 16)
                sp.dma_start(bab[:, :], a["bab"].partition_broadcast(P)).then_inc(s_w0, 16)
                sp.dma_start(wo[:, :], a["wo"]).then_inc(s_w0, 16)
                sp.dma_start(bo_b[:, :], a["bo"].partition_broadcast(P)).then_inc(s_w0, 16)
                sp.dma_start(bout_b[:, :], a["bout"].partition_broadcast(P)).then_inc(s_w0, 16)
                sp.dma_start(wr0[:, :], a["wr0"]).then_inc(s_w0, 16)
                sp.dma_start(br0[:, :], a["br0"].partition_broadcast(P)).then_inc(s_w0, 16)
                sp.dma_start(wr1[:, :], a["wr1"]).then_inc(s_w0, 16)
                sp.dma_start(w1a[:, :], a["w1a"]).then_inc(s_ffn0, 16)
                sp.dma_start(w2a[:, :], a["w2a"]).then_inc(s_ffn0, 16)
                sp.dma_start(b1a[:, :], a["b1a"].partition_broadcast(P)).then_inc(s_ffn0, 16)
                sp.dma_start(b2a[:, :], a["b2a"].partition_broadcast(P)).then_inc(s_ffn0, 16)
                sp.wait_ge(s_fillz, 2)
                for n in range(2):
                    rows = slot_tiles(n + 1)
                    for r in range(0, rows, 4):
                        k = min(4, rows - r)
                        sp.dma_start(slots[n][r * P:(r + k) * P, :].rearrange("(a p) w -> p a w", p=P),
                                     mid_col(fill[:, :], k)).then_inc(s_fill, 16)

            @block.gpsimd
            def _(pool):
                pool.memset(fill[:, :], 0.0).then_inc(s_fillz, 1)
                pool.wait_ge(s_fillz, 1)
                pool.memset(fill[:, DEST:DEST + 1], FAR).then_inc(s_fillz, 1)

            @block.vector
            def _(dve):
                dve.wait_ge(s_x, 16)
                layernorm_stats(dve, chain, X, st6, mv, var, rstd, tmp)
                dve.wait_ge(s_w0, 16 * 10)
                with dve.Fori(0, 2) as gg:
                    for half in range(2):
                        dve.wait_ge(s_tr, gg * 2 + half + 1)
                        for k in range(4):
                            n = gg * 8 + half * 4 + k
                            last = dve.tensor_scalar(xn[half][:, k, :], X[:, bass.ds(n, 1), :].rearrange("p a n -> p (a n)"),
                                                     mv[:, bass.ds(n, 1), 0:1].rearrange("p a n -> p (a n)"),
                                                     rstd[:, bass.ds(n, 1)], ALU.subtract, ALU.mult)
                        last.then_inc(s_xn, 1)
                        for k in range(4):
                            n = gg * 8 + half * 4 + k
                            dve.wait_ge(s_pj, n + 9)
                            dve.tensor_tensor(kvqg[:, bass.ds(n, 1), :, :].rearrange("p a c n -> p (a c n)"),
                                              bank[2 + k][:, :], bcat[:, :], ALU.add).then_inc(s_ev, 1)
                chain.run(dve, dve.tensor_tensor(X[:, :, :], X[:, :, :], mid_col(bo_b[:, :], TILES), ALU.add))
                chain.run(dve, dve.tensor_tensor(z[:, :, :], bank[6][:, 0:2 * TILES].rearrange("p (a n) -> p a n", n=2),
                                            mid_col(bab[:, :], TILES), ALU.add))
                dve.scalar_tensor_tensor(az[:, :, :], z[:, :, :], -1.0, z[:, :, :], ALU.mult, ALU.max).then_inc(s_az, 1)
                dve.wait_ge(s_lz, 2)
                dve.scalar_tensor_tensor(lb[:, :], z[:, :, 1], 0.0, lz[:, :, 1], ALU.min, ALU.subtract).then_inc(s_la, 1)
                dve.scalar_tensor_tensor(la[:, :], z[:, :, 0], 0.0, lz[:, :, 0], ALU.min, ALU.subtract).then_inc(s_la, 1)
                dve.wait_ge(s_sq, TILES)
                chain.run(dve, dve.tensor_scalar(ss[:, :], ss[:, :], 1e-24, None, ALU.max))
                rsqrt(dve, chain, ss[:, :], rn[:, :], tmp[:, :])

            @block.tensor
            def _(pe):
                pe.sem_inc(s_tr, 2)
                pe.sem_inc(s_pj, 8)
                pe.wait_ge(s_const, 32)
                pe.wait_ge(s_w0, 16 * 10)
                with pe.Fori(0, 2) as gg:
                    for half in range(2):
                        g = gg * 2 + half
                        pe.wait_ge(s_xn, g + 1)
                        pe.wait_ge(s_xT, g + 1)
                        for k in range(4):
                            last = pe.transpose(bank[half][:, k * P:(k + 1) * P], xn[half][:, k, :], ident)
                        last.then_inc(s_tr, 1)
                        pe.wait_ge(s_xT, g + 3)
                        for k in range(4):
                            n = g * 4 + k
                            pe.wait_ge(s_ev, n + 1)
                            pe.matmul(bank[6][:, bass.ds(n * 2, 2)], xnT[half][:, k * P:(k + 1) * P], wab[:, :],
                                      start=True, stop=True)
                            pe.matmul(bank[2 + k][:, :], xnT[half][:, k * P:(k + 1) * P], wcat[:, :],
                                      start=True, stop=True).then_inc(s_pj, 1)
                pe.wait_ge(s_la, 2)
                pe.matmul(bank[7][:, 0:16], C[:, TRI_INC, :], la[:, :], start=True, stop=True)
                pe.matmul(bank[7][:, 16:32], C[:, LOW_STRICT, :], la[:, :], start=True, stop=True)
                pe.matmul(bank[7][:, 32:48], C[:, ONES, :], la[:, :], start=True, stop=True).then_inc(s_cum, 1)

            @block.scalar
            def _(act):
                act.sem_inc(s_xT, 2)
                act.sem_inc(s_ev, 4)
                with act.Fori(0, 2) as gg:
                    for half in range(2):
                        g = gg * 2 + half
                        act.wait_ge(s_tr, g + 3)
                        act.wait_ge(s_pj, g * 4 + 4)
                        act.activation(xnT[half][:, :], bank[half][:, :], ACT.Copy).then_inc(s_xT, 1)
                act.wait_ge(s_ev, 4 + TILES)
                act.activation(kvqg[:, :, 3, :], kvqg[:, :, 3, :], ACT.Sigmoid)
                with act.Fori(0, TILES) as n:
                    act.wait_ge(s_act, n)
                    act.activation(junk[:, :], kvqg[:, bass.ds(n, 1), 0, :].rearrange("p a n -> p (a n)"), ACT.Square,
                                   accum_out=ss[:, bass.ds(n, 1)]).then_inc(s_act, 1)
                act.wait_ge(s_act, TILES)
                act.sem_inc(s_sq, TILES)
                act.wait_ge(s_az, 1)
                act.activation(ez[:, :, :], az[:, :, :], ACT.Exp, scale=-1.0).then_inc(s_lz, 1)
                act.wait_ge(s_lz, 1)
                act.activation(lz[:, :, :], ez[:, :, :], ACT.Ln, bias=1.0).then_inc(s_lz, 1)
                act.wait_ge(s_la, 1)
                act.activation(beta[:, :], lb[:, :], ACT.Exp)
                act.wait_ge(s_cum, 1)
                act.activation(dec[:, :, :].rearrange("p a n -> p (a n)"), bank[7][:, 0:48], ACT.Exp)

        with ExitStack() as ctx:
            s2 = alloc(ctx)
            bgK = s2("bgK", [P, TILES, P])
            EK = s2("EK", [P, TILES, P])
            QT = s2("QT", [P, TILES, P])
            gQT = s2("gQT", [P, TILES, P])
            gateT = s2("gateT", [P, TILES, P])
            DT = s2("DT", [P, TILES, P])
            AT = s2("AT", [P, TILES, P])
            AM = s2("AM", [P, TILES, P])
            XL = s2("XL", [P, TILES, P])
            TI = s2("TI", [P, TILES, P])
            RI = s2("RI", [P, TILES, P])
            t_a = s2("t_a", [P, 4, P])
            kb, gQ, rla = TI, XL, AM
            d_kn = sem("b_kn")
            d_kb = sem("b_kb")
            p_el = sem("b_el")
            p_dt = sem("b_dt")
            q_tr = sem("b_tr")
            q_lt = sem("b_lt")
            q_at = sem("b_at")
            a_ev = sem("b_aev")
            a_lt = sem("b_alt")
            d_ev = sem("b_dev")
            d_at = sem("b_dat")
            d_r0 = sem("b_r0")
            d_c = sem("b_dvec")
            q_t0 = sem("b_t0")
            a_t0 = sem("b_at0")
            p_am = sem("b_am")
            q_x = sem("b_x")
            a_x = sem("b_ax")
            q_y = sem("b_y")
            d_t = sem("b_t")
            q_r = sem("b_r")
            a_r = sem("b_ar")
            KTb = s2("KTb", [P, 4, P])
            kbTb = s2("kbTb", [P, 4, P])

            with nc.Block() as block:
                def grp(t, g):
                    return t[:, 4 * g:4 * g + 4, :]

                def col(t, g):
                    return last_col(t[:, 4 * g:4 * g + 4], P)

                def kv(g, c):
                    return kvqg[:, 4 * g:4 * g + 4, c, :]

                @block.vector
                def _(dve):
                    for g in range(CHUNKS):
                        dve.tensor_tensor(kv(g, 0), kv(g, 0), col(rn, g), ALU.mult).then_inc(d_kn, 1)
                        dve.wait_ge(d_kn, g + 1)
                        dve.tensor_tensor(grp(kb, g), kv(g, 0), col(beta, g), ALU.mult).then_inc(d_kb, 1)
                        dve.tensor_tensor(kv(g, 1), kv(g, 1), col(beta, g), ALU.mult).then_inc(d_kb, 1)
                    for g in range(CHUNKS):
                        dve.wait_ge(q_tr, 5 * g + 3)
                        dve.tensor_copy(grp(QT, g), quad(bank[2][:, :])).then_inc(d_ev, 1)
                        dve.wait_ge(q_tr, 5 * g + 5)
                        dve.tensor_copy(grp(gateT, g), quad(bank[4][:, :])).then_inc(d_ev, 1)
                        dve.wait_ge(q_at, g + 1)
                        dve.wait_ge(p_dt, g + 1)
                        dve.tensor_tensor(grp(AT, g), quad(bank[6][:, :]), grp(DT, g), ALU.mult).then_inc(d_at, 1)
                        dve.wait_ge(d_at, g + 1)
                        if g:
                            dve.wait_ge(d_r0, g)
                        dve.tensor_tensor(t_a[:, :, :], grp(AT, g), mid_col(C[:, PAIRS, :], 4), ALU.mult).then_inc(d_c, 1)
                        dve.wait_ge(d_c, g + 1)
                        dve.tensor_tensor(grp(RI, g), mid_col(ident, 4), t_a[:, :, :], ALU.subtract).then_inc(d_r0, 1)
                    with dve.Fori(1, LEVELS) as lv:
                        for g in range(CHUNKS):
                            dve.wait_ge(q_y, lv * 4 + (g + 1 - 4))
                            dve.tensor_tensor(grp(TI, g), grp(TI, g), quad(bank[4 + g][:, :]), ALU.subtract).then_inc(d_t, 1)

                @block.gpsimd
                def _(pool):
                    for g in range(CHUNKS):
                        pool.tensor_tensor(grp(rla, g), mid_col(C[:, TRI_INC, :], 4), col(la, g), ALU.mult).then_inc(p_el, 1)
                        pool.tensor_tensor(grp(gQ, g), kv(g, 2), last_col(dec[:, 0, 4 * g:4 * g + 4], P), ALU.mult).then_inc(p_el, 1)
                        pool.wait_ge(d_kn, g + 1)
                        pool.tensor_tensor(grp(EK, g), kv(g, 0), last_col(dec[:, 1, 4 * g:4 * g + 4], P), ALU.mult).then_inc(p_el, 1)
                        pool.wait_ge(d_kb, 2 * g + 1)
                        pool.tensor_tensor(grp(bgK, g), grp(kb, g), last_col(dec[:, 0, 4 * g:4 * g + 4], P), ALU.mult).then_inc(p_el, 1)
                        pool.wait_ge(a_lt, g + 1)
                        pool.tensor_tensor(grp(DT, g), grp(DT, g), mid_col(C[:, TRI_INC, :], 4), ALU.mult).then_inc(p_dt, 1)
                    pool.wait_ge(q_lt, CHUNKS)
                    for lv in range(1, LEVELS):
                        for g in range(CHUNKS):
                            pool.wait_ge(d_at, g + 1)
                            pool.wait_ge(q_x, lv * 4 + (g + 1 - 4))
                            pool.tensor_tensor(grp(AM, g), grp(AT, g),
                                               mid_col(C[:, PAIRS + lv, :], 4),
                                               ALU.mult).then_inc(p_am, 1)

                @block.tensor
                def _(pe):
                    pe.sem_inc(q_x, 4)
                    for g in range(CHUNKS):
                        pe.wait_ge(p_el, 4 * g + 1)
                        if g:
                            pe.wait_ge(a_lt, g)
                        pe.matmul(bank[5][:, :], C[:, LOW_STRICT, :], grp(rla, g).rearrange("p a n -> p (a n)"),
                                  start=True, stop=True).then_inc(q_lt, 1)
                        pe.wait_ge(d_kb, 2 * g + 2)
                        pe.wait_ge(p_el, 4 * g + 2)
                        for i, src in enumerate((kv(g, 0), grp(kb, g), kv(g, 2), grp(gQ, g), kv(g, 3))):
                            if g:
                                if i in (2, 4):
                                    pe.wait_ge(d_ev, 2 * g - (1 if i == 2 else 0))
                                else:
                                    pe.wait_ge(a_ev, 3 * (g - 1) + {0: 1, 1: 2, 3: 3}[i])
                            for b in range(SEQS):
                                last = pe.transpose(bank[i][:, b * P:(b + 1) * P], src[:, b, :], ident)
                            last.then_inc(q_tr, 1)
                        pe.wait_ge(a_ev, 3 * g + 2)
                        if g:
                            pe.wait_ge(d_at, g)
                        for b in range(SEQS):
                            last = pe.matmul(bank[6][:, b * P:(b + 1) * P], KTb[:, b, :], kbTb[:, b, :], start=True, stop=True)
                        last.then_inc(q_at, 1)
                    for g in range(CHUNKS):
                        pe.wait_ge(d_r0, g + 1)
                        if g:
                            pe.wait_ge(a_t0, g)
                        for b in range(SEQS):
                            last = pe.transpose(bank[7][:, b * P:(b + 1) * P], RI[:, 4 * g + b, :], ident)
                        last.then_inc(q_t0, 1)
                    pe.wait_ge(a_t0, CHUNKS)
                    pe.wait_ge(a_ev, 3 * CHUNKS)
                    pe.wait_ge(d_ev, 2 * CHUNKS)
                    with pe.Fori(1, LEVELS) as lv:
                        for g in range(CHUNKS):
                            pe.wait_ge(a_r, lv * 4 + (g + 1 - 4))
                            pe.wait_ge(p_am, lv * 4 + (g + 1 - 4))
                            for b in range(SEQS):
                                last = pe.matmul(bank[g][:, b * P:(b + 1) * P], AM[:, 4 * g + b, :], TI[:, 4 * g + b, :],
                                                 start=True, stop=True)
                            last.then_inc(q_x, 1)
                        for g in range(CHUNKS):
                            pe.wait_ge(a_x, lv * 4 + (g + 1 - 4))
                            for b in range(SEQS):
                                last = pe.matmul(bank[4 + g][:, b * P:(b + 1) * P], RI[:, 4 * g + b, :], XL[:, 4 * g + b, :],
                                                 start=True, stop=True)
                            last.then_inc(q_y, 1)
                        for g in range(CHUNKS):
                            pe.wait_ge(d_t, lv * 4 + (g + 1 - 4))
                            for b in range(SEQS):
                                last = pe.transpose(bank[g][:, b * P:(b + 1) * P], TI[:, 4 * g + b, :], ident)
                            last.then_inc(q_r, 1)

                @block.scalar
                def _(act):
                    act.sem_inc(a_r, 4)
                    for g in range(CHUNKS):
                        act.wait_ge(q_lt, g + 1)
                        act.activation(grp(DT, g), quad(bank[5][:, :]), ACT.Exp).then_inc(a_lt, 1)
                        act.wait_ge(q_tr, 5 * g + 1)
                        if g:
                            act.wait_ge(q_at, g)
                        act.activation(KTb[:, :, :], quad(bank[0][:, :]), ACT.Copy).then_inc(a_ev, 1)
                        act.wait_ge(q_tr, 5 * g + 2)
                        act.activation(kbTb[:, :, :], quad(bank[1][:, :]), ACT.Copy).then_inc(a_ev, 1)
                        act.wait_ge(q_tr, 5 * g + 4)
                        act.activation(grp(gQT, g), quad(bank[3][:, :]), ACT.Copy).then_inc(a_ev, 1)
                    for g in range(CHUNKS):
                        act.wait_ge(q_t0, g + 1)
                        act.wait_ge(p_el, 4 * CHUNKS)
                        act.activation(grp(TI, g), quad(bank[7][:, :]), ACT.Copy).then_inc(a_t0, 1)
                    with act.Fori(1, LEVELS) as lv:
                        for g in range(CHUNKS):
                            act.wait_ge(q_x, lv * 4 + (g + 1))
                            act.activation(grp(XL, g), quad(bank[g][:, :]), ACT.Copy).then_inc(a_x, 1)
                        for g in range(CHUNKS):
                            act.wait_ge(q_r, lv * 4 + (g + 1 - 4))
                            act.activation(grp(RI, g), quad(bank[g][:, :]), ACT.Copy).then_inc(a_r, 1)

            nZT, U, UT, M = AT, AM, XL, TI
            S = s2("S", [P, 4, P])
            ST = s2("ST", [P, 4, P])
            Sg = s2("Sg", [P, 4, P])
            STg = s2("STg", [P, 4, P])
            c_zt = sem("c_zt")
            c_nzt = sem("c_nzt")
            c_u = sem("c_u")
            c_ue = sem("c_ue")
            c_ut = sem("c_ut")
            c_ute = sem("c_ute")
            c_m = sem("c_m")
            c_me = sem("c_me")
            c_o = sem("c_o")
            c_oe = sem("c_oe")
            c_out = sem("c_out")
            c_x = sem("c_x")
            c_s = sem("c_s")
            c_st = sem("c_st")
            c_se = sem("c_se")
            c_g = sem("c_g")
            with nc.Block() as block:
                GO = bgK

                @block.tensor
                def _(pe):
                    def mm4(dst, pairs):
                        for b in range(SEQS):
                            for i, (l, r) in enumerate(pairs):
                                last = pe.matmul(dst[:, b * P:(b + 1) * P], l(b), r(b), start=(i == 0), stop=(i == len(pairs) - 1))
                        return last

                    def at(t, g):
                        return lambda b: t[:, 4 * g + b, :]

                    def kvb(g, c):
                        return lambda b: kvqg[:, 4 * g + b, c, :]

                    def zt(g):
                        if g:
                            pe.wait_ge(c_nzt, g)
                        mm4(bank[0], [(at(bgK, g), at(RI, g))]).then_inc(c_zt, 1)

                    def project(g):
                        pe.wait_ge(c_oe, g + 1)
                        if g:
                            pe.wait_ge(c_x, g)
                        mm4(bank[5], [(at(GO, g), lambda b: wo[:, :])]).then_inc(c_out, 1)

                    pe.wait_ge(c_g, 2)
                    zt(0)
                    for g in range(CHUNKS):
                        pe.wait_ge(c_nzt, g + 1)
                        if g:
                            pe.wait_ge(c_se, 2 * g)
                        mm4(bank[1], [(at(RI, g), kvb(g, 1)), (at(nZT, g), lambda b: ST[:, b, :])]).then_inc(c_u, 1)
                        mm4(bank[2], [(kvb(g, 1), at(RI, g)), (lambda b: ST[:, b, :], at(nZT, g))]).then_inc(c_ut, 1)
                        if g:
                            project(g - 1)
                        if g < CHUNKS - 1:
                            zt(g + 1)
                            pe.wait_ge(c_ue, g + 1)
                            mm4(bank[6], [(at(EK, g), at(U, g))]).then_inc(c_st, 1)
                            mm4(bank[7], [(at(U, g), at(EK, g))]).then_inc(c_s, 1)
                        pe.wait_ge(c_ute, g + 1)
                        if g:
                            pe.wait_ge(c_me, g)
                        mm4(bank[3], [(at(UT, g), at(QT, g))]).then_inc(c_m, 1)
                        pe.wait_ge(c_me, g + 1)
                        mm4(bank[4], [(kvb(g, 0), at(M, g)), (lambda b: S[:, b, :], at(gQT, g))]).then_inc(c_o, 1)
                    project(CHUNKS - 1)

                @block.scalar
                def _(act):
                    def nzt(g):
                        act.wait_ge(c_zt, g + 1)
                        act.activation(grp(nZT, g), quad(bank[0][:, :]), ACT.Copy, scale=-1.0).then_inc(c_nzt, 1)

                    nzt(0)
                    for g in range(CHUNKS):
                        act.wait_ge(c_ut, g + 1)
                        act.activation(grp(UT, g), quad(bank[2][:, :]), ACT.Copy).then_inc(c_ute, 1)
                        if g < CHUNKS - 1:
                            nzt(g + 1)

                @block.gpsimd
                def _(pool):
                    pool.memset(S[:, :, :], 0.0).then_inc(c_g, 1)
                    pool.memset(ST[:, :, :], 0.0).then_inc(c_g, 1)
                    pool.wait_ge(c_g, 2)
                    for g in range(CHUNKS - 1):
                        if g:
                            pool.wait_ge(c_se, 2 * g)
                        for src, dst in ((ST, STg), (S, Sg)):
                            pool.tensor_tensor(dst[:, :, :], src[:, :, :], last_col(dec[:, 2, 4 * g:4 * g + 4], P),
                                               ALU.mult).then_inc(c_g, 1)

                @block.vector
                def _(dve):
                    for g in range(CHUNKS):
                        dve.wait_ge(c_u, g + 1)
                        dve.tensor_copy(grp(U, g), quad(bank[1][:, :])).then_inc(c_ue, 1)
                        if g:
                            dve.wait_ge(c_out, g)
                            dve.tensor_tensor(grp(X, g - 1), grp(X, g - 1), quad(bank[5][:, :]), ALU.add).then_inc(c_x, 1)
                        dve.wait_ge(c_m, g + 1)
                        dve.tensor_tensor(grp(M, g), quad(bank[3][:, :]), grp(DT, g), ALU.mult).then_inc(c_me, 1)
                        if g < CHUNKS - 1:
                            dve.wait_ge(c_g, 2 * g + 4)
                            dve.wait_ge(c_st, g + 1)
                            dve.wait_ge(c_ut, g + 1)
                            dve.tensor_tensor(ST[:, :, :], STg[:, :, :], quad(bank[6][:, :]), ALU.add).then_inc(c_se, 1)
                        dve.wait_ge(c_o, g + 1)
                        if g < CHUNKS - 1:
                            dve.wait_ge(c_s, g + 1)
                            dve.tensor_tensor(S[:, :, :], Sg[:, :, :], quad(bank[7][:, :]), ALU.add).then_inc(c_se, 1)
                        dve.tensor_tensor(grp(GO, g), quad(bank[4][:, :]), grp(gateT, g), ALU.mult).then_inc(c_oe, 1)
                    g = CHUNKS - 1
                    dve.wait_ge(c_out, CHUNKS)
                    dve.tensor_tensor(grp(X, g), grp(X, g), quad(bank[5][:, :]), ALU.add).then_inc(c_x, 1)
        ab.close()

        if STAGE >= 2:
            route(nc, top, chain, bank, a, 0, X, C, V, wr0, br0, mv, st6, var, rstd, tmp, plan_i, expert_i, slots[0], s_fill, s_const)
            experts(nc, top, chain, bank, 0, X, C, (w1a, w2a, b1a, b2a, None, None), expert_i, slots[0], byrow[0], s_ffn0, 64)
        ffn.close()

        if STAGE >= 3:
            with ExitStack() as ctx1:
                s7 = alloc(ctx1)
                u1 = s7("u1", [P, E * F])
                ug = s7("ug", [P, E * F])
                u2 = s7("u2", [P, E * F])
                c1 = s7("c1", [P, E * F])
                cg = s7("cg", [P, E * F])
                c2 = s7("c2", [P, E * D])
                attention(nc, top, chain, bank, a, X, C, bout_b, mv, st6, var, rstd, tmp,
                          [(u1, "w1b"), (ug, "wgb"), (u2, "w2b"), (c1, "b1b"), (cg, "bgb"), (c2, "b2b")], s_ffn1)
                if STAGE >= 4:
                    route(nc, top, chain, bank, a, 1, X, C, V, wr1, None, mv, st6, var, rstd, tmp, plan_i, expert_i, slots[1], s_fill, s_const)
                    experts(nc, top, chain, bank, 1, X, C, (u1, u2, c1, c2, ug, cg), expert_i, slots[1], byrow[1], s_ffn1, 96)

        with ExitStack() as ctx:
            s_out = sem("s_out")
            block = ctx.enter_context(nc.Block())

            @block.sync
            def _(sp):
                sp.dma_start(out, X[:, :, :]).then_inc(s_out, 16)
                sp.wait_ge(s_out, 16)
                sp.wait_ge(s_fill, 16 * sum(-(-slot_tiles(n) // 4) for n in (1, 2)))
                sp.wait_ge(s_ffn0, 64)


def route(nc, top, chain, bank, a, layer, X, C, V, wr, br, mv, st6, var, rstd, tmp, plan_i, expert_i, slots, s_fill, s_const):
    K = layer + 1
    NT = slot_tiles(K)
    ident = C[:, IDENT, :]

    def sem(name):
        return top.enter_context(nc.semaphore(f"r{layer}_{name}"))

    with ExitStack() as ctx:
        def sb(name, shape, dt=F32):
            return ctx.enter_context(nc.sbuf_tensor(f"r{layer}_{name}", shape, dt))

        rows = [sb(f"rows{c}", [P, TILES, ROW]) for c in range(K)]
        xnT = [sb(f"xnT{i}", [P, 512]) for i in range(2)]
        lg = sb("lg", [P, TILES, E])
        wk = sb("wk", [P, TILES, E])
        ex = sb("ex", [P, TILES, E])
        mx = sb("mx", [P, TILES])
        sm = sb("sm", [P, TILES])
        one = [sb(f"one{c}", [P, TILES, E]) for c in range(K)]
        both = sb("both", [P, TILES, E]) if K == 2 else one[0]
        tot = sb("tot", [P, E, TILES])
        run = sb("run", [P, E, TILES])
        cnt = sb("cnt", [P, E, TILES])
        ntl = sb("ntl", [P, E])
        end = sb("end", [P, E])
        beg = sb("beg", [P, E])
        base = sb("base", [P, TILES, E])
        pos = sb("pos", [P, TILES])
        ew = sb("ew", [1, NT, E])
        ef = sb("ef", [1, NT])
        s_row, s_tr, s_xT, s_lg, s_ex, s_exd, s_one, s_rank, s_plan, s_sc, s_dup = (
            sem(n) for n in ("row", "tr", "xT", "lg", "ex", "exd", "one", "rank", "plan", "sc", "dup"))
        block = ctx.enter_context(nc.Block())
        LG, WITHIN, TOTAL = bank[4][:, 0:P], bank[5][:, 0:P], bank[6][:, 0:P]

        def te(ap):
            return ap.rearrange("p (a n) -> p a n", n=E)

        @block.vector
        def _(dve):
            layernorm_stats(dve, chain, X, st6, mv, var, rstd, tmp)
            for j in range(TILES):
                dve.tensor_scalar(rows[0][:, j, 0:D], X[:, j, :], mv[:, j, 0:1], rstd[:, j:j + 1],
                                  ALU.subtract, ALU.mult).then_inc(s_row, 1)
            dve.wait_ge(s_lg, 1)
            if br is not None:
                chain.run(dve, dve.tensor_tensor(lg[:, :, :], te(LG), mid_col(br[:, :], TILES), ALU.add))
            else:
                chain.run(dve, dve.tensor_copy(lg[:, :, :], te(LG)))
            chain.run(dve, dve.tensor_reduce(mx[:, :], lg[:, :, :], AX.X, ALU.max))
            dve.tensor_tensor(wk[:, :, :], lg[:, :, :], last_col(mx[:, :], E), ALU.subtract).then_inc(s_ex, 1)
            dve.wait_ge(s_exd, 1)
            chain.run(dve, dve.tensor_reduce(sm[:, :], ex[:, :, :], AX.X, ALU.add))
            chain.run(dve, dve.reciprocal(sm[:, :], sm[:, :]))
            chain.run(dve, dve.tensor_tensor(ex[:, :, :], ex[:, :, :], last_col(sm[:, :], E), ALU.mult))
            for c in range(K):
                chain.run(dve, dve.tensor_reduce(mx[:, :], ex[:, :, :], AX.X, ALU.max))
                chain.run(dve, dve.tensor_copy(rows[c][:, :, GATE:GATE + 1], mx[:, :].unsqueeze(2)))
                chain.run(dve, dve.tensor_tensor(wk[:, :, :], ex[:, :, :], last_col(mx[:, :], E), ALU.is_ge))
                chain.run(dve, dve.tensor_tensor(wk[:, :, :], wk[:, :, :], mid_col(V[:, V_EM8:V_EM8 + E], TILES), ALU.mult))
                chain.run(dve, dve.tensor_reduce(sm[:, :], wk[:, :, :], AX.X, ALU.min))
                chain.run(dve, dve.tensor_tensor(one[c][:, :, :], mid_col(V[:, V_EM8:V_EM8 + E], TILES), last_col(sm[:, :], E),
                                            ALU.is_equal))
                if c < K - 1:
                    chain.run(dve, dve.scalar_tensor_tensor(ex[:, :, :].rearrange("p a n -> p (a n)"),
                                                       one[c][:, :, :].rearrange("p a n -> p (a n)"), -2.0,
                                                       ex[:, :, :].rearrange("p a n -> p (a n)"), ALU.mult, ALU.add))
            if K == 2:
                chain.run(dve, dve.tensor_tensor(both[:, :, :], one[0][:, :, :], one[1][:, :, :], ALU.add))
            dve.sem_inc(s_one, 1)
            dve.wait_ge(s_rank, 1)
            chain.run(dve, dve.tensor_copy(tot[:, :, :], te(TOTAL).rearrange("p a n -> p n a")))
            chain.run(dve, dve.tensor_tensor_scan(run[:, :, :].rearrange("p a n -> p (a n)"), V[:, V_SCAN:V_SCAN + P],
                                             tot[:, :, :].rearrange("p a n -> p (a n)"), 0.0, ALU.mult, ALU.add))
            chain.run(dve, dve.tensor_tensor(cnt[:, :, :], run[:, :, TILES - 1:TILES].broadcast_to([P, E, TILES]),
                                        mid_col(V[:, V_KTH:V_KTH + TILES], E), ALU.is_gt))
            chain.run(dve, dve.tensor_reduce(ntl[:, :], cnt[:, :, :], AX.X, ALU.add))
            chain.run(dve, dve.tensor_tensor_scan(end[:, :], C[:, ONES, 0:E], ntl[:, :], 0.0, ALU.mult, ALU.add))
            chain.run(dve, dve.tensor_tensor(beg[:, :], end[:, :], ntl[:, :], ALU.subtract))
            chain.run(dve, dve.tensor_scalar(beg[:, :], beg[:, :], float(P), None, ALU.mult))
            chain.run(dve, dve.tensor_tensor(run[:, :, :], run[:, :, :], tot[:, :, :], ALU.subtract))
            chain.run(dve, dve.tensor_tensor(run[:, :, :], run[:, :, :], last_col(beg[:, :], TILES), ALU.add))
            chain.run(dve, dve.tensor_tensor(base[:, :, :], te(WITHIN), run[:, :, :].rearrange("p a n -> p n a"), ALU.add))
            for c in range(K):
                chain.run(dve, dve.tensor_tensor(wk[:, :, :], base[:, :, :], one[c][:, :, :], ALU.mult))
                chain.run(dve, dve.tensor_reduce(pos[:, :], wk[:, :, :], AX.X, ALU.add))
                chain.run(dve, dve.tensor_copy(plan_i[:, c * TILES:(c + 1) * TILES], pos[:, :]))
                chain.run(dve, dve.tensor_scalar(rows[c][:, :, DEST:DEST + 1], V[:, V_ROW:V_ROW + TILES].unsqueeze(2),
                                            float(c * TILES * P), None, ALU.add))
                dve.sem_inc(s_plan, 1)
            chain.run(dve, dve.tensor_tensor(ew[:, :, 0:E - 1], last_col(V[0:1, V_TILE:V_TILE + NT], E - 1),
                                        mid_col(end[0:1, 0:E - 1], NT), ALU.is_ge))
            chain.run(dve, dve.tensor_reduce(ef[:, :], ew[:, :, 0:E - 1], AX.X, ALU.add))
            chain.run(dve, dve.tensor_copy(expert_i[:, 0:NT], ef[:, :]))

        @block.tensor
        def _(pe):
            for g in range(CHUNKS):
                pe.wait_ge(s_row, 4 * g + 4)
                if g >= 2:
                    pe.wait_ge(s_xT, g - 1)
                for k in range(4):
                    last = pe.transpose(bank[g % 2][:, k * P:(k + 1) * P], rows[0][:, 4 * g + k, 0:D], ident)
                last.then_inc(s_tr, 1)
                pe.wait_ge(s_xT, g + 1)
                for k in range(4):
                    n = 4 * g + k
                    last = pe.matmul(LG[:, n * E:(n + 1) * E], xnT[g % 2][:, k * P:(k + 1) * P], wr[:, :], start=True, stop=True)
                last.then_inc(s_tr, 1)
            pe.wait_ge(s_tr, 2 * CHUNKS)
            pe.sem_inc(s_lg, 1)
            pe.wait_ge(s_one, 1)
            pe.matmul(WITHIN, C[:, UP_STRICT, :], both[:, :, :].rearrange("p a n -> p (a n)"), start=True, stop=True)
            pe.matmul(TOTAL, C[:, ONES, :], both[:, :, :].rearrange("p a n -> p (a n)"), start=True, stop=True).then_inc(s_rank, 1)

        @block.scalar
        def _(act):
            for g in range(CHUNKS):
                act.wait_ge(s_tr, 2 * g + 1)
                act.activation(xnT[g % 2][:, :], bank[g % 2][:, :], ACT.Copy).then_inc(s_xT, 1)
            act.wait_ge(s_ex, 1)
            act.activation(ex[:, :, :], wk[:, :, :], ACT.Exp).then_inc(s_exd, 1)

        @block.gpsimd
        def _(pool):
            if K == 2:
                pool.wait_ge(s_row, TILES)
                pool.tensor_copy(rows[1][:, :, 0:D], rows[0][:, :, 0:D]).then_inc(s_dup, 1)
                pool.wait_ge(s_dup, 1)
            pool.wait_ge(s_fill, 16 * sum(-(-slot_tiles(n) // 4) for n in (1, 2)))
            for c in range(K):
                pool.wait_ge(s_plan, c + 1)
                for j in range(TILES):
                    n = c * TILES + j
                    pool.indirect_dma_start(out=slots, out_offset=bass.IndirectOffsetOnAxis(
                        ap=plan_i[:, n:n + 1].bitcast(U32), axis=0), in_=rows[c][:, j, :], in_offset=None).then_inc(s_sc, 16)
            pool.wait_ge(s_sc, 16 * K * TILES)


def experts(nc, top, chain, bank, layer, X, C, weights, expert_i, slots, byrow, s_w, w_count):
    w1, w2, b1, b2, wg, bg = weights
    K = layer + 1
    NT = slot_tiles(K)
    gated = wg is not None
    ident = C[:, IDENT, :]

    def sem(name):
        return top.enter_context(nc.semaphore(f"e{layer}_{name}"))

    with ExitStack() as ctx:
        def sb(name, shape, dt=F32):
            return ctx.enter_context(nc.sbuf_tensor(f"e{layer}_{name}", shape, dt))

        xs = [sb(f"xs{i}", [P, ROW]) for i in range(4)]
        xT = [sb(f"xT{i}", [P, P]) for i in range(2)]
        h = [sb(f"h{i}", [P, F]) for i in range(2)]
        hg = [sb(f"hg{i}", [P, F]) for i in range(2)] if gated else None
        hT = [sb(f"hT{i}", [P, F]) for i in range(2)]
        y = [sb(f"y{i}", [P, D]) for i in range(4)]
        dst = sb("dst", [P, NT], I32)
        gate = sb("gate", [P, NT])
        back = sb("back", [P, K * TILES, D])
        s_xs = [sem(f"xs{i}") for i in range(4)]
        s_sc = [sem(f"sc{i}") for i in range(4)]
        s_xt, s_xT, s_h, s_hs, s_t, s_hT, s_y, s_yb, s_yg, s_take, s_bk = (
            sem(n) for n in ("xt", "xT", "h", "hs", "t", "hT", "y", "yb", "yg", "take", "bk"))
        if gated:
            s_g, s_gs, s_ge, s_p = (sem(n) for n in ("g", "gs", "ge", "p"))
        block = ctx.enter_context(nc.Block())
        BX, BH, BG, BT, BY = bank[0], (bank[1], bank[7]), bank[2], bank[3:5], bank[5:7]
        Q = NT // 4

        def tiles(eng, body, weights=False):
            regs = [eng.alloc_register(f"expert{layer}_{j}") for j in range(6)] if weights else []

            def fetch(i, lo, n):
                if weights:
                    at = expert_i[0:1, bass.ds(i + lo, n - lo)] if not isinstance(i, int) else expert_i[0:1, i + lo:i + n]
                    eng.load(regs[lo + 1:n + 1], at)
                return [None] * (lo + 1) + [nc.snap(r).with_bounds(min_val=0, max_val=E - 1) for r in regs[lo + 1:n + 1]] + [None] * 8

            e = fetch(0, 0, 5)
            if weights:
                weights(e[1])
            for i in range(4):
                body(i, i, e[i:])
            with eng.Fori(1, Q) as q:
                e = fetch(q * 4, -1, 5)
                for k in range(4):
                    body(q * 4 + k, k, e[k:])
            e = fetch(4 * Q, -1, NT - 4 * Q)
            for i in range(4 * Q, NT):
                body(i, i % 4, e[i % 4:])
            return e[NT % 4]

        def inside(i):
            return not isinstance(i, int) or 0 <= i < NT

        def later(i):
            return not isinstance(i, int) or i >= 4

        @block.sync
        def _(sp):
            def load(i, k, _):
                if later(i):
                    sp.wait_ge(s_xt, i - 3)
                    sp.wait_ge(s_take, i - 3)
                src = slots[bass.ds(i * P, P), :] if not isinstance(i, int) else slots[i * P:(i + 1) * P, :]
                sp.dma_start(xs[k][:, :], src).then_inc(s_xs[k], 16)
            tiles(sp, load)
            for k in range(4):
                sp.wait_ge(s_sc[k], 16 * len(range(k, NT, 4)))
            sp.dma_start(back[:, :, :], byrow.rearrange("(c p j) d -> p c j d", c=K, p=P)).then_inc(s_bk, 16)

        @block.tensor
        def _(pe):
            def turn(i, k):
                if inside(i):
                    pe.wait_ge(s_xs[k], (i - k) * 4 + 16)
                    pe.wait_ge(s_xT, i + 1)
                    pe.transpose(BX[:, 0:P], xs[k][:, 0:D], ident).then_inc(s_xt, 1)

            def hidden_gate(i, k, e):
                if gated and inside(i):
                    pe.wait_ge(s_xT, i + 2)
                    pe.wait_ge(s_gs, i + 1)
                    pe.matmul(BG[:, :], xT[k % 2][:, :], wg[:, bass.ds(e * F, F)], start=True, stop=True).then_inc(s_g, 1)

            def hidden(i, k, e):
                if inside(i):
                    pe.wait_ge(s_xT, i + 2)
                    pe.wait_ge(s_hs, i + 1)
                    pe.matmul(BH[k % 2][:, :], xT[k % 2][:, :], w1[:, bass.ds(e * F, F)], start=True, stop=True).then_inc(s_h, 1)

            def turn_hidden(i, k):
                src = hg if gated else h
                if gated:
                    pe.wait_ge(s_p, i + 1)
                else:
                    pe.wait_ge(s_hs, i + 3)
                pe.wait_ge(s_hT, i + 1)
                for t in range(FT):
                    last = pe.transpose(BT[k % 2][:, t * P:(t + 1) * P], src[k % 2][:, t * P:(t + 1) * P], ident)
                last.then_inc(s_t, 1)

            def result(i, k, e):
                if inside(i):
                    pe.wait_ge(s_hT, i + 3)
                    pe.wait_ge(s_yb, i + 1)
                    for t in range(FT):
                        last = pe.matmul(BY[k % 2][:, 0:D], hT[k % 2][:, t * P:(t + 1) * P], w2[:, bass.ds(e * F + t * D, D)],
                                         start=(t == 0), stop=(t == FT - 1))
                    last.then_inc(s_y, 1)

            def body(i, k, e):
                if gated:
                    hidden_gate(i + 1, (k + 1) % 4, e[2])
                    turn(i + 2, (k + 2) % 4)
                    result(i - 1, (k - 1) % 4, e[0])
                    turn_hidden(i, k)
                    hidden(i + 1, (k + 1) % 4, e[2])
                else:
                    hidden(i + 1, (k + 1) % 4, e[2])
                    turn(i + 2, (k + 2) % 4)
                    result(i - 1, (k - 1) % 4, e[0])
                    turn_hidden(i, k)

            def first(e):
                turn(0, 0)
                hidden_gate(0, 0, e)
                hidden(0, 0, e)
                turn(1, 1)

            pe.wait_ge(s_w, w_count)
            e = tiles(pe, body, first)
            result(NT - 1, (NT - 1) % 4, e)

        @block.scalar
        def _(act):
            def turned(i, k):
                if inside(i):
                    act.wait_ge(s_xt, i + 1)
                    act.activation(xT[k % 2][:, :], BX[:, 0:P], ACT.Copy).then_inc(s_xT, 1)

            def gelu(i, k):
                if gated and inside(i):
                    act.wait_ge(s_gs, i + 2)
                    act.activation(hg[k % 2][:, :], hg[k % 2][:, :], ACT.Gelu).then_inc(s_ge, 1)

            def body(i, k, _):
                turned(i + 2, (k + 2) % 4)
                gelu(i + 1, (k + 1) % 4)
                act.wait_ge(s_t, i + 1)
                act.activation(hT[k % 2][:, :], BT[k % 2][:, :], ACT.Copy if gated else ACT.Relu).then_inc(s_hT, 1)

            act.sem_inc(s_xT, 1)
            act.sem_inc(s_hT, 2)
            turned(0, 0)
            gelu(0, 0)
            turned(1, 1)
            tiles(act, body)

        @block.vector
        def _(dve):
            def bias_gate(i, k, e):
                if gated and inside(i):
                    dve.wait_ge(s_g, i + 1)
                    dve.tensor_tensor(hg[k % 2][:, :], BG[:, :], bg[:, bass.ds(e * F, F)], ALU.add).then_inc(s_gs, 1)

            def bias(i, k, e):
                if inside(i):
                    dve.wait_ge(s_h, i + 1)
                    dve.tensor_tensor(h[k % 2][:, :], BH[k % 2][:, :], b1[:, bass.ds(e * F, F)], ALU.add).then_inc(s_hs, 1)

            def result(i, k, e):
                if inside(i):
                    if later(i):
                        dve.wait_ge(s_sc[k], (i - k) * 4)
                    dve.wait_ge(s_y, i + 1)
                    dve.tensor_tensor(y[k][:, :], BY[k % 2][:, 0:D], b2[:, bass.ds(e * D, D)], ALU.add).then_inc(s_yb, 1)
                    dve.wait_ge(s_yb, i + 3)
                    dve.wait_ge(s_take, i + 1)
                    g = gate[:, bass.ds(i, 1)] if not isinstance(i, int) else gate[:, i:i + 1]
                    dve.tensor_scalar(y[k][:, :], y[k][:, :], g, None, ALU.mult).then_inc(s_yg, 1)

            def body(i, k, e):
                if gated:
                    dve.wait_ge(s_ge, i + 1)
                    dve.wait_ge(s_hs, i + 3)
                    dve.tensor_tensor(hg[k % 2][:, :], hg[k % 2][:, :], h[k % 2][:, :], ALU.mult).then_inc(s_p, 1)
                    bias_gate(i + 1, (k + 1) % 4, e[2])
                    result(i - 1, (k - 1) % 4, e[0])
                    bias(i + 1, (k + 1) % 4, e[2])
                else:
                    bias(i + 1, (k + 1) % 4, e[2])
                    result(i - 1, (k - 1) % 4, e[0])

            def first(e):
                bias_gate(0, 0, e)
                bias(0, 0, e)

            dve.sem_inc(s_hs, 2)
            if gated:
                dve.sem_inc(s_gs, 1)
            dve.sem_inc(s_yb, 2)
            e = tiles(dve, body, first)
            result(NT - 1, (NT - 1) % 4, e)
            dve.wait_ge(s_bk, 16)
            for c in range(K):
                chain.run(dve, dve.tensor_tensor(X[:, :, :], X[:, :, :], back[:, c * TILES:(c + 1) * TILES, :], ALU.add))

        @block.gpsimd
        def _(pool):
            def take(i):
                pool.wait_ge(s_xs[i % 4], 16 * (i // 4) + 16)
                pool.tensor_copy(dst[:, i:i + 1], xs[i % 4][:, DEST:DEST + 1])
                pool.tensor_copy(gate[:, i:i + 1], xs[i % 4][:, GATE:GATE + 1]).then_inc(s_take, 1)

            take(0)
            take(1)
            for i in range(NT):
                k = i % 4
                if i + 2 < NT:
                    take(i + 2)
                pool.wait_ge(s_take, i + 1)
                pool.wait_ge(s_yg, i + 1)
                pool.indirect_dma_start(out=byrow, out_offset=bass.IndirectOffsetOnAxis(
                    ap=dst[:, i:i + 1].bitcast(U32), axis=0), in_=y[k][:, :], in_offset=None,
                    bounds_check=K * TILES * P - 1, oob_is_err=False).then_inc(s_sc[k], 16)


def attention(nc, top, chain, bank, a, X, C, bout_b, mv, st6, var, rstd, tmp, ffn_loads, s_ffn1):
    ident = C[:, IDENT, :]

    def sem(name):
        return top.enter_context(nc.semaphore(f"t_{name}"))

    with ExitStack() as ctx:
        def sb(name, shape, dt=F32):
            return ctx.enter_context(nc.sbuf_tensor(f"t_{name}", shape, dt))

        Kq = sb("Kq", [P, HEADS, KEYS])
        VW = sb("VW", [P, HEADS, KT_N, D])
        xnT = sb("xnT", [P, TILES * P])
        s_w, s_kt, s_kte, s_vt, s_vte, s_kq, s_vw, s_vwe, s_mean, s_me2, s_bq, s_xn, s_tr, s_xT = (
            sem(n) for n in ("w", "kt", "kte", "vt", "vte", "kq", "vw", "vwe", "mean", "me2", "bq",
                             "xn", "tr", "xT"))
        with ExitStack() as ctx2:
            def sb2(name, shape, dt=F32):
                return ctx2.enter_context(nc.sbuf_tensor(f"t_{name}", shape, dt))
            cT = sb2("cT", [CTX, KEYS])
            wk = sb2("wk", [CTX, HEADS * P])
            wv = sb2("wv", [CTX, HEADS * P])
            wqT = sb2("wqT", [P, HEADS, P])
            wout = sb2("wout", [P, HEADS, P])
            KTh = [sb2(f"KTh{i}", [P, KEYS]) for i in range(2)]
            VTh = [sb2(f"VTh{i}", [P, KEYS]) for i in range(2)]
            ksum = sb2("ksum", [P, HEADS])
            xn = [sb2(f"xn{i}", [P, 4, D]) for i in range(2)]
            with nc.Block() as block:
                @block.sync
                def _(sp):
                    for t, name in ((cT, "ctxT"), (wk, "wk"), (wqT, "wqT"), (wv, "wv"), (wout, "wout")):
                        sp.dma_start(t[:], a[name]).then_inc(s_w, 16)
                    for t, name in ffn_loads:
                        src = a[name]
                        if len(src.shape) == 1:
                            src = src.partition_broadcast(P)
                        sp.dma_start(t[:, :], src).then_inc(s_ffn1, 16)

                @block.tensor
                def _(pe):
                    pe.wait_ge(s_w, 16 * 5)
                    for hd in range(HEADS):
                        if hd:
                            pe.wait_ge(s_kte, hd)
                        pe.matmul(bank[0][:, :], wk[:, hd * P:(hd + 1) * P], cT[:, :], start=True, stop=True).then_inc(s_kt, 1)
                        if hd:
                            pe.wait_ge(s_vte, hd)
                        pe.matmul(bank[1][:, :], wv[:, hd * P:(hd + 1) * P], cT[:, :], start=True, stop=True).then_inc(s_vt, 1)
                        if hd:
                            pe.wait_ge(s_bq, hd)
                        pe.wait_ge(s_kte, hd + 1)
                        pe.matmul(bank[2][:, :], wqT[:, hd, :], KTh[hd % 2][:, :], start=True, stop=True).then_inc(s_kq, 1)
                        if hd:
                            pe.wait_ge(s_vwe, hd)
                        pe.wait_ge(s_vte, hd + 1)
                        for t in range(KT_N):
                            last = pe.matmul(bank[3][:, t * P:(t + 1) * P], VTh[hd % 2][:, t * P:(t + 1) * P], wout[:, hd, :],
                                             start=True, stop=True)
                        last.then_inc(s_vw, 1)
                    for g in range(CHUNKS):
                        pe.wait_ge(s_xn, g + 1)
                        if g >= 2:
                            pe.wait_ge(s_xT, g - 1)
                        for k in range(4):
                            last = pe.transpose(bank[4 + g % 2][:, k * P:(k + 1) * P], xn[g % 2][:, k, :], ident)
                        last.then_inc(s_tr, 1)

                @block.scalar
                def _(act):
                    for hd in range(HEADS):
                        act.wait_ge(s_kt, hd + 1)
                        if hd >= 2:
                            act.wait_ge(s_kq, hd - 1)
                        act.activation(KTh[hd % 2][:, :], bank[0][:, :], ACT.Copy).then_inc(s_kte, 1)
                        act.wait_ge(s_vt, hd + 1)
                        if hd >= 2:
                            act.wait_ge(s_vw, hd - 1)
                        act.activation(VTh[hd % 2][:, :], bank[1][:, :], ACT.Copy).then_inc(s_vte, 1)
                        act.wait_ge(s_vw, hd + 1)
                        act.activation(VW[:, hd, :, :].rearrange("p a n -> p (a n)"), bank[3][:, :], ACT.Copy).then_inc(s_vwe, 1)
                    for g in range(CHUNKS):
                        act.wait_ge(s_tr, g + 1)
                        act.activation(xnT[:, g * 512:(g + 1) * 512], bank[4 + g % 2][:, :], ACT.Copy).then_inc(s_xT, 1)

                def norm4(dve, g):
                    for k in range(4):
                        j = 4 * g + k
                        last = dve.tensor_scalar(xn[g % 2][:, k, :], X[:, j, :], mv[:, j, 0:1], rstd[:, j:j + 1],
                                                 ALU.subtract, ALU.mult)
                    last.then_inc(s_xn, 1)

                @block.vector
                def _(dve):
                    layernorm_stats(dve, chain, X, st6, mv, var, rstd, tmp)
                    for g in range(2):
                        norm4(dve, g)
                    for hd in range(HEADS):
                        dve.wait_ge(s_kq, hd + 1)
                        dve.tensor_reduce(ksum[:, hd:hd + 1], bank[2][:, :], AX.X, ALU.add).then_inc(s_mean, 1)
                        dve.wait_ge(s_mean, hd + 1)
                        dve.tensor_scalar(ksum[:, hd:hd + 1], ksum[:, hd:hd + 1],
                                          SIM_SCALE * (1.0 - MATRIX_SCALE) / KEYS, None, ALU.mult).then_inc(s_me2, 1)
                        dve.wait_ge(s_me2, hd + 1)
                        dve.tensor_scalar(Kq[:, hd, :], bank[2][:, :], SIM_SCALE * MATRIX_SCALE, ksum[:, hd:hd + 1],
                                          ALU.mult, ALU.add).then_inc(s_bq, 1)
                    for g in range(2, 4):
                        dve.wait_ge(s_tr, g - 1)
                        norm4(dve, g)
                    dve.wait_ge(s_xn, CHUNKS)
                    chain.run(dve, dve.tensor_tensor(X[:, :, :], X[:, :, :], mid_col(bout_b[:, :], TILES), ALU.add))

        xq = [sb(f"xq{i}", [P, P]) for i in range(2)]
        Pr = [sb(f"Pr{i}", [P, KEYS]) for i in range(2)]
        PT = [sb(f"PT{i}", [P, KEYS]) for i in range(2)]
        nmx = sb("nmx", [P, 16])
        den = sb("den", [P, 16])
        rec = sb("rec", [P, 16])
        acc = [sb(f"acc{i}", [P, D]) for i in range(2)]
        s_q, s_s, s_m, s_e, s_t, s_pt, s_o, s_rc, s_acc = (
            sem(n) for n in ("q", "s", "m", "e", "t", "pt", "o", "rc", "acc"))
        UN = 2 * HEADS
        BS, BT, BO = bank[0:4], bank[4:6], bank[6:8]
        with nc.Block() as block:
            @block.gpsimd
            def _(pool):
                pool.tensor_copy(xq[0][:, :], xnT[:, 0:P]).then_inc(s_q, 1)
                with pool.Fori(0, TILES // 2) as tt:
                    pool.wait_ge(s_s, tt * UN + 1)
                    pool.tensor_copy(xq[1][:, :], xnT[:, bass.ds(tt * 2 * P + P, P)]).then_inc(s_q, 1)
                    pool.wait_ge(s_s, tt * UN + HEADS + 1)
                    pool.tensor_copy(xq[0][:, :], xnT[:, bass.ds((tt * 2 + 2) % TILES * P, P)]).then_inc(s_q, 1)

            @block.tensor
            def _(pe):
                def score(n, u):
                    pe.wait_ge(s_e, n + 1)
                    hd = u % HEADS
                    pe.matmul(BS[u % 4][:, :], xq[u // HEADS][:, :], Kq[:, hd, :], start=True, stop=True).then_inc(s_s, 1)

                pe.wait_ge(s_q, 1)
                score(0, 0)
                score(1, 1)
                with pe.Fori(0, TILES // 2) as tt:
                    for u in range(UN):
                        n = tt * UN + u
                        nx = u + 2
                        if nx == HEADS:
                            pe.wait_ge(s_q, tt * 2 + 2)
                        if nx == UN:
                            pe.wait_ge(s_q, tt * 2 + 3)
                        pe.wait_ge(s_e, n + 5)
                        pe.wait_ge(s_pt, n + 1)
                        for t in range(KT_N):
                            last = pe.transpose(BT[u % 2][:, t * P:(t + 1) * P], Pr[u % 2][:, t * P:(t + 1) * P], ident)
                        last.then_inc(s_t, 1)
                        score(n + 2, nx % UN)
                        pe.wait_ge(s_pt, n + 3)
                        pe.wait_ge(s_acc, n + 1)
                        for t in range(KT_N):
                            last = pe.matmul(BO[u % 2][:, 0:D], PT[u % 2][:, t * P:(t + 1) * P], VW[:, u % HEADS, t, :],
                                             start=(t == 0), stop=(t == KT_N - 1))
                        last.then_inc(s_o, 1)

            @block.scalar
            def _(act):
                def exps(n, u):
                    act.wait_ge(s_m, n + 1)
                    act.activation(Pr[u % 2][:, :], BS[u % 4][:, :], ACT.Exp, bias=nmx[:, u:u + 1],
                                   accum_out=den[:, u:u + 1]).then_inc(s_e, 1)

                act.sem_inc(s_e, 4)
                act.sem_inc(s_pt, 2)
                exps(0, 0)
                with act.Fori(0, TILES // 2) as tt:
                    for u in range(UN):
                        n = tt * UN + u
                        act.wait_ge(s_t, n + 1)
                        act.activation(PT[u % 2][:, :], BT[u % 2][:, :], ACT.Copy).then_inc(s_pt, 1)
                        exps(n + 1, (u + 1) % UN)

            @block.vector
            def _(dve):
                def top(n, u):
                    dve.wait_ge(s_s, n + 1)
                    dve.tensor_reduce(nmx[:, u:u + 1], BS[u % 4][:, :], AX.X, ALU.max, negate=True).then_inc(s_m, 1)

                dve.sem_inc(s_acc, 2)
                top(0, 0)
                top(1, 1)
                with dve.Fori(0, TILES // 2) as tt:
                    for u in range(UN):
                        n = tt * UN + u
                        top(n + 2, (u + 2) % UN)
                        dve.wait_ge(s_e, n + 5)
                        dve.reciprocal(rec[:, u:u + 1], den[:, u:u + 1]).then_inc(s_rc, 1)
                        dve.wait_ge(s_rc, n + 1)
                        dve.wait_ge(s_o, n + 1)
                        j = tt * 2 + u // HEADS
                        xj = X[:, bass.ds(j, 1), :].rearrange("p a n -> p (a n)")
                        dve.wait_ge(s_acc, n + 2)
                        dve.scalar_tensor_tensor(xj, BO[u % 2][:, 0:D], rec[:, u:u + 1], xj, ALU.mult, ALU.add).then_inc(s_acc, 1)


def kernel(**inp):
    import numpy as np
    import concourse.bacc as bacc
    from concourse import mybir as mb
    from concourse.bass_utils import run_bass_kernel_spmd as run

    g = {k: np.asarray(v) for k, v in inp.items()}
    f = np.float32
    r, c = np.arange(P)[:, None], np.arange(P)[None, :]
    planes = [r == c, r <= c, r > c, r < c, np.ones((P, P))]
    for lv in range(LEVELS):
        m = 1 << lv
        planes.append((r // (2 * m) == c // (2 * m)) & ((r // m) % 2 == 0) & ((c // m) % 2 == 1))
    vecs = np.zeros((P, V_END), f)
    vecs[:, V_EM8:V_EM8 + E] = np.arange(E) - E
    vecs[:, V_KTH:V_KTH + TILES] = P * np.arange(TILES)
    vecs[:, V_TILE:V_TILE + 40] = np.arange(40)
    vecs[:, V_ROW:V_ROW + TILES] = r * TILES + np.arange(TILES)
    vecs[:, V_SCAN:V_SCAN + P] = np.arange(P) % TILES != 0

    def pick(*names):
        return [g["L0_attn_" + n] for n in names]

    ex0, ex1 = g["L0_ffn_W1"], g["L1_ffn_w1_w"]
    arrays = {
        "x": g["L0_attn_x"].reshape(SEQS, CHUNKS, P, D).transpose(2, 1, 0, 3).reshape(P, TILES, D),
        "consts": np.stack(planes, 1).astype(f),
        "vecs": vecs,
        "wcat": np.concatenate(pick("Wk", "Wv", "Wq", "Wg"), 1),
        "bcat": np.concatenate(pick("bk", "bv", "bq", "bg")),
        "wab": np.concatenate(pick("Wa", "Wb"), 1),
        "bab": np.concatenate(pick("ba", "bb")),
        "wo": g["L0_attn_Wo"], "bo": g["L0_attn_bo"], "bout": g["L1_attn_bout"],
        "wr0": g["L0_ffn_Wr"], "br0": g["L0_ffn_br"], "wr1": g["L1_ffn_router_w"].T,
        "w1a": g["L0_ffn_W1"].transpose(1, 0, 2).reshape(D, E * F),
        "b1a": g["L0_ffn_b1"].reshape(-1),
        "w2a": g["L0_ffn_W2"].reshape(E, FT, P, D).transpose(2, 0, 1, 3).reshape(P, E * F),
        "b2a": g["L0_ffn_b2"].reshape(-1),
        "ctxT": g["L1_attn_context"].reshape(KEYS, CTX).T,
        "wk": g["L1_attn_Wk"], "wv": g["L1_attn_Wv"],
        "wqT": g["L1_attn_Wq"].reshape(D, HEADS, P).transpose(2, 1, 0),
        "wout": g["L1_attn_Wout"].reshape(HEADS, P, D).transpose(1, 0, 2),
        "w1b": g["L1_ffn_w1_w"].transpose(2, 0, 1).reshape(D, E * F),
        "wgb": g["L1_ffn_wg_w"].transpose(2, 0, 1).reshape(D, E * F),
        "w2b": g["L1_ffn_w2_w"].reshape(E, D, FT, P).transpose(3, 0, 2, 1).reshape(P, E * F),
        "b1b": g["L1_ffn_w1_b"].reshape(-1), "bgb": g["L1_ffn_wg_b"].reshape(-1), "b2b": g["L1_ffn_w2_b"].reshape(-1),
    }
    nc = bacc.Bacc("TRN2", target_bir_lowering=False, num_devices=1)
    feeds, aps = {}, {}
    for name, arr in arrays.items():
        arr = np.ascontiguousarray(arr)
        feeds[f"in_{name}"] = arr
        aps[name] = nc.dram_tensor(f"in_{name}", arr.shape, mb.dt.from_np(arr.dtype), kind="ExternalInput").ap()
    out = nc.dram_tensor("out_0", (P, TILES, D), F32, kind="ExternalOutput").ap()
    build(nc, aps, out)
    res = run(nc, [feeds], core_ids=[0]).results[0]["out_0"]
    return res.reshape(P, CHUNKS, SEQS, D).transpose(2, 1, 0, 3).reshape(SEQS, CHUNKS * P, D)
```

```python
from contextlib import ExitStack

import concourse.bass as bass
from concourse import mybir

F32 = mybir.dt.float32
I32 = mybir.dt.int32
U32 = mybir.dt.uint32
ALU = mybir.AluOpType
ACT = mybir.ActivationFunctionType
AX = mybir.AxisListType

STAGE = 4
P = 128
SEQS, CHUNKS = 4, 4
TILES = SEQS * CHUNKS
D = 128
E = 8
F = 512
FT = F // P
HEADS = 8
KEYS = 512
KT_N = KEYS // P
CTX = 96
LEVELS = 7
ROW = 130
DEST, GATE = 128, 129
FAR = 1.0e6
SIM_SCALE = 128 ** -0.5
MATRIX_SCALE = 1.5
EPS = 1e-5
IDENT, TRI_INC, LOW_STRICT, UP_STRICT, ONES, PAIRS = 0, 1, 2, 3, 4, 5
V_EM8, V_KTH, V_TILE, V_ROW, V_SCAN, V_END = 0, 8, 24, 64, 80, 208


REGION = TILES * P
LINKS = 12 + 1 + 1 + 3 + 6 + 6 + 6


def slot_tiles(choices):
    return choices * TILES + E - 1


def last_col(ap, n):
    return ap.unsqueeze(2).broadcast_to([ap.shape[0], ap.shape[1], n])


def mid_col(ap, n):
    return ap.unsqueeze(1).broadcast_to([ap.shape[0], n, ap.shape[1]])


class Chain:

    def __init__(self, sem):
        self.sem, self.n = sem, 0

    def run(self, eng, ins):
        self.n += 1
        ins.then_inc(self.sem, 1)
        eng.wait_ge(self.sem, self.n)


def rsqrt(dve, chain, v, y, t):
    chain.run(dve, dve.tensor_scalar(y.bitcast(I32), v.bitcast(I32), 1, None, ALU.logical_shift_right))
    chain.run(dve, dve.tensor_scalar(y.bitcast(I32), y.bitcast(I32), -1.0, float(0x5F3759DF), ALU.mult, ALU.add))
    for _ in range(3):
        chain.run(dve, dve.tensor_tensor(t, y, y, ALU.mult))
        chain.run(dve, dve.scalar_tensor_tensor(t, t, -0.5, v, ALU.mult, ALU.mult))
        chain.run(dve, dve.scalar_tensor_tensor(y, t, 1.5, y, ALU.add, ALU.mult))


def layernorm_stats(dve, chain, X, st6, mv, var, rstd, tmp):
    moments(dve, chain, X, st6, mv, range(TILES))
    deviations(dve, chain, mv, var, rstd, tmp)


def moments(dve, chain, X, st6, mv, tiles):
    for j in tiles:
        last = dve.bn_stats(st6[:, j, :], X[:, j, :])
    chain.run(dve, last)
    for j in tiles:
        last = dve.bn_aggr(mv[:, j, :], st6[:, j, :])
    chain.run(dve, last)


def deviations(dve, chain, mv, var, rstd, tmp):
    chain.run(dve, dve.tensor_scalar(var[:, :], mv[:, :, 1], EPS, None, ALU.add))
    rsqrt(dve, chain, var[:, :], rstd[:, :], tmp[:, :])


class KeyValues:

    def __init__(self, top, nc, bank, a, Kq, VW, bout_b):
        self.bout_b = bout_b
        self.bank, self.a, self.Kq, self.VW = bank, a, Kq, VW
        self.s_w, self.s_kt, self.s_kte, self.s_vt, self.s_vte, self.s_kq, self.s_vw, self.s_vwe, self.s_mean, self.s_me2, self.s_bq = (
            top.enter_context(nc.semaphore(f"kv_{n}"))
            for n in ("w", "kt", "kte", "vt", "vte", "kq", "vw", "vwe", "mean", "me2", "bq"))

    def place(self, sb):
        self.cT = sb("kv_cT", [CTX, KEYS])
        self.wk = sb("kv_wk", [CTX, HEADS * P])
        self.wv = sb("kv_wv", [CTX, HEADS * P])
        self.wqT = sb("kv_wqT", [P, HEADS, P])
        self.wout = sb("kv_wout", [P, HEADS, P])
        self.KTh = [sb(f"kv_KTh{i}", [P, KEYS]) for i in range(2)]
        self.VTh = [sb(f"kv_VTh{i}", [P, KEYS]) for i in range(2)]
        self.ksum = sb("kv_ksum", [P, HEADS])

    def sync(self, sp):
        for t, name in ((self.cT, "ctxT"), (self.wk, "wk"), (self.wqT, "wqT"), (self.wv, "wv"), (self.wout, "wout")):
            sp.dma_start(t[:], self.a[name]).then_inc(self.s_w, 16)

    def tensor(self, pe):
        bank = self.bank
        pe.wait_ge(self.s_w, 16 * 5)

        def spread(hd):
            if hd:
                pe.wait_ge(self.s_kte, hd)
            pe.matmul(bank[0][:, :], self.wk[:, hd * P:(hd + 1) * P], self.cT[:, :], start=True, stop=True).then_inc(self.s_kt, 1)
            if hd:
                pe.wait_ge(self.s_vte, hd)
            pe.matmul(bank[1][:, :], self.wv[:, hd * P:(hd + 1) * P], self.cT[:, :], start=True, stop=True).then_inc(self.s_vt, 1)

        spread(0)
        for hd in range(HEADS):
            if hd < HEADS - 1:
                spread(hd + 1)
            if hd:
                pe.wait_ge(self.s_bq, hd)
            pe.wait_ge(self.s_kte, hd + 1)
            pe.matmul(bank[2][:, :], self.wqT[:, hd, :], self.KTh[hd % 2][:, :], start=True, stop=True).then_inc(self.s_kq, 1)
            if hd:
                pe.wait_ge(self.s_vwe, hd)
            pe.wait_ge(self.s_vte, hd + 1)
            for t in range(KT_N):
                last = pe.matmul(bank[3][:, t * P:(t + 1) * P], self.VTh[hd % 2][:, t * P:(t + 1) * P], self.wout[:, hd, :],
                                 start=True, stop=True)
            last.then_inc(self.s_vw, 1)

    def scalar(self, act):
        bank = self.bank

        def spread(hd):
            act.wait_ge(self.s_kt, hd + 1)
            if hd >= 2:
                act.wait_ge(self.s_kq, hd - 1)
            act.activation(self.KTh[hd % 2][:, :], bank[0][:, :], ACT.Copy).then_inc(self.s_kte, 1)
            act.wait_ge(self.s_vt, hd + 1)
            if hd >= 2:
                act.wait_ge(self.s_vw, hd - 1)
            act.activation(self.VTh[hd % 2][:, :], bank[1][:, :], ACT.Copy).then_inc(self.s_vte, 1)

        spread(0)
        for hd in range(HEADS):
            if hd < HEADS - 1:
                spread(hd + 1)
            if hd == 0:
                continue
            act.wait_ge(self.s_vw, hd + 1)
            act.activation(self.VW[:, hd, :, :].rearrange("p a n -> p (a n)"), bank[3][:, :], ACT.Copy).then_inc(self.s_vwe, 1)

    def vector(self, dve):
        bank, ksum = self.bank, self.ksum
        for hd in range(HEADS):
            dve.wait_ge(self.s_kq, hd + 1)
            dve.tensor_reduce(ksum[:, hd:hd + 1], bank[2][:, :], AX.X, ALU.add).then_inc(self.s_mean, 1)
            dve.wait_ge(self.s_mean, hd + 1)
            dve.tensor_scalar(ksum[:, hd:hd + 1], ksum[:, hd:hd + 1],
                              SIM_SCALE * (1.0 - MATRIX_SCALE) / KEYS, None, ALU.mult).then_inc(self.s_me2, 1)
            dve.wait_ge(self.s_me2, hd + 1)
            dve.tensor_scalar(self.Kq[:, hd, :], bank[2][:, :], SIM_SCALE * MATRIX_SCALE, ksum[:, hd:hd + 1],
                              ALU.mult, ALU.add).then_inc(self.s_bq, 1)
            if hd == 0:
                dve.wait_ge(self.s_vw, 1)
                dve.tensor_tensor(self.VW[:, 0, :, :], bank[3][:, :].rearrange("p (t d) -> p t d", t=KT_N),
                                  mid_col(self.bout_b[:, :], KT_N), ALU.add).then_inc(self.s_vwe, 1)


def build(nc, a, out):
    with ExitStack() as top:
        def alloc(ctx):
            return lambda name, shape, dt=F32: ctx.enter_context(nc.sbuf_tensor(name, shape, dt))

        def sem(name):
            return top.enter_context(nc.semaphore(name))

        sb = alloc(top)
        bank = [top.enter_context(nc.psum_tensor(f"bank{i}", [P, 512], F32)) for i in range(8)]

        def quad(ap):
            return ap.rearrange("p (a n) -> p a n", a=4)

        X = sb("X", [P, TILES, D])
        C = sb("C", [P, 5 + LEVELS, P])
        V = sb("V", [P, V_END])
        ident = C[:, IDENT, :]
        mv = sb("mv", [P, TILES, 2])
        st6 = sb("st6", [P, TILES, 6])
        var = sb("var", [P, TILES])
        rstd = sb("rstd", [P, TILES])
        tmp = sb("tmp", [P, TILES])
        bo_b = sb("bo_b", [P, D])
        bout_b = sb("bout_b", [P, D])
        wr0 = sb("wr0", [P, E])
        br0 = sb("br0", [P, E])
        wr1 = sb("wr1", [P, E])
        fill = sb("fill", [P, ROW])
        plan_i = sb("plan_i", [P, TILES * 2], I32)
        expert_i = sb("expert_i", [1, 40], I32)
        start_i = sb("start_i", [1, 40], I32)
        cum = sb("cum", [P, E])

        wide = sb("wide", [P, 2 * HEADS * KEYS])
        kvqg = wide[:, :].rearrange("p (t c n) -> p t c n", t=TILES, c=4)
        Kq = wide[:, 0:HEADS * KEYS].rearrange("p (h k) -> p h k", h=HEADS)
        VW = wide[:, HEADS * KEYS:2 * HEADS * KEYS].rearrange("p (h t d) -> p h t d", h=HEADS, t=KT_N)

        slots = [nc.dram_tensor(f"slots{n}", [rows, ROW], F32, kind="Internal").ap()
                 for n, rows in enumerate((slot_tiles(1) * P, (E - 1) * REGION + slot_tiles(2) * P))]
        fills = [(n, r, min(r + 16 * P, slots[n].shape[0])) for n in range(2) for r in range(0, slots[n].shape[0], 16 * P)]
        byrow = [nc.dram_tensor(f"byrow{n}", [(n + 1) * TILES * P, D], F32, kind="Internal").ap()
                 for n in range(2)]

        chain = Chain(sem("s_chain"))
        s_x = sem("s_x")
        s_const = sem("s_const")
        s_w0 = sem("s_w0")
        s_ffn0 = sem("s_ffn0")
        s_fillz = sem("s_fillz")
        s_fill = sem("s_fill")
        s_attnw = sem("s_attnw")
        s_ffn1 = sem("s_ffn1")

        s_out = sem("s_out")
        norm = (st6, mv, var, rstd, tmp)

        ffn = ExitStack()
        sf = alloc(ffn)
        w1a = sf("w1a", [P, E * F])
        w2a = sf("w2a", [P, E * F])
        b1a = sf("b1a", [P, E * F])
        b2a = sf("b2a", [P, E * D])

        ab = ExitStack()
        sa = alloc(ab)
        dec = sa("dec", [P, 3, TILES])
        beta = sa("beta", [P, TILES])
        la = sa("la", [P, TILES])
        rn = sa("rn", [P, TILES])
        wo = sa("wo", [P, D])

        with ExitStack() as ctx:
            s1 = alloc(ctx)
            wcat = s1("wcat", [P, 512])
            bcat = s1("bcat", [P, 512])
            wab = s1("wab", [P, 2])
            bab = s1("bab", [P, 2])
            xn = [s1(f"xn{i}", [P, 4, D]) for i in range(CHUNKS)]
            xnT = [s1(f"xnT{i}", [P, 512]) for i in range(CHUNKS)]
            nmr = s1("nmr", [P, TILES])
            z = s1("z", [P, TILES, 2])
            az = s1("az", [P, TILES, 2])
            ez = s1("ez", [P, TILES, 2])
            lz = s1("lz", [P, TILES, 2])
            lb = s1("lb", [P, TILES])
            junk = s1("junk", [P, D])
            ss = s1("ss", [P, TILES])
            s_ln = sem("a_ln")
            s_x1 = sem("a_x1")
            s_wp = sem("a_wp")
            s_xn = sem("a_xn")
            s_tr = sem("a_tr")
            s_xT = sem("a_xT")
            s_pj = sem("a_pj")
            s_ev = sem("a_ev")
            s_az = sem("a_az")
            s_lz = sem("a_lz")
            s_la = sem("a_la")
            s_cum = sem("a_cum")
            s_z = sem("a_z")
            s_sq = sem("a_sq")
            block = ctx.enter_context(nc.Block())

            @block.sync
            def _(sp):
                sp.dma_start(X[:, 0:4, :], a["x"][:, 0:4, :]).then_inc(s_x, 16)
                sp.dma_start(C[:, :, :], a["consts"]).then_inc(s_const, 16)
                sp.dma_start(X[:, 4:TILES, :], a["x"][:, 4:TILES, :]).then_inc(s_x1, 16)
                sp.dma_start(wab[:, :], a["wab"]).then_inc(s_wp, 16)
                sp.dma_start(wcat[:, :], a["wcat"]).then_inc(s_wp, 16)
                sp.dma_start(bcat[:, :], a["bcat"].partition_broadcast(P)).then_inc(s_wp, 16)
                sp.dma_start(bab[:, :], a["bab"].partition_broadcast(P)).then_inc(s_wp, 16)
                sp.dma_start(V[:, :], a["vecs"]).then_inc(s_const, 16)
                sp.dma_start(wo[:, :], a["wo"]).then_inc(s_w0, 16)
                sp.dma_start(bo_b[:, :], a["bo"].partition_broadcast(P)).then_inc(s_w0, 16)
                sp.dma_start(bout_b[:, :], a["bout"].partition_broadcast(P)).then_inc(s_w0, 16)
                sp.dma_start(wr0[:, :], a["wr0"]).then_inc(s_w0, 16)
                sp.dma_start(br0[:, :], a["br0"].partition_broadcast(P)).then_inc(s_w0, 16)
                sp.dma_start(wr1[:, :], a["wr1"]).then_inc(s_w0, 16)
                sp.dma_start(w1a[:, :], a["w1a"]).then_inc(s_ffn0, 16)
                sp.dma_start(w2a[:, :], a["w2a"]).then_inc(s_ffn0, 16)
                sp.dma_start(b1a[:, :], a["b1a"].partition_broadcast(P)).then_inc(s_ffn0, 16)
                sp.dma_start(b2a[:, :], a["b2a"].partition_broadcast(P)).then_inc(s_ffn0, 16)
                sp.wait_ge(s_fillz, 2)
                for n, lo, hi in fills:
                    sp.dma_start(slots[n][lo:hi, :].rearrange("(a p) w -> p a w", p=P),
                                 mid_col(fill[:, :], (hi - lo) // P)).then_inc(s_fill, 16)

            @block.gpsimd
            def _(pool):
                pool.memset(fill[:, :], 0.0).then_inc(s_fillz, 1)
                pool.wait_ge(s_fillz, 1)
                pool.memset(fill[:, DEST:DEST + 1], FAR).then_inc(s_fillz, 1)

            @block.vector
            def _(dve):
                def norm(lo, hi):
                    moments(dve, chain, X, st6, mv, range(lo, hi))
                    deviations(dve, chain, mv[:, lo:hi, :], var[:, lo:hi], rstd[:, lo:hi], tmp[:, lo:hi])
                    dve.scalar_tensor_tensor(nmr[:, lo:hi], mv[:, lo:hi, 0], -1.0, rstd[:, lo:hi], ALU.mult, ALU.mult).then_inc(s_ln, 1)

                def evict(n):
                    dve.wait_ge(s_pj, n + 1)
                    dve.tensor_tensor(kvqg[:, n, :, :].rearrange("p c n -> p (c n)"),
                                      bank[2 + n % 4][:, :], bcat[:, :], ALU.add).then_inc(s_ev, 1)

                def normalize(g):
                    for k in range(4):
                        j = 4 * g + k
                        last = dve.tensor_scalar(xn[g][:, k, :], X[:, j, :], mv[:, j, 0:1], rstd[:, j:j + 1],
                                                 ALU.subtract, ALU.mult)
                    last.then_inc(s_xn, 1)

                dve.wait_ge(s_x, 16)
                moments(dve, chain, X, st6, mv, range(4))
                deviations(dve, chain, mv[:, 0:4, :], var[:, 0:4], rstd[:, 0:4], tmp[:, 0:4])
                normalize(0)
                dve.wait_ge(s_x1, 16)
                norm(4, TILES)
                normalize(1)
                dve.wait_ge(s_wp, 64)
                for n in range(6):
                    evict(n)
                dve.wait_ge(s_z, 1)
                chain.run(dve, dve.tensor_tensor(z[:, :, :], bank[6][:, 0:2 * TILES].rearrange("p (a n) -> p a n", n=2),
                                            mid_col(bab[:, :], TILES), ALU.add))
                dve.scalar_tensor_tensor(az[:, :, :], z[:, :, :], -1.0, z[:, :, :], ALU.mult, ALU.max).then_inc(s_az, 1)
                for n in range(6, 12):
                    evict(n)
                dve.wait_ge(s_lz, 2)
                dve.scalar_tensor_tensor(lb[:, :], z[:, :, 1], 0.0, lz[:, :, 1], ALU.min, ALU.subtract).then_inc(s_la, 1)
                dve.scalar_tensor_tensor(la[:, :], z[:, :, 0], 0.0, lz[:, :, 0], ALU.min, ALU.subtract).then_inc(s_la, 1)
                for n in range(12, TILES):
                    evict(n)
                dve.wait_ge(s_sq, TILES)
                chain.run(dve, dve.tensor_scalar(ss[:, :], ss[:, :], 1e-24, None, ALU.max))
                rsqrt(dve, chain, ss[:, :], rn[:, :], tmp[:, :])
                dve.wait_ge(s_w0, 16 * 6)

            @block.tensor
            def _(pe):
                def turn(g):
                    pe.wait_ge(s_xn, g + 1)
                    if g >= 2:
                        pe.wait_ge(s_xT, g - 1)
                    for k in range(4):
                        last = pe.transpose(bank[g % 2][:, k * P:(k + 1) * P], xn[g][:, k, :], ident)
                    last.then_inc(s_tr, 1)

                def gates(g):
                    pe.wait_ge(s_xT, g + 1)
                    for k in range(4):
                        n = 4 * g + k
                        last = pe.matmul(bank[6][:, n * 2:n * 2 + 2], xnT[g][:, k * P:(k + 1) * P], wab[:, :], start=True, stop=True)
                    return last

                def project(g):
                    for k in range(4):
                        if g:
                            pe.wait_ge(s_ev, 4 * g + k - 3)
                        pe.matmul(bank[2 + k][:, :], xnT[g][:, k * P:(k + 1) * P], wcat[:, :],
                                  start=True, stop=True).then_inc(s_pj, 1)

                pe.wait_ge(s_const, 32)
                turn(0)
                pe.wait_ge(s_wp, 64)
                gates(0)
                project(0)
                turn(1)
                turn(2)
                gates(1)
                project(1)
                turn(3)
                gates(2)
                gates(3).then_inc(s_z, 1)
                project(2)
                project(3)
                pe.wait_ge(s_la, 2)
                pe.matmul(bank[7][:, 0:16], C[:, TRI_INC, :], la[:, :], start=True, stop=True)
                pe.matmul(bank[7][:, 16:32], C[:, LOW_STRICT, :], la[:, :], start=True, stop=True)
                pe.matmul(bank[7][:, 32:48], C[:, ONES, :], la[:, :], start=True, stop=True).then_inc(s_cum, 1)
                pe.wait_ge(s_w0, 16 * 6)

            @block.scalar
            def _(act):
                def square(n):
                    act.wait_ge(s_ev, n + 1)
                    if n:
                        act.wait_ge(s_sq, n)
                    act.activation(junk[:, :], kvqg[:, n, 0, :], ACT.Square, accum_out=ss[:, n:n + 1]).then_inc(s_sq, 1)

                for g in range(CHUNKS):
                    if g >= 2:
                        act.wait_ge(s_ln, 1)
                        act.wait_ge(s_xn, g)
                        for k in range(4):
                            j = 4 * g + k
                            last = act.activation(xn[g][:, k, :], X[:, j, :], ACT.Identity, bias=nmr[:, j:j + 1], scale=rstd[:, j:j + 1])
                        last.then_inc(s_xn, 1)
                    act.wait_ge(s_tr, g + 1)
                    act.activation(xnT[g][:, :], bank[g % 2][:, :], ACT.Copy).then_inc(s_xT, 1)
                act.wait_ge(s_az, 1)
                act.activation(ez[:, :, :], az[:, :, :], ACT.Exp, scale=-1.0).then_inc(s_lz, 1)
                act.wait_ge(s_lz, 1)
                act.activation(lz[:, :, :], ez[:, :, :], ACT.Ln, bias=1.0).then_inc(s_lz, 1)
                for n in range(8):
                    square(n)
                act.wait_ge(s_la, 1)
                act.activation(beta[:, :], lb[:, :], ACT.Exp)
                for n in range(8, TILES):
                    square(n)
                act.wait_ge(s_cum, 1)
                act.activation(dec[:, :, :].rearrange("p a n -> p (a n)"), bank[7][:, 0:48], ACT.Exp)
                act.activation(kvqg[:, :, 3, :], kvqg[:, :, 3, :], ACT.Sigmoid)

        with ExitStack() as ctx:
            s2 = alloc(ctx)
            bgK = s2("bgK", [P, TILES, P])
            EK = s2("EK", [P, TILES, P])
            QT = s2("QT", [P, TILES, P])
            gQT = s2("gQT", [P, TILES, P])
            gateT = s2("gateT", [P, TILES, P])
            DT = s2("DT", [P, TILES, P])
            AT = s2("AT", [P, TILES, P])
            AM = s2("AM", [P, TILES, P])
            XL = s2("XL", [P, TILES, P])
            TI = s2("TI", [P, TILES, P])
            RI = s2("RI", [P, TILES, P])
            t_a = s2("t_a", [P, 4, P])
            kb, gQ, rla = TI, XL, AM
            d_kn = sem("b_kn")
            d_kb = sem("b_kb")
            p_el = sem("b_el")
            p_dt = sem("b_dt")
            q_tr = sem("b_tr")
            q_lt = sem("b_lt")
            q_at = sem("b_at")
            a_ev = sem("b_aev")
            a_lt = sem("b_alt")
            d_ev = sem("b_dev")
            d_at = sem("b_dat")
            d_r0 = sem("b_r0")
            d_c = sem("b_dvec")
            q_t0 = sem("b_t0")
            a_t0 = sem("b_at0")
            p_am = sem("b_am")
            q_x = sem("b_x")
            a_x = sem("b_ax")
            q_y = sem("b_y")
            d_t = sem("b_t")
            q_r = sem("b_r")
            a_r = sem("b_ar")
            KTb = s2("KTb", [P, 4, P])
            kbTb = s2("kbTb", [P, 4, P])

            with nc.Block() as block:
                def grp(t, g):
                    return t[:, 4 * g:4 * g + 4, :]

                def col(t, g):
                    return last_col(t[:, 4 * g:4 * g + 4], P)

                def kv(g, c):
                    return kvqg[:, 4 * g:4 * g + 4, c, :]

                @block.vector
                def _(dve):
                    for g in range(CHUNKS):
                        dve.tensor_tensor(kv(g, 0), kv(g, 0), col(rn, g), ALU.mult).then_inc(d_kn, 1)
                        dve.wait_ge(d_kn, g + 1)
                        dve.tensor_tensor(grp(kb, g), kv(g, 0), col(beta, g), ALU.mult).then_inc(d_kb, 1)
                        dve.tensor_tensor(kv(g, 1), kv(g, 1), col(beta, g), ALU.mult).then_inc(d_kb, 1)
                    for g in range(CHUNKS):
                        dve.wait_ge(q_tr, 5 * g + 3)
                        dve.tensor_copy(grp(QT, g), quad(bank[2][:, :])).then_inc(d_ev, 1)
                        dve.wait_ge(q_tr, 5 * g + 5)
                        dve.tensor_copy(grp(gateT, g), quad(bank[4][:, :])).then_inc(d_ev, 1)
                        dve.wait_ge(q_at, g + 1)
                        dve.wait_ge(p_dt, g + 1)
                        dve.tensor_tensor(grp(AT, g), quad(bank[6][:, :]), grp(DT, g), ALU.mult).then_inc(d_at, 1)
                        dve.wait_ge(d_at, g + 1)
                        if g:
                            dve.wait_ge(d_r0, g)
                        dve.tensor_tensor(t_a[:, :, :], grp(AT, g), mid_col(C[:, PAIRS, :], 4), ALU.mult).then_inc(d_c, 1)
                        dve.wait_ge(d_c, g + 1)
                        dve.tensor_tensor(grp(RI, g), mid_col(ident, 4), t_a[:, :, :], ALU.subtract).then_inc(d_r0, 1)
                    chain.run(dve, dve.tensor_tensor(X[:, :, :], X[:, :, :], mid_col(bo_b[:, :], TILES), ALU.add))
                    with dve.Fori(1, LEVELS) as lv:
                        for g in range(CHUNKS):
                            dve.wait_ge(q_y, lv * 4 + (g + 1 - 4))
                            dve.tensor_tensor(grp(TI, g), grp(TI, g), quad(bank[4 + g][:, :]), ALU.subtract).then_inc(d_t, 1)

                @block.gpsimd
                def _(pool):
                    for g in range(CHUNKS):
                        pool.tensor_tensor(grp(rla, g), mid_col(C[:, TRI_INC, :], 4), col(la, g), ALU.mult).then_inc(p_el, 1)
                        pool.tensor_tensor(grp(gQ, g), kv(g, 2), last_col(dec[:, 0, 4 * g:4 * g + 4], P), ALU.mult).then_inc(p_el, 1)
                        pool.wait_ge(d_kn, g + 1)
                        pool.tensor_tensor(grp(EK, g), kv(g, 0), last_col(dec[:, 1, 4 * g:4 * g + 4], P), ALU.mult).then_inc(p_el, 1)
                        pool.wait_ge(d_kb, 2 * g + 1)
                        pool.tensor_tensor(grp(bgK, g), grp(kb, g), last_col(dec[:, 0, 4 * g:4 * g + 4], P), ALU.mult).then_inc(p_el, 1)
                        pool.wait_ge(a_lt, g + 1)
                        pool.tensor_tensor(grp(DT, g), grp(DT, g), mid_col(C[:, TRI_INC, :], 4), ALU.mult).then_inc(p_dt, 1)
                    pool.wait_ge(q_lt, CHUNKS)
                    for lv in range(1, LEVELS):
                        for g in range(CHUNKS):
                            pool.wait_ge(d_at, g + 1)
                            pool.wait_ge(q_x, lv * 4 + (g + 1 - 4))
                            pool.tensor_tensor(grp(AM, g), grp(AT, g),
                                               mid_col(C[:, PAIRS + lv, :], 4),
                                               ALU.mult).then_inc(p_am, 1)

                @block.tensor
                def _(pe):
                    pe.sem_inc(q_x, 4)
                    for g in range(CHUNKS):
                        pe.wait_ge(p_el, 4 * g + 1)
                        if g:
                            pe.wait_ge(a_lt, g)
                        pe.matmul(bank[5][:, :], C[:, LOW_STRICT, :], grp(rla, g).rearrange("p a n -> p (a n)"),
                                  start=True, stop=True).then_inc(q_lt, 1)
                        pe.wait_ge(d_kb, 2 * g + 2)
                        pe.wait_ge(p_el, 4 * g + 2)
                        for i, src in enumerate((kv(g, 0), grp(kb, g), kv(g, 2), grp(gQ, g), kv(g, 3))):
                            if g:
                                if i in (2, 4):
                                    pe.wait_ge(d_ev, 2 * g - (1 if i == 2 else 0))
                                else:
                                    pe.wait_ge(a_ev, 3 * (g - 1) + {0: 1, 1: 2, 3: 3}[i])
                            for b in range(SEQS):
                                last = pe.transpose(bank[i][:, b * P:(b + 1) * P], src[:, b, :], ident)
                            last.then_inc(q_tr, 1)
                        pe.wait_ge(a_ev, 3 * g + 2)
                        if g:
                            pe.wait_ge(d_at, g)
                        for b in range(SEQS):
                            last = pe.matmul(bank[6][:, b * P:(b + 1) * P], KTb[:, b, :], kbTb[:, b, :], start=True, stop=True)
                        last.then_inc(q_at, 1)
                    for g in range(CHUNKS):
                        pe.wait_ge(d_r0, g + 1)
                        if g:
                            pe.wait_ge(a_t0, g)
                        for b in range(SEQS):
                            last = pe.transpose(bank[7][:, b * P:(b + 1) * P], RI[:, 4 * g + b, :], ident)
                        last.then_inc(q_t0, 1)
                    pe.wait_ge(a_t0, CHUNKS)
                    pe.wait_ge(a_ev, 3 * CHUNKS)
                    pe.wait_ge(d_ev, 2 * CHUNKS)
                    with pe.Fori(1, LEVELS) as lv:
                        for g in range(CHUNKS):
                            pe.wait_ge(a_r, lv * 4 + (g + 1 - 4))
                            pe.wait_ge(p_am, lv * 4 + (g + 1 - 4))
                            for b in range(SEQS):
                                last = pe.matmul(bank[g][:, b * P:(b + 1) * P], AM[:, 4 * g + b, :], TI[:, 4 * g + b, :],
                                                 start=True, stop=True)
                            last.then_inc(q_x, 1)
                        for g in range(CHUNKS):
                            pe.wait_ge(a_x, lv * 4 + (g + 1 - 4))
                            for b in range(SEQS):
                                last = pe.matmul(bank[4 + g][:, b * P:(b + 1) * P], RI[:, 4 * g + b, :], XL[:, 4 * g + b, :],
                                                 start=True, stop=True)
                            last.then_inc(q_y, 1)
                        for g in range(CHUNKS):
                            pe.wait_ge(d_t, lv * 4 + (g + 1 - 4))
                            for b in range(SEQS):
                                last = pe.transpose(bank[g][:, b * P:(b + 1) * P], TI[:, 4 * g + b, :], ident)
                            last.then_inc(q_r, 1)

                @block.scalar
                def _(act):
                    act.sem_inc(a_r, 4)
                    for g in range(CHUNKS):
                        act.wait_ge(q_lt, g + 1)
                        act.activation(grp(DT, g), quad(bank[5][:, :]), ACT.Exp).then_inc(a_lt, 1)
                        act.wait_ge(q_tr, 5 * g + 1)
                        if g:
                            act.wait_ge(q_at, g)
                        act.activation(KTb[:, :, :], quad(bank[0][:, :]), ACT.Copy).then_inc(a_ev, 1)
                        act.wait_ge(q_tr, 5 * g + 2)
                        act.activation(kbTb[:, :, :], quad(bank[1][:, :]), ACT.Copy).then_inc(a_ev, 1)
                        act.wait_ge(q_tr, 5 * g + 4)
                        act.activation(grp(gQT, g), quad(bank[3][:, :]), ACT.Copy).then_inc(a_ev, 1)
                    for g in range(CHUNKS):
                        act.wait_ge(q_t0, g + 1)
                        act.wait_ge(p_el, 4 * CHUNKS)
                        act.activation(grp(TI, g), quad(bank[7][:, :]), ACT.Copy).then_inc(a_t0, 1)
                    with act.Fori(1, LEVELS) as lv:
                        for g in range(CHUNKS):
                            act.wait_ge(q_x, lv * 4 + (g + 1))
                            act.activation(grp(XL, g), quad(bank[g][:, :]), ACT.Copy).then_inc(a_x, 1)
                        for g in range(CHUNKS):
                            act.wait_ge(q_r, lv * 4 + (g + 1 - 4))
                            act.activation(grp(RI, g), quad(bank[g][:, :]), ACT.Copy).then_inc(a_r, 1)

            nZT, U, UT, M = AT, AM, XL, TI
            S = s2("S", [P, 4, P])
            ST = s2("ST", [P, 4, P])
            Sg = s2("Sg", [P, 4, P])
            STg = s2("STg", [P, 4, P])
            c_zt = sem("c_zt")
            c_nzt = sem("c_nzt")
            c_u = sem("c_u")
            c_ue = sem("c_ue")
            c_ut = sem("c_ut")
            c_ute = sem("c_ute")
            c_m = sem("c_m")
            c_me = sem("c_me")
            c_o = sem("c_o")
            c_oe = sem("c_oe")
            c_out = sem("c_out")
            c_x = sem("c_x")
            c_s = sem("c_s")
            c_st = sem("c_st")
            c_se = sem("c_se")
            c_g = sem("c_g")
            with nc.Block() as block:
                GO = bgK

                @block.tensor
                def _(pe):
                    def mm4(dst, pairs):
                        for b in range(SEQS):
                            for i, (l, r) in enumerate(pairs):
                                last = pe.matmul(dst[:, b * P:(b + 1) * P], l(b), r(b), start=(i == 0), stop=(i == len(pairs) - 1))
                        return last

                    def at(t, g):
                        return lambda b: t[:, 4 * g + b, :]

                    def kvb(g, c):
                        return lambda b: kvqg[:, 4 * g + b, c, :]

                    def zt(g):
                        if g:
                            pe.wait_ge(c_nzt, g)
                        mm4(bank[0], [(at(bgK, g), at(RI, g))]).then_inc(c_zt, 1)

                    def project(g):
                        pe.wait_ge(c_oe, g + 1)
                        if g:
                            pe.wait_ge(c_x, g)
                        mm4(bank[5], [(at(GO, g), lambda b: wo[:, :])]).then_inc(c_out, 1)

                    pe.wait_ge(c_g, 2)
                    zt(0)
                    for g in range(CHUNKS):
                        pe.wait_ge(c_nzt, g + 1)
                        if g:
                            pe.wait_ge(c_se, 2 * g)
                        mm4(bank[1], [(at(RI, g), kvb(g, 1)), (at(nZT, g), lambda b: ST[:, b, :])]).then_inc(c_u, 1)
                        mm4(bank[2], [(kvb(g, 1), at(RI, g)), (lambda b: ST[:, b, :], at(nZT, g))]).then_inc(c_ut, 1)
                        if g:
                            project(g - 1)
                        if g < CHUNKS - 1:
                            zt(g + 1)
                            pe.wait_ge(c_ue, g + 1)
                            mm4(bank[6], [(at(EK, g), at(U, g))]).then_inc(c_st, 1)
                            mm4(bank[7], [(at(U, g), at(EK, g))]).then_inc(c_s, 1)
                        pe.wait_ge(c_ute, g + 1)
                        if g:
                            pe.wait_ge(c_me, g)
                        mm4(bank[3], [(at(UT, g), at(QT, g))]).then_inc(c_m, 1)
                        pe.wait_ge(c_me, g + 1)
                        mm4(bank[4], [(kvb(g, 0), at(M, g)), (lambda b: S[:, b, :], at(gQT, g))]).then_inc(c_o, 1)
                    project(CHUNKS - 1)

                @block.scalar
                def _(act):
                    def nzt(g):
                        act.wait_ge(c_zt, g + 1)
                        act.activation(grp(nZT, g), quad(bank[0][:, :]), ACT.Copy, scale=-1.0).then_inc(c_nzt, 1)

                    nzt(0)
                    for g in range(CHUNKS):
                        act.wait_ge(c_ut, g + 1)
                        act.activation(grp(UT, g), quad(bank[2][:, :]), ACT.Copy).then_inc(c_ute, 1)
                        if g < CHUNKS - 1:
                            nzt(g + 1)

                @block.gpsimd
                def _(pool):
                    pool.memset(S[:, :, :], 0.0).then_inc(c_g, 1)
                    pool.memset(ST[:, :, :], 0.0).then_inc(c_g, 1)
                    pool.wait_ge(c_g, 2)
                    for g in range(CHUNKS - 1):
                        if g:
                            pool.wait_ge(c_se, 2 * g)
                        for src, dst in ((ST, STg), (S, Sg)):
                            pool.tensor_tensor(dst[:, :, :], src[:, :, :], last_col(dec[:, 2, 4 * g:4 * g + 4], P),
                                               ALU.mult).then_inc(c_g, 1)

                @block.vector
                def _(dve):
                    for g in range(CHUNKS):
                        dve.wait_ge(c_u, g + 1)
                        dve.tensor_copy(grp(U, g), quad(bank[1][:, :])).then_inc(c_ue, 1)
                        if g:
                            dve.wait_ge(c_out, g)
                            dve.tensor_tensor(grp(X, g - 1), grp(X, g - 1), quad(bank[5][:, :]), ALU.add).then_inc(c_x, 1)
                        dve.wait_ge(c_m, g + 1)
                        dve.tensor_tensor(grp(M, g), quad(bank[3][:, :]), grp(DT, g), ALU.mult).then_inc(c_me, 1)
                        if g < CHUNKS - 1:
                            dve.wait_ge(c_g, 2 * g + 4)
                            dve.wait_ge(c_st, g + 1)
                            dve.wait_ge(c_ut, g + 1)
                            dve.tensor_tensor(ST[:, :, :], STg[:, :, :], quad(bank[6][:, :]), ALU.add).then_inc(c_se, 1)
                        dve.wait_ge(c_o, g + 1)
                        if g < CHUNKS - 1:
                            dve.wait_ge(c_s, g + 1)
                            dve.tensor_tensor(S[:, :, :], Sg[:, :, :], quad(bank[7][:, :]), ALU.add).then_inc(c_se, 1)
                        dve.tensor_tensor(grp(GO, g), quad(bank[4][:, :]), grp(gateT, g), ALU.mult).then_inc(c_oe, 1)
                        if g:
                            moments(dve, chain, X, st6, mv, range(4 * g - 4, 4 * g))
                    g = CHUNKS - 1
                    dve.wait_ge(c_out, CHUNKS)
                    dve.tensor_tensor(grp(X, g), grp(X, g), quad(bank[5][:, :]), ALU.add).then_inc(c_x, 1)
                    dve.wait_ge(c_x, CHUNKS)
                    moments(dve, chain, X, st6, mv, range(4 * g, 4 * g + 4))
                    deviations(dve, chain, mv, var, rstd, tmp)
        ab.close()

        kv = KeyValues(top, nc, bank, a, Kq, VW, bout_b)
        if STAGE >= 2:
            route(nc, top, chain, bank, a, 0, X, C, V, wr0, br0, mv, st6, var, rstd, tmp, plan_i, expert_i, slots[0], s_fill, 16 * len(fills), kv)
            experts(nc, top, chain, bank, 0, X, C, (w1a, w2a, b1a, b2a, None, None), expert_i, slots[0], byrow[0], s_ffn0, 64, None, s_out, norm)
        ffn.close()

        if STAGE >= 3:
            with ExitStack() as ctx1:
                s7 = alloc(ctx1)
                u1 = s7("u1", [P, E * F])
                ug = s7("ug", [P, E * F])
                u2 = s7("u2", [P, E * F])
                c1 = s7("c1", [P, E * F])
                cg = s7("cg", [P, E * F])
                c2 = s7("c2", [P, E * D])
                attention(nc, top, chain, bank, a, X, C, V, Kq, VW, wr1, mv, rstd, plan_i, cum, expert_i, start_i, slots[1],
                          [(u1, "w1b"), (ug, "wgb"), (u2, "w2b"), (c1, "b1b"), (cg, "bgb"), (c2, "b2b")], s_ffn1)
                if STAGE >= 4:
                    experts(nc, top, chain, bank, 1, X, C, (u1, u2, c1, c2, ug, cg), expert_i, slots[1], byrow[1], s_ffn1, 96, out, s_out, norm, start_i)

        with ExitStack() as ctx:
            block = ctx.enter_context(nc.Block())

            @block.sync
            def _(sp):
                if STAGE < 4:
                    sp.dma_start(out, X[:, :, :]).then_inc(s_out, 16)
                    sp.wait_ge(s_out, 16)
                sp.wait_ge(s_fill, 16 * len(fills))
                sp.wait_ge(s_ffn0, 64)


def route(nc, top, chain, bank, a, layer, X, C, V, wr, br, mv, st6, var, rstd, tmp, plan_i, expert_i, slots, s_fill, fill_count, kv=None):
    K = layer + 1
    NT = slot_tiles(K)
    ident = C[:, IDENT, :]

    def sem(name):
        return top.enter_context(nc.semaphore(f"r{layer}_{name}"))

    with ExitStack() as ctx:
        def sb(name, shape, dt=F32):
            return ctx.enter_context(nc.sbuf_tensor(f"r{layer}_{name}", shape, dt))

        rows = [sb(f"rows{c}", [P, TILES, ROW]) for c in range(K)]
        xnT = [sb(f"xnT{i}", [P, 512]) for i in range(CHUNKS)]
        lg = sb("lg", [P, TILES, E])
        wk = sb("wk", [P, TILES, E])
        ex = sb("ex", [P, TILES, E])
        mx = sb("mx", [P, TILES])
        sm = sb("sm", [P, TILES])
        one = [sb(f"one{c}", [P, TILES, E]) for c in range(K)]
        both = sb("both", [P, TILES, E]) if K == 2 else one[0]
        tot = sb("tot", [P, E, TILES])
        run = sb("run", [P, E, TILES])
        cnt = sb("cnt", [P, E, TILES])
        ntl = sb("ntl", [P, E])
        end = sb("end", [P, E])
        beg = sb("beg", [P, E])
        base = sb("base", [P, TILES, E])
        pos = sb("pos", [P, TILES])
        ew = sb("ew", [1, NT, E])
        ef = sb("ef", [1, NT])
        s_row, s_tr, s_xT, s_lg, s_ex, s_exd, s_one, s_rank, s_plan, s_sc, s_dup = (
            sem(n) for n in ("row", "tr", "xT", "lg", "ex", "exd", "one", "rank", "plan", "sc", "dup"))
        block = ctx.enter_context(nc.Block())
        LG, WITHIN, TOTAL = bank[4][:, 0:P], bank[5][:, 0:P], bank[6][:, 0:P]

        if kv:
            kv.place(sb)

            @block.sync
            def _(sp):
                kv.sync(sp)

        def te(ap):
            return ap.rearrange("p (a n) -> p a n", n=E)

        @block.vector
        def _(dve):
            if layer:
                deviations(dve, chain, mv, var, rstd, tmp)
            for j in range(TILES):
                dve.tensor_scalar(rows[0][:, j, 0:D], X[:, j, :], mv[:, j, 0:1], rstd[:, j:j + 1],
                                  ALU.subtract, ALU.mult).then_inc(s_row, 1)
            for c in range(K):
                dve.tensor_scalar(rows[c][:, :, DEST:DEST + 1], V[:, V_ROW:V_ROW + TILES].unsqueeze(2),
                                  float(c * TILES * P), None, ALU.add)
            dve.wait_ge(s_lg, 1)
            logits = te(LG)
            if br is not None:
                logits = lg[:, :, :]
                chain.run(dve, dve.tensor_tensor(logits, te(LG), mid_col(br[:, :], TILES), ALU.add))
            chain.run(dve, dve.tensor_reduce(mx[:, :], logits, AX.X, ALU.max))
            dve.tensor_tensor(wk[:, :, :], logits, last_col(mx[:, :], E), ALU.subtract).then_inc(s_ex, 1)
            dve.wait_ge(s_exd, 1)
            chain.run(dve, dve.tensor_reduce(sm[:, :], ex[:, :, :], AX.X, ALU.add))
            chain.run(dve, dve.reciprocal(sm[:, :], sm[:, :]))
            chain.run(dve, dve.tensor_tensor(ex[:, :, :], ex[:, :, :], last_col(sm[:, :], E), ALU.mult))
            for c in range(K):
                chain.run(dve, dve.tensor_reduce(mx[:, :], ex[:, :, :], AX.X, ALU.max))
                dve.tensor_copy(rows[c][:, :, GATE:GATE + 1], mx[:, :].unsqueeze(2))
                chain.run(dve, dve.tensor_tensor(wk[:, :, :], ex[:, :, :], last_col(mx[:, :], E), ALU.is_ge))
                chain.run(dve, dve.tensor_tensor(wk[:, :, :], wk[:, :, :], mid_col(V[:, V_EM8:V_EM8 + E], TILES), ALU.mult))
                chain.run(dve, dve.tensor_reduce(sm[:, :], wk[:, :, :], AX.X, ALU.min))
                chain.run(dve, dve.tensor_tensor(one[c][:, :, :], mid_col(V[:, V_EM8:V_EM8 + E], TILES), last_col(sm[:, :], E),
                                            ALU.is_equal))
                if c < K - 1:
                    chain.run(dve, dve.scalar_tensor_tensor(ex[:, :, :].rearrange("p a n -> p (a n)"),
                                                       one[c][:, :, :].rearrange("p a n -> p (a n)"), -2.0,
                                                       ex[:, :, :].rearrange("p a n -> p (a n)"), ALU.mult, ALU.add))
            if K == 2:
                chain.run(dve, dve.tensor_tensor(both[:, :, :], one[0][:, :, :], one[1][:, :, :], ALU.add))
            dve.sem_inc(s_one, 1)
            dve.wait_ge(s_rank, 1)
            chain.run(dve, dve.tensor_copy(tot[:, :, :], te(TOTAL).rearrange("p a n -> p n a")))
            chain.run(dve, dve.tensor_tensor_scan(run[:, :, :].rearrange("p a n -> p (a n)"), V[:, V_SCAN:V_SCAN + P],
                                             tot[:, :, :].rearrange("p a n -> p (a n)"), 0.0, ALU.mult, ALU.add))
            chain.run(dve, dve.tensor_tensor(cnt[:, :, :], run[:, :, TILES - 1:TILES].broadcast_to([P, E, TILES]),
                                        mid_col(V[:, V_KTH:V_KTH + TILES], E), ALU.is_gt))
            chain.run(dve, dve.tensor_reduce(ntl[:, :], cnt[:, :, :], AX.X, ALU.add))
            chain.run(dve, dve.tensor_tensor_scan(end[:, :], C[:, ONES, 0:E], ntl[:, :], 0.0, ALU.mult, ALU.add))
            chain.run(dve, dve.tensor_tensor(beg[:, :], end[:, :], ntl[:, :], ALU.subtract))
            chain.run(dve, dve.tensor_scalar(beg[:, :], beg[:, :], float(P), None, ALU.mult))
            chain.run(dve, dve.tensor_tensor(run[:, :, :], run[:, :, :], tot[:, :, :], ALU.subtract))
            chain.run(dve, dve.tensor_tensor(run[:, :, :], run[:, :, :], last_col(beg[:, :], TILES), ALU.add))
            chain.run(dve, dve.tensor_tensor(base[:, :, :], te(WITHIN), run[:, :, :].rearrange("p a n -> p n a"), ALU.add))
            for c in range(K):
                chain.run(dve, dve.tensor_tensor(wk[:, :, :], base[:, :, :], one[c][:, :, :], ALU.mult))
                chain.run(dve, dve.tensor_reduce(pos[:, :], wk[:, :, :], AX.X, ALU.add))
                chain.run(dve, dve.tensor_copy(plan_i[:, c * TILES:(c + 1) * TILES], pos[:, :]))
                dve.sem_inc(s_plan, 1)
            chain.run(dve, dve.tensor_tensor(ew[:, :, 0:E - 1], last_col(V[0:1, V_TILE:V_TILE + NT], E - 1),
                                        mid_col(end[0:1, 0:E - 1], NT), ALU.is_ge))
            chain.run(dve, dve.tensor_reduce(ef[:, :], ew[:, :, 0:E - 1], AX.X, ALU.add))
            chain.run(dve, dve.tensor_copy(expert_i[:, 0:NT], ef[:, :]))
            if kv:
                kv.vector(dve)

        @block.tensor
        def _(pe):
            def turn(g):
                pe.wait_ge(s_row, 4 * g + 4)
                for k in range(4):
                    last = pe.transpose(bank[g][:, k * P:(k + 1) * P], rows[0][:, 4 * g + k, 0:D], ident)
                last.then_inc(s_tr, 1)

            def router(g):
                pe.wait_ge(s_xT, g + 1)
                for k in range(4):
                    n = 4 * g + k
                    last = pe.matmul(LG[:, n * E:(n + 1) * E], xnT[g][:, k * P:(k + 1) * P], wr[:, :], start=True, stop=True)
                return last

            turn(0)
            for g in range(CHUNKS):
                if g < CHUNKS - 1:
                    turn(g + 1)
                last = router(g)
            last.then_inc(s_lg, 1)
            pe.wait_ge(s_one, 1)
            pe.matmul(WITHIN, C[:, UP_STRICT, :], both[:, :, :].rearrange("p a n -> p (a n)"), start=True, stop=True)
            pe.matmul(TOTAL, C[:, ONES, :], both[:, :, :].rearrange("p a n -> p (a n)"), start=True, stop=True).then_inc(s_rank, 1)
            if kv:
                kv.tensor(pe)

        @block.scalar
        def _(act):
            for g in range(CHUNKS):
                act.wait_ge(s_tr, g + 1)
                act.activation(xnT[g][:, :], bank[g][:, :], ACT.Copy).then_inc(s_xT, 1)
            act.wait_ge(s_ex, 1)
            act.activation(ex[:, :, :], wk[:, :, :], ACT.Exp).then_inc(s_exd, 1)
            if kv:
                kv.scalar(act)

        @block.gpsimd
        def _(pool):
            if K == 2:
                pool.wait_ge(s_row, TILES)
                pool.tensor_copy(rows[1][:, :, 0:D], rows[0][:, :, 0:D]).then_inc(s_dup, 1)
                pool.wait_ge(s_dup, 1)
            pool.wait_ge(s_fill, fill_count)
            for c in range(K):
                pool.wait_ge(s_plan, c + 1)
                for j in range(TILES):
                    n = c * TILES + j
                    pool.indirect_dma_start(out=slots, out_offset=bass.IndirectOffsetOnAxis(
                        ap=plan_i[:, n:n + 1].bitcast(U32), axis=0), in_=rows[c][:, j, :], in_offset=None).then_inc(s_sc, 16)
            pool.wait_ge(s_sc, 16 * K * TILES)


def experts(nc, top, chain, bank, layer, X, C, weights, expert_i, slots, byrow, s_w, w_count, out, s_out, norm, start_i=None):
    w1, w2, b1, b2, wg, bg = weights
    st6, mv, var, rstd, tmp = norm
    K = layer + 1
    NT = slot_tiles(K)
    gated = wg is not None
    ident = C[:, IDENT, :]

    def sem(name):
        return top.enter_context(nc.semaphore(f"e{layer}_{name}"))

    with ExitStack() as ctx:
        def sb(name, shape, dt=F32):
            return ctx.enter_context(nc.sbuf_tensor(f"e{layer}_{name}", shape, dt))

        xs = [sb(f"xs{i}", [P, ROW]) for i in range(4)]
        xT = [sb(f"xT{i}", [P, P]) for i in range(2)]
        h = [sb(f"h{i}", [P, F]) for i in range(2)]
        hg = [sb(f"hg{i}", [P, F]) for i in range(2)] if gated else None
        hT = [sb(f"hT{i}", [P, F]) for i in range(2)]
        y = [sb(f"y{i}", [P, D]) for i in range(4)]
        dst = sb("dst", [P, NT], I32)
        gate = sb("gate", [P, NT])
        back = sb("back", [P, CHUNKS, K, 4, D])
        s_xs = [sem(f"xs{i}") for i in range(4)]
        s_sc = [sem(f"sc{i}") for i in range(4)]
        s_xt, s_xT, s_h, s_hs, s_t, s_hT, s_y, s_yb, s_yg, s_take, s_bk = (
            sem(n) for n in ("xt", "xT", "h", "hs", "t", "hT", "y", "yb", "yg", "take", "bk"))
        if gated:
            s_g, s_gs, s_ge, s_p = (sem(n) for n in ("g", "gs", "ge", "p"))
        block = ctx.enter_context(nc.Block())
        BX, BH, BG, BT, BY = bank[0], (bank[1], bank[7]), bank[2], bank[3:5], bank[5:7]
        Q = NT // 4

        def tiles(eng, body, weights=None, what=expert_i, most=E - 1):
            regs = [eng.alloc_register(f"expert{layer}_{j}") for j in range(6)] if weights else []

            def fetch(i, lo, n):
                if weights:
                    at = what[0:1, bass.ds(i + lo, n - lo)] if not isinstance(i, int) else what[0:1, i + lo:i + n]
                    eng.load(regs[lo + 1:n + 1], at)
                return [None] * (lo + 1) + [nc.snap(r).with_bounds(min_val=0, max_val=most) for r in regs[lo + 1:n + 1]] + [None] * 8

            e = fetch(0, 0, 5)
            if weights:
                weights(e[1])
            for i in range(4):
                body(i, i, e[i:])
            with eng.Fori(1, Q) as q:
                e = fetch(q * 4, -1, 5)
                for k in range(4):
                    body(q * 4 + k, k, e[k:])
            e = fetch(4 * Q, -1, NT - 4 * Q)
            for i in range(4 * Q, NT):
                body(i, i % 4, e[i % 4:])
            return e[NT % 4]

        def inside(i):
            return not isinstance(i, int) or 0 <= i < NT

        def later(i):
            return not isinstance(i, int) or i >= 4

        @block.sync
        def _(sp):
            def load(i, k, e):
                if later(i):
                    sp.wait_ge(s_xt, i - 3)
                    sp.wait_ge(s_take, i - 3)
                if start_i is not None:
                    src = slots[bass.ds(e[1], P), :]
                else:
                    src = slots[bass.ds(i * P, P), :] if not isinstance(i, int) else slots[i * P:(i + 1) * P, :]
                sp.dma_start(xs[k][:, :], src).then_inc(s_xs[k], 16)

            if start_i is not None:
                tiles(sp, load, lambda e: None, start_i, slots.shape[0] - P)
            else:
                tiles(sp, load)
            for k in range(4):
                sp.wait_ge(s_sc[k], 16 * len(range(k, NT, 4)))
            by_token = byrow.rearrange("(c p j) d -> p c j d", c=K, p=P)
            for g in range(CHUNKS):
                sp.dma_start(back[:, g, :, :, :], by_token[:, :, 4 * g:4 * g + 4, :]).then_inc(s_xs[g], 16)
            if out is not None:
                for g in range(CHUNKS):
                    sp.wait_ge(s_bk, g + 1)
                    sp.dma_start(out[:, 4 * g:4 * g + 4, :], X[:, 4 * g:4 * g + 4, :]).then_inc(s_out, 16)
                sp.wait_ge(s_out, 16 * CHUNKS)

        @block.tensor
        def _(pe):
            def turn(i, k):
                if inside(i):
                    pe.wait_ge(s_xs[k], (i - k) * 4 + 16)
                    pe.wait_ge(s_xT, i + 1)
                    pe.transpose(BX[:, 0:P], xs[k][:, 0:D], ident).then_inc(s_xt, 1)

            def hidden_gate(i, k, e):
                if gated and inside(i):
                    pe.wait_ge(s_xT, i + 2)
                    pe.wait_ge(s_gs, i + 1)
                    pe.matmul(BG[:, :], xT[k % 2][:, :], wg[:, bass.ds(e * F, F)], start=True, stop=True).then_inc(s_g, 1)

            def hidden(i, k, e):
                if inside(i):
                    pe.wait_ge(s_xT, i + 2)
                    pe.wait_ge(s_hs, i + 1)
                    pe.matmul(BH[k % 2][:, :], xT[k % 2][:, :], w1[:, bass.ds(e * F, F)], start=True, stop=True).then_inc(s_h, 1)

            def turn_hidden(i, k):
                src = hg if gated else h
                if gated:
                    pe.wait_ge(s_p, i + 1)
                else:
                    pe.wait_ge(s_hs, i + 3)
                pe.wait_ge(s_hT, i + 1)
                for t in range(FT):
                    last = pe.transpose(BT[k % 2][:, t * P:(t + 1) * P], src[k % 2][:, t * P:(t + 1) * P], ident)
                last.then_inc(s_t, 1)

            def result(i, k, e):
                if inside(i):
                    pe.wait_ge(s_hT, i + 3)
                    pe.wait_ge(s_yb, i + 1)
                    for t in range(FT):
                        last = pe.matmul(BY[k % 2][:, 0:D], hT[k % 2][:, t * P:(t + 1) * P], w2[:, bass.ds(e * F + t * D, D)],
                                         start=(t == 0), stop=(t == FT - 1))
                    last.then_inc(s_y, 1)

            def body(i, k, e):
                if gated:
                    hidden_gate(i + 1, (k + 1) % 4, e[2])
                    turn(i + 2, (k + 2) % 4)
                    result(i - 1, (k - 1) % 4, e[0])
                    turn_hidden(i, k)
                    hidden(i + 1, (k + 1) % 4, e[2])
                else:
                    hidden(i + 1, (k + 1) % 4, e[2])
                    turn(i + 2, (k + 2) % 4)
                    result(i - 1, (k - 1) % 4, e[0])
                    turn_hidden(i, k)

            def first(e):
                turn(0, 0)
                hidden_gate(0, 0, e)
                hidden(0, 0, e)
                turn(1, 1)

            pe.wait_ge(s_w, w_count)
            e = tiles(pe, body, first)
            result(NT - 1, (NT - 1) % 4, e)

        @block.scalar
        def _(act):
            def turned(i, k):
                if inside(i):
                    act.wait_ge(s_xt, i + 1)
                    act.activation(xT[k % 2][:, :], BX[:, 0:P], ACT.Copy).then_inc(s_xT, 1)

            def gelu(i, k):
                if gated and inside(i):
                    act.wait_ge(s_gs, i + 2)
                    act.activation(hg[k % 2][:, :], hg[k % 2][:, :], ACT.Gelu).then_inc(s_ge, 1)

            def body(i, k, _):
                turned(i + 2, (k + 2) % 4)
                gelu(i + 1, (k + 1) % 4)
                act.wait_ge(s_t, i + 1)
                act.activation(hT[k % 2][:, :], BT[k % 2][:, :], ACT.Copy if gated else ACT.Relu).then_inc(s_hT, 1)

            act.sem_inc(s_xT, 1)
            act.sem_inc(s_hT, 2)
            turned(0, 0)
            gelu(0, 0)
            turned(1, 1)
            tiles(act, body)

        @block.vector
        def _(dve):
            def bias_gate(i, k, e):
                if gated and inside(i):
                    dve.wait_ge(s_g, i + 1)
                    dve.tensor_tensor(hg[k % 2][:, :], BG[:, :], bg[:, bass.ds(e * F, F)], ALU.add).then_inc(s_gs, 1)

            def bias(i, k, e):
                if inside(i):
                    dve.wait_ge(s_h, i + 1)
                    dve.tensor_tensor(h[k % 2][:, :], BH[k % 2][:, :], b1[:, bass.ds(e * F, F)], ALU.add).then_inc(s_hs, 1)

            def result(i, k, e):
                if inside(i):
                    if later(i):
                        dve.wait_ge(s_sc[k], (i - k) * 4)
                    dve.wait_ge(s_y, i + 1)
                    dve.tensor_tensor(y[k][:, :], BY[k % 2][:, 0:D], b2[:, bass.ds(e * D, D)], ALU.add).then_inc(s_yb, 1)
                    dve.wait_ge(s_yb, i + 3)
                    dve.wait_ge(s_take, i + 1)
                    g = gate[:, bass.ds(i, 1)] if not isinstance(i, int) else gate[:, i:i + 1]
                    dve.tensor_scalar(y[k][:, :], y[k][:, :], g, None, ALU.mult).then_inc(s_yg, 1)

            def body(i, k, e):
                if gated:
                    dve.wait_ge(s_ge, i + 1)
                    dve.wait_ge(s_hs, i + 3)
                    dve.tensor_tensor(hg[k % 2][:, :], hg[k % 2][:, :], h[k % 2][:, :], ALU.mult).then_inc(s_p, 1)
                    bias_gate(i + 1, (k + 1) % 4, e[2])
                    result(i - 1, (k - 1) % 4, e[0])
                    bias(i + 1, (k + 1) % 4, e[2])
                else:
                    bias(i + 1, (k + 1) % 4, e[2])
                    result(i - 1, (k - 1) % 4, e[0])

            def first(e):
                bias_gate(0, 0, e)
                bias(0, 0, e)

            dve.sem_inc(s_hs, 2)
            if gated:
                dve.sem_inc(s_gs, 1)
            dve.sem_inc(s_yb, 2)
            e = tiles(dve, body, first)
            result(NT - 1, (NT - 1) % 4, e)
            for g in range(CHUNKS):
                dve.wait_ge(s_xs[g], 16 * len(range(g, NT, 4)) + 16)
                xg = X[:, 4 * g:4 * g + 4, :]
                for c in range(K):
                    chain.run(dve, dve.tensor_tensor(xg, xg, back[:, g, c, :, :], ALU.add))
                dve.sem_inc(s_bk, 1)
                if out is None:
                    moments(dve, chain, X, st6, mv, range(4 * g, 4 * g + 4))
            if out is None:
                deviations(dve, chain, mv, var, rstd, tmp)

        @block.gpsimd
        def _(pool):
            def take(i):
                pool.wait_ge(s_xs[i % 4], 16 * (i // 4) + 16)
                pool.tensor_copy(dst[:, i:i + 1], xs[i % 4][:, DEST:DEST + 1])
                pool.tensor_copy(gate[:, i:i + 1], xs[i % 4][:, GATE:GATE + 1]).then_inc(s_take, 1)

            take(0)
            take(1)
            for i in range(NT):
                k = i % 4
                if i + 2 < NT:
                    take(i + 2)
                pool.wait_ge(s_take, i + 1)
                pool.wait_ge(s_yg, i + 1)
                pool.indirect_dma_start(out=byrow, out_offset=bass.IndirectOffsetOnAxis(
                    ap=dst[:, i:i + 1].bitcast(U32), axis=0), in_=y[k][:, :], in_offset=None,
                    bounds_check=K * TILES * P - 1, oob_is_err=False).then_inc(s_sc[k], 16)


def attention(nc, top, chain, bank, a, X, C, V, Kq, VW, wr, mv, rstd, plan_i, cum, expert_i, start_i, slots, ffn_loads, s_ffn1):
    ident = C[:, IDENT, :]

    def sem(name):
        return top.enter_context(nc.semaphore(f"t_{name}"))

    with ExitStack() as ctx:
        def sb(name, shape, dt=F32):
            return ctx.enter_context(nc.sbuf_tensor(f"t_{name}", shape, dt))

        xnT = sb("xnT", [P, TILES * P])
        s_xn, s_tr, s_xT = (sem(n) for n in ("xn", "tr", "xT"))
        with ExitStack() as ctx2:
            def sb2(name, shape, dt=F32):
                return ctx2.enter_context(nc.sbuf_tensor(f"t_{name}", shape, dt))
            xn = [sb2(f"xn{i}", [P, 4, D]) for i in range(2)]
            with nc.Block() as block:
                @block.sync
                def _(sp):
                    for t, name in ffn_loads:
                        src = a[name]
                        if len(src.shape) == 1:
                            src = src.partition_broadcast(P)
                        sp.dma_start(t[:, :], src).then_inc(s_ffn1, 16)

                @block.tensor
                def _(pe):
                    for g in range(CHUNKS):
                        pe.wait_ge(s_xn, g + 1)
                        if g >= 2:
                            pe.wait_ge(s_xT, g - 1)
                        for k in range(4):
                            last = pe.transpose(bank[4 + g % 2][:, k * P:(k + 1) * P], xn[g % 2][:, k, :], ident)
                        last.then_inc(s_tr, 1)

                @block.scalar
                def _(act):
                    for g in range(CHUNKS):
                        act.wait_ge(s_tr, g + 1)
                        act.activation(xnT[:, g * 512:(g + 1) * 512], bank[4 + g % 2][:, :], ACT.Copy).then_inc(s_xT, 1)

                def norm4(dve, g):
                    for k in range(4):
                        j = 4 * g + k
                        last = dve.tensor_scalar(xn[g % 2][:, k, :], X[:, j, :], mv[:, j, 0:1], rstd[:, j:j + 1],
                                                 ALU.subtract, ALU.mult)
                    last.then_inc(s_xn, 1)

                @block.vector
                def _(dve):
                    for g in range(2):
                        norm4(dve, g)
                    for g in range(2, 4):
                        dve.wait_ge(s_tr, g - 1)
                        norm4(dve, g)

        xq = [sb(f"xq{i}", [P, P]) for i in range(2)]
        Pr = [sb(f"Pr{i}", [P, KEYS]) for i in range(2)]
        PT = [sb(f"PT{i}", [P, KEYS]) for i in range(2)]
        nmx = sb("nmx", [P, 16])
        den = sb("den", [P, 16])
        rec = sb("rec", [P, 16])
        s_mo = sem("mo")
        s_q, s_s, s_m, s_e, s_t, s_pt, s_o, s_rc, s_acc = (
            sem(n) for n in ("q", "s", "m", "e", "t", "pt", "o", "rc", "acc"))
        UN = 2 * HEADS
        PAIRS_N = TILES // 2
        BS, BT, BO, BR = bank[0:4], bank[4:6], bank[6], bank[7]
        x1 = sb("x1", [P, D])
        pad = sb("pad", [P, 2])
        st1 = sb("st1", [P, 6])
        mv2 = sb("mv2", [P, 2, 2])
        var2, rs2, tmp2, mx2, sm2, pos2 = (sb(n, [P, 2]) for n in ("var2", "rs2", "tmp2", "mx2", "sm2", "pos2"))
        rows = [[sb(f"rows{c}{h}", [P, ROW]) for h in range(2)] for c in range(2)]
        last_rows = [[sb(f"last{c}{h}", [P, ROW]) for h in range(2)] for c in range(2)]
        xT2 = sb("xT2", [P, 2 * P])
        wk2, ex2, both2, base2 = (sb(n, [P, 2, E]) for n in ("wk2", "ex2", "both2", "base2"))
        pair2 = sb("pair2", [P, E])
        one2 = [sb(f"one2{c}", [P, 2, E]) for c in range(2)]
        s_rx, s_rt, s_rxT, s_rl, s_rs, s_rex, s_rone, s_rr, s_plan, s_dup, s_free, s_sc, s_link, s_cum = (
            sem(n) for n in ("rx", "rt", "rxT", "rl", "rs", "rex", "rone", "rr", "plan", "dup", "free", "sc", "link", "cum"))
        LOGITS, WITHIN, TOTAL = BR[:, 256:256 + 2 * E], BR[:, 288:288 + 2 * E], BR[:, 320:320 + E]

        def pe2(ap):
            return ap.rearrange("p (a n) -> p a n", n=E)

        def at(i, n=1):
            return bass.ds(i, n) if not isinstance(i, int) else slice(i, i + n)

        def each_pair(eng, body):
            body(0, None)
            with eng.Fori(1, PAIRS_N) as tt:
                body(tt, tt - 1)

        NT = slot_tiles(2)
        num, ntl, end, skip = (sb(n, [1, E]) for n in ("num", "ntl", "end", "skip"))
        cnt = sb("cnt", [1, E, TILES])
        ew = sb("ew", [1, NT, E - 1])
        ef = sb("ef", [1, NT])

        def slot_table(dve):
            chain.run(dve, dve.scalar_tensor_tensor(num[:, :], V[0:1, V_EM8:V_EM8 + E], -float(REGION), cum[0:1, :], ALU.mult, ALU.add))
            chain.run(dve, dve.tensor_scalar(num[:, :], num[:, :], -float(E * REGION), None, ALU.add))
            chain.run(dve, dve.tensor_tensor(cnt[:, :, :], last_col(num[:, :], TILES), mid_col(V[0:1, V_KTH:V_KTH + TILES], E), ALU.is_gt))
            chain.run(dve, dve.tensor_reduce(ntl[:, :], cnt[:, :, :], AX.X, ALU.add))
            chain.run(dve, dve.tensor_tensor_scan(end[:, :], C[0:1, ONES, 0:E], ntl[:, :], 0.0, ALU.mult, ALU.add))
            chain.run(dve, dve.tensor_tensor(ew[:, :, :], last_col(V[0:1, V_TILE:V_TILE + NT], E - 1), mid_col(end[:, 0:E - 1], NT), ALU.is_ge))
            chain.run(dve, dve.tensor_reduce(ef[:, :], ew[:, :, :], AX.X, ALU.add))
            chain.run(dve, dve.tensor_copy(expert_i[:, 0:NT], ef[:, :]))
            chain.run(dve, dve.tensor_scalar(skip[:, :], ntl[:, :], -float(P), float(REGION), ALU.mult, ALU.add))
            chain.run(dve, dve.tensor_tensor(ew[:, :, :], ew[:, :, :], mid_col(skip[:, 0:E - 1], NT), ALU.mult))
            chain.run(dve, dve.tensor_reduce(ef[:, :], ew[:, :, :], AX.X, ALU.add))
            chain.run(dve, dve.scalar_tensor_tensor(ef[:, :], V[0:1, V_TILE:V_TILE + NT], float(P), ef[:, :], ALU.mult, ALU.add))
            chain.run(dve, dve.tensor_copy(start_i[:, 0:NT], ef[:, :]))

        with nc.Block() as block:
            @block.gpsimd
            def _(pool):
                def query(t, scored):
                    if scored:
                        pool.wait_ge(s_s, scored)
                    pool.tensor_copy(xq[t % 2][:, :], xnT[:, t % TILES * P:(t % TILES + 1) * P]).then_inc(s_q, 1)

                def send(r, rows):
                    pool.wait_ge(s_rx, r + 1)
                    for h in range(2):
                        pool.tensor_copy(rows[1][h][:, 0:D], rows[0][h][:, 0:D]).then_inc(s_dup, 1)
                    pool.wait_ge(s_dup, 2 * r + 2)
                    pool.wait_ge(s_plan, r + 1)
                    for c in range(2):
                        for h in range(2):
                            n = c * TILES + 2 * r + h
                            pool.indirect_dma_start(out=slots, out_offset=bass.IndirectOffsetOnAxis(
                                ap=plan_i[:, n:n + 1].bitcast(U32), axis=0), in_=rows[c][h][:, :], in_offset=None).then_inc(s_sc, 16)

                pool.sem_inc(s_free, 1)
                query(0, 0)
                for tt in range(PAIRS_N):
                    query(2 * tt + 1, 16 * tt + 1 if tt else 0)
                    if tt >= 2:
                        pool.wait_ge(s_sc, 64 * (tt - 1))
                        pool.sem_inc(s_free, 1)
                    query(2 * tt + 2, 16 * tt + HEADS + 1)
                    if tt:
                        send(tt - 1, rows)
                send(PAIRS_N - 1, last_rows)
                pool.wait_ge(s_sc, 64 * PAIRS_N)

            @block.tensor
            def _(pe):
                def score(n, u):
                    pe.wait_ge(s_e, n + 1)
                    hd = u % HEADS
                    pe.matmul(BS[u % 4][:, :], xq[u // HEADS][:, :], Kq[:, hd, :], start=True, stop=True).then_inc(s_s, 1)

                def turn(r, rows):
                    pe.wait_ge(s_rx, r + 1)
                    for h in range(2):
                        last = pe.transpose(BR[:, h * P:(h + 1) * P], rows[0][h][:, 0:D], ident)
                    last.then_inc(s_rt, 1)

                def router(r):
                    pe.wait_ge(s_rxT, r + 1)
                    for h in range(2):
                        last = pe.matmul(LOGITS[:, h * E:(h + 1) * E], xT2[:, h * P:(h + 1) * P], wr[:, :], start=True, stop=True)
                    last.then_inc(s_rl, 1)

                def rank(r):
                    pe.wait_ge(s_rone, r + 1)
                    up, ones = C[:, UP_STRICT, :], C[:, ONES, :]
                    pe.matmul(WITHIN, up, both2[:, :, :].rearrange("p a n -> p (a n)"), start=True, stop=False)
                    pe.matmul(WITHIN[:, E:2 * E], ones, both2[:, 0, :], start=False, stop=True)
                    pe.matmul(TOTAL, ones, pair2[:, :], start=True, stop=True).then_inc(s_rr, 1)

                def body(tt, r):
                    for u in range(UN):
                        n = tt * UN + u
                        nx = u + 2
                        if nx == HEADS:
                            pe.wait_ge(s_q, tt * 2 + 2)
                        if nx == UN:
                            pe.wait_ge(s_q, tt * 2 + 3)
                        pe.wait_ge(s_e, n + 5)
                        pe.wait_ge(s_pt, n + 1)
                        for t in range(KT_N):
                            last = pe.transpose(BT[u % 2][:, t * P:(t + 1) * P], Pr[u % 2][:, t * P:(t + 1) * P], ident)
                        last.then_inc(s_t, 1)
                        score(n + 2, nx % UN)
                        if r is not None and u == 5:
                            turn(r, rows)
                        if r is not None and u == 7:
                            router(r)
                        if r is not None and u == 14:
                            rank(r)
                        pe.wait_ge(s_pt, n + 3)
                        pe.wait_ge(s_acc, n + 2)
                        for t in range(KT_N):
                            last = pe.matmul(BO[:, 0:D], PT[u % 2][:, t * P:(t + 1) * P], VW[:, u % HEADS, t, :],
                                             start=(t == 0), stop=(t == KT_N - 1))
                        last.then_inc(s_o, 1)

                pe.wait_ge(s_q, 1)
                score(0, 0)
                score(1, 1)
                each_pair(pe, body)
                r = PAIRS_N - 1
                turn(r, last_rows)
                router(r)
                rank(r)

            @block.scalar
            def _(act):
                def exps(n, u):
                    act.wait_ge(s_m, n + 1)
                    act.activation(Pr[u % 2][:, :], BS[u % 4][:, :], ACT.Exp, bias=nmx[:, u:u + 1],
                                   accum_out=den[:, u:u + 1]).then_inc(s_e, 1)

                act.sem_inc(s_e, 4)
                act.sem_inc(s_pt, 2)
                exps(0, 0)

                def turned(r):
                    act.wait_ge(s_rt, r + 1)
                    act.activation(xT2[:, :], BR[:, 0:2 * P], ACT.Copy).then_inc(s_rxT, 1)

                def softmax(r):
                    act.wait_ge(s_rs, r + 1)
                    act.activation(ex2[:, :, :], wk2[:, :, :], ACT.Exp).then_inc(s_rex, 1)

                def body(tt, r):
                    for u in range(UN):
                        n = tt * UN + u
                        act.wait_ge(s_t, n + 1)
                        act.activation(PT[u % 2][:, :], BT[u % 2][:, :], ACT.Copy).then_inc(s_pt, 1)
                        exps(n + 1, (u + 1) % UN)
                        if r is not None and u == 5:
                            turned(r)
                        if r is not None and u == 9:
                            softmax(r)

                each_pair(act, body)
                turned(PAIRS_N - 1)
                softmax(PAIRS_N - 1)

            @block.vector
            def _(dve):
                def top(n, u):
                    dve.wait_ge(s_s, n + 1)
                    dve.tensor_reduce(nmx[:, u:u + 1], BS[u % 4][:, :], AX.X, ALU.max, negate=True).then_inc(s_m, 1)

                count = 0

                def link(r, ins):
                    nonlocal count
                    count += 1
                    ins.then_inc(s_link, 1)
                    dve.wait_ge(s_link, r * LINKS + count)

                def moments_of(j, half, n):
                    dve.wait_ge(s_acc, n + 3)
                    dve.tensor_scalar(x1[:, :], X[:, at(j), :].rearrange("p a n -> p (a n)"), 1.0, None, ALU.mult).then_inc(s_mo, 1)
                    dve.wait_ge(s_mo, j * 3 + 1)
                    dve.tensor_scalar(pad[:, 0:1], ident[:, 0:1], 1.0, None, ALU.mult)
                    dve.bn_stats(st1[:, :], x1[:, :]).then_inc(s_mo, 1)
                    dve.wait_ge(s_mo, j * 3 + 2)
                    dve.tensor_scalar(pad[:, 1:2], ident[:, 0:1], 1.0, None, ALU.mult)
                    dve.bn_aggr(mv2[:, half, :], st1[:, :]).then_inc(s_mo, 1)

                def seed(r):
                    dve.wait_ge(s_mo, r * 6 + 6)
                    link(r, dve.tensor_scalar(var2[:, :], mv2[:, :, 1], EPS, None, ALU.add))
                    link(r, dve.tensor_scalar(rs2[:, :].bitcast(I32), var2[:, :].bitcast(I32), 1, None, ALU.logical_shift_right))
                    link(r, dve.tensor_scalar(rs2[:, :].bitcast(I32), rs2[:, :].bitcast(I32), -1.0, float(0x5F3759DF), ALU.mult, ALU.add))

                def newton(r):
                    link(r, dve.tensor_tensor(tmp2[:, :], rs2[:, :], rs2[:, :], ALU.mult))
                    link(r, dve.scalar_tensor_tensor(tmp2[:, :], tmp2[:, :], -0.5, var2[:, :], ALU.mult, ALU.mult))
                    link(r, dve.scalar_tensor_tensor(rs2[:, :], tmp2[:, :], 1.5, rs2[:, :], ALU.add, ALU.mult))

                def normalize(r, rows):
                    for h in range(2):
                        xj = X[:, at(r * 2 + h), :].rearrange("p a n -> p (a n)")
                        last = dve.tensor_scalar(rows[0][h][:, 0:D], xj, mv2[:, h, 0:1], rs2[:, h:h + 1], ALU.subtract, ALU.mult)
                    last.then_inc(s_rx, 1)
                    for c in range(2):
                        for h in range(2):
                            last = dve.tensor_scalar(rows[c][h][:, DEST:DEST + 1], V[:, at(r * 2 + (V_ROW + h))],
                                                     float(c * TILES * P), None, ALU.add)
                    link(r, last)

                def shift(r):
                    dve.wait_ge(s_rl, r + 1)
                    link(r, dve.tensor_reduce(mx2[:, :], pe2(LOGITS), AX.X, ALU.max))
                    dve.tensor_tensor(wk2[:, :, :], pe2(LOGITS), last_col(mx2[:, :], E), ALU.subtract).then_inc(s_rs, 1)

                def divide(r):
                    dve.wait_ge(s_rex, r + 1)
                    link(r, dve.tensor_reduce(sm2[:, :], ex2[:, :, :], AX.X, ALU.add))
                    link(r, dve.reciprocal(sm2[:, :], sm2[:, :]))
                    link(r, dve.tensor_tensor(ex2[:, :, :], ex2[:, :, :], last_col(sm2[:, :], E), ALU.mult))

                def choose(r, c, rows):
                    link(r, dve.tensor_reduce(mx2[:, :], ex2[:, :, :], AX.X, ALU.max))
                    for h in range(2):
                        dve.tensor_scalar(rows[c][h][:, GATE:GATE + 1], mx2[:, h:h + 1], 1.0, None, ALU.mult)
                    link(r, dve.tensor_tensor(wk2[:, :, :], ex2[:, :, :], last_col(mx2[:, :], E), ALU.is_ge))
                    link(r, dve.tensor_tensor(wk2[:, :, :], wk2[:, :, :], mid_col(V[:, V_EM8:V_EM8 + E], 2), ALU.mult))
                    link(r, dve.tensor_reduce(sm2[:, :], wk2[:, :, :], AX.X, ALU.min))
                    link(r, dve.tensor_tensor(one2[c][:, :, :], mid_col(V[:, V_EM8:V_EM8 + E], 2), last_col(sm2[:, :], E), ALU.is_equal))
                    if c == 0:
                        link(r, dve.scalar_tensor_tensor(ex2[:, :, :].rearrange("p a n -> p (a n)"),
                                                         one2[0][:, :, :].rearrange("p a n -> p (a n)"), -2.0,
                                                         ex2[:, :, :].rearrange("p a n -> p (a n)"), ALU.mult, ALU.add))
                    else:
                        link(r, dve.tensor_tensor(both2[:, :, :], one2[0][:, :, :], one2[1][:, :, :], ALU.add))
                        dve.tensor_tensor(pair2[:, :], both2[:, 0, :], both2[:, 1, :], ALU.add).then_inc(s_rone, 1)

                def place(r):
                    dve.wait_ge(s_rr, r + 1)
                    link(r, dve.tensor_tensor(base2[:, :, :], pe2(WITHIN), mid_col(cum[:, :], 2), ALU.add))
                    link(r, dve.tensor_tensor(cum[:, :], cum[:, :], TOTAL, ALU.add))
                    for c in range(2):
                        link(r, dve.tensor_tensor(wk2[:, :, :], base2[:, :, :], one2[c][:, :, :], ALU.mult))
                        link(r, dve.tensor_reduce(pos2[:, :], wk2[:, :, :], AX.X, ALU.add))
                        last = dve.tensor_scalar(plan_i[:, at(r * 2 + c * TILES, 2)], pos2[:, :], 1.0, None, ALU.mult)
                    last.then_inc(s_plan, 1)

                def body(tt, r):
                    nonlocal count
                    count = 0
                    for u in range(UN):
                        n = tt * UN + u
                        top(n + 2, (u + 2) % UN)
                        dve.wait_ge(s_e, n + 5)
                        dve.reciprocal(rec[:, u:u + 1], den[:, u:u + 1]).then_inc(s_rc, 1)
                        dve.wait_ge(s_rc, n + 1)
                        dve.wait_ge(s_o, n + 1)
                        j = tt * 2 + u // HEADS
                        xj = X[:, at(j), :].rearrange("p a n -> p (a n)")
                        dve.wait_ge(s_acc, n + 2)
                        dve.scalar_tensor_tensor(xj, BO[:, 0:D], rec[:, u:u + 1], xj, ALU.mult, ALU.add).then_inc(s_acc, 1)
                        if r is not None:
                            if u == 0:
                                seed(r)
                            if u in (1, 2, 3):
                                newton(r)
                            if u == 4:
                                dve.wait_ge(s_free, r + 1)
                                normalize(r, rows)
                            if u == 8:
                                shift(r)
                            if u == 10:
                                divide(r)
                            if u in (11, 12):
                                choose(r, u - 11, rows)
                            if u == 14:
                                place(r)
                        if u % HEADS == HEADS - 1:
                            moments_of(j, u // HEADS, n)

                dve.sem_inc(s_acc, 2)
                dve.tensor_scalar(cum[:, :], V[:, V_EM8:V_EM8 + E], float(E), float(REGION), ALU.add, ALU.mult).then_inc(s_cum, 1)
                dve.wait_ge(s_cum, 1)
                top(0, 0)
                top(1, 1)
                each_pair(dve, body)
                assert count == LINKS
                r, count = PAIRS_N - 1, 0
                seed(r)
                for _ in range(3):
                    newton(r)
                normalize(r, last_rows)
                shift(r)
                divide(r)
                choose(r, 0, last_rows)
                choose(r, 1, last_rows)
                place(r)
                slot_table(dve)


def kernel(**inp):
    import numpy as np
    import concourse.bacc as bacc
    from concourse import mybir as mb
    from concourse.bass_utils import run_bass_kernel_spmd as run

    g = {k: np.asarray(v) for k, v in inp.items()}
    f = np.float32
    r, c = np.arange(P)[:, None], np.arange(P)[None, :]
    planes = [r == c, r <= c, r > c, r < c, np.ones((P, P))]
    for lv in range(LEVELS):
        m = 1 << lv
        planes.append((r // (2 * m) == c // (2 * m)) & ((r // m) % 2 == 0) & ((c // m) % 2 == 1))
    vecs = np.zeros((P, V_END), f)
    vecs[:, V_EM8:V_EM8 + E] = np.arange(E) - E
    vecs[:, V_KTH:V_KTH + TILES] = P * np.arange(TILES)
    vecs[:, V_TILE:V_TILE + 40] = np.arange(40)
    vecs[:, V_ROW:V_ROW + TILES] = r * TILES + np.arange(TILES)
    vecs[:, V_SCAN:V_SCAN + P] = np.arange(P) % TILES != 0

    def pick(*names):
        return [g["L0_attn_" + n] for n in names]

    ex0, ex1 = g["L0_ffn_W1"], g["L1_ffn_w1_w"]
    arrays = {
        "x": g["L0_attn_x"].reshape(SEQS, CHUNKS, P, D).transpose(2, 1, 0, 3).reshape(P, TILES, D),
        "consts": np.stack(planes, 1).astype(f),
        "vecs": vecs,
        "wcat": np.concatenate(pick("Wk", "Wv", "Wq", "Wg"), 1),
        "bcat": np.concatenate(pick("bk", "bv", "bq", "bg")),
        "wab": np.concatenate(pick("Wa", "Wb"), 1),
        "bab": np.concatenate(pick("ba", "bb")),
        "wo": g["L0_attn_Wo"], "bo": g["L0_attn_bo"], "bout": g["L1_attn_bout"],
        "wr0": g["L0_ffn_Wr"], "br0": g["L0_ffn_br"], "wr1": g["L1_ffn_router_w"].T,
        "w1a": g["L0_ffn_W1"].transpose(1, 0, 2).reshape(D, E * F),
        "b1a": g["L0_ffn_b1"].reshape(-1),
        "w2a": g["L0_ffn_W2"].reshape(E, FT, P, D).transpose(2, 0, 1, 3).reshape(P, E * F),
        "b2a": g["L0_ffn_b2"].reshape(-1),
        "ctxT": g["L1_attn_context"].reshape(KEYS, CTX).T,
        "wk": g["L1_attn_Wk"], "wv": g["L1_attn_Wv"],
        "wqT": g["L1_attn_Wq"].reshape(D, HEADS, P).transpose(2, 1, 0),
        "wout": g["L1_attn_Wout"].reshape(HEADS, P, D).transpose(1, 0, 2),
        "w1b": g["L1_ffn_w1_w"].transpose(2, 0, 1).reshape(D, E * F),
        "wgb": g["L1_ffn_wg_w"].transpose(2, 0, 1).reshape(D, E * F),
        "w2b": g["L1_ffn_w2_w"].reshape(E, D, FT, P).transpose(3, 0, 2, 1).reshape(P, E * F),
        "b1b": g["L1_ffn_w1_b"].reshape(-1), "bgb": g["L1_ffn_wg_b"].reshape(-1), "b2b": g["L1_ffn_w2_b"].reshape(-1),
    }
    nc = bacc.Bacc("TRN2", target_bir_lowering=False, num_devices=1)
    feeds, aps = {}, {}
    for name, arr in arrays.items():
        arr = np.ascontiguousarray(arr)
        feeds[f"in_{name}"] = arr
        aps[name] = nc.dram_tensor(f"in_{name}", arr.shape, mb.dt.from_np(arr.dtype), kind="ExternalInput").ap()
    out = nc.dram_tensor("out_0", (P, TILES, D), F32, kind="ExternalOutput").ap()
    build(nc, aps, out)
    res = run(nc, [feeds], core_ids=[0]).results[0]["out_0"]
    return res.reshape(P, CHUNKS, SEQS, D).transpose(2, 1, 0, 3).reshape(SEQS, CHUNKS * P, D)
```

```python
from contextlib import ExitStack

import concourse.bass as bass
from concourse import mybir

F32 = mybir.dt.float32
I32 = mybir.dt.int32
U32 = mybir.dt.uint32
ALU = mybir.AluOpType
ACT = mybir.ActivationFunctionType
AX = mybir.AxisListType

P = 128
SEQS, CHUNKS = 4, 4
TILES = SEQS * CHUNKS
D = 128
E = 8
F = 512
FT = F // P
HEADS = 8
KEYS = 512
KT_N = KEYS // P
CTX = 96
LEVELS = 7
ROW = 130
DEST, GATE = 128, 129
FAR = 1.0e6
SIM_SCALE = 128 ** -0.5
MATRIX_SCALE = 1.5
EPS = 1e-5
IDENT, TRI_INC, LOW_STRICT, UP_STRICT, ONES, PAIRS = 0, 1, 2, 3, 4, 5
V_EM8, V_KTH, V_TILE, V_ROW, V_SCAN, V_END = 0, 8, 24, 64, 80, 208
REGION = TILES * P
NORMS = ((0, 2), (2, 4), (4, 8), (8, 12), (12, 16))
LINKS = 12 + 1 + 1 + 3 + 6 + 6 + 4


def slot_tiles(choices):
    return choices * TILES + E - 1


def last_col(ap, n):
    return ap.unsqueeze(2).broadcast_to([ap.shape[0], ap.shape[1], n])


def mid_col(ap, n):
    return ap.unsqueeze(1).broadcast_to([ap.shape[0], n, ap.shape[1]])


class Chain:

    def __init__(self, sem):
        self.sem, self.n = sem, 0

    def run(self, eng, ins):
        self.n += 1
        ins.then_inc(self.sem, 1)
        eng.wait_ge(self.sem, self.n)


def rsqrt_seed(dve, chain, v, y):
    chain.run(dve, dve.tensor_scalar(y.bitcast(I32), v.bitcast(I32), 1, None, ALU.logical_shift_right))
    chain.run(dve, dve.tensor_scalar(y.bitcast(I32), y.bitcast(I32), -1.0, float(0x5F3759DF), ALU.mult, ALU.add))


def rsqrt_step(dve, chain, v, y, t):
    chain.run(dve, dve.tensor_tensor(t, y, y, ALU.mult))
    chain.run(dve, dve.scalar_tensor_tensor(t, t, -0.5, v, ALU.mult, ALU.mult))
    chain.run(dve, dve.scalar_tensor_tensor(y, t, 1.5, y, ALU.add, ALU.mult))


def rsqrt(dve, chain, v, y, t):
    rsqrt_seed(dve, chain, v, y)
    for _ in range(3):
        rsqrt_step(dve, chain, v, y, t)


def moments(dve, chain, X, st6, mv, tiles):
    for j in tiles:
        last = dve.bn_stats(st6[:, j, :], X[:, j, :])
    chain.run(dve, last)
    for j in tiles:
        last = dve.bn_aggr(mv[:, j, :], st6[:, j, :])
    chain.run(dve, last)


def deviations(dve, chain, mv, var, rstd, tmp):
    chain.run(dve, dve.tensor_scalar(var[:, :], mv[:, :, 1], EPS, None, ALU.add))
    rsqrt(dve, chain, var[:, :], rstd[:, :], tmp[:, :])


class KeyValues:

    def __init__(self, top, nc, bank, a, Kq, VW, bout_b):
        self.bout_b = bout_b
        self.bank, self.a, self.Kq, self.VW = bank, a, Kq, VW
        self.s_w, self.s_kt, self.s_kte, self.s_vt, self.s_vte, self.s_kq, self.s_vw, self.s_vwe, self.s_mean, self.s_bq = (
            top.enter_context(nc.semaphore(f"kv_{n}"))
            for n in ("w", "kt", "kte", "vt", "vte", "kq", "vw", "vwe", "mean", "bq"))

    def place(self, sb):
        self.cT = sb("kv_cT", [CTX, KEYS])
        self.wk = sb("kv_wk", [CTX, HEADS * P])
        self.wv = sb("kv_wv", [CTX, HEADS * P])
        self.wqT = sb("kv_wqT", [P, HEADS, P])
        self.wout = sb("kv_wout", [P, HEADS, P])

    def place_products(self, sb):
        self.KTh = [sb(f"kv_KTh{i}", [P, KEYS]) for i in range(2)]
        self.VTh = [sb(f"kv_VTh{i}", [P, KEYS]) for i in range(2)]
        self.ksum = sb("kv_ksum", [P, HEADS])

    def sync(self, sp):
        for t, name in ((self.cT, "ctxT"), (self.wk, "wk"), (self.wqT, "wqT"), (self.wv, "wv"), (self.wout, "wout")):
            sp.dma_start(t[:], self.a[name]).then_inc(self.s_w, 16)

    def tensor(self, pe, lo, hi):
        bank = self.bank
        if lo == 0:
            pe.wait_ge(self.s_w, 16 * 5)

        def spread(hd):
            if hd:
                pe.wait_ge(self.s_kte, hd)
            pe.matmul(bank[0][:, :], self.wk[:, hd * P:(hd + 1) * P], self.cT[:, :], start=True, stop=True).then_inc(self.s_kt, 1)
            if hd:
                pe.wait_ge(self.s_vte, hd)
            pe.matmul(bank[1][:, :], self.wv[:, hd * P:(hd + 1) * P], self.cT[:, :], start=True, stop=True).then_inc(self.s_vt, 1)

        spread(lo)
        for hd in range(lo, hi):
            if hd < hi - 1:
                spread(hd + 1)
            if hd:
                pe.wait_ge(self.s_bq, hd)
            pe.wait_ge(self.s_kte, hd + 1)
            pe.matmul(bank[2][:, :], self.wqT[:, hd, :], self.KTh[hd % 2][:, :], start=True, stop=True).then_inc(self.s_kq, 1)
            if hd:
                pe.wait_ge(self.s_vwe, hd)
            pe.wait_ge(self.s_vte, hd + 1)
            for t in range(KT_N):
                last = pe.matmul(bank[3][:, t * P:(t + 1) * P], self.VTh[hd % 2][:, t * P:(t + 1) * P], self.wout[:, hd, :],
                                 start=True, stop=True)
            last.then_inc(self.s_vw, 1)

    def scalar(self, act, lo, hi):
        bank = self.bank

        def spread(hd):
            act.wait_ge(self.s_kt, hd + 1)
            if hd >= 2:
                act.wait_ge(self.s_kq, hd - 1)
            act.activation(self.KTh[hd % 2][:, :], bank[0][:, :], ACT.Copy).then_inc(self.s_kte, 1)
            act.wait_ge(self.s_vt, hd + 1)
            if hd >= 2:
                act.wait_ge(self.s_vw, hd - 1)
            act.activation(self.VTh[hd % 2][:, :], bank[1][:, :], ACT.Copy).then_inc(self.s_vte, 1)

        spread(lo)
        for hd in range(lo, hi):
            if hd < hi - 1:
                spread(hd + 1)
            act.wait_ge(self.s_kq, hd + 1)
            act.activation(self.Kq[:, hd, :], bank[2][:, :], ACT.Copy, accum_out=self.ksum[:, hd:hd + 1]).then_inc(self.s_bq, 1)
            act.wait_ge(self.s_vw, hd + 1)
            act.activation(self.VW[:, hd, :, :].rearrange("p a n -> p (a n)"), bank[3][:, :], ACT.Copy).then_inc(self.s_vwe, 1)

    def vector(self, dve):
        ksum = self.ksum
        dve.wait_ge(self.s_vwe, 1)
        dve.tensor_tensor(self.VW[:, 0, :, :], self.VW[:, 0, :, :], mid_col(self.bout_b[:, :], KT_N), ALU.add)
        for hd in range(HEADS):
            dve.wait_ge(self.s_bq, hd + 1)
            dve.tensor_scalar(ksum[:, hd:hd + 1], ksum[:, hd:hd + 1], SIM_SCALE * (1.0 - MATRIX_SCALE) / KEYS,
                              None, ALU.mult).then_inc(self.s_mean, 1)
            dve.wait_ge(self.s_mean, hd + 1)
            dve.tensor_scalar(self.Kq[:, hd, :], self.Kq[:, hd, :], SIM_SCALE * MATRIX_SCALE, ksum[:, hd:hd + 1],
                              ALU.mult, ALU.add)


def build(nc, a, out):
    with ExitStack() as top:
        def alloc(ctx):
            return lambda name, shape, dt=F32: ctx.enter_context(nc.sbuf_tensor(name, shape, dt))

        def sem(name):
            return top.enter_context(nc.semaphore(name))

        sb = alloc(top)
        bank = [top.enter_context(nc.psum_tensor(f"bank{i}", [P, 512], F32)) for i in range(8)]

        def quad(ap):
            return ap.rearrange("p (a n) -> p a n", a=4)

        X = sb("X", [P, TILES, D])
        C = sb("C", [P, 5 + LEVELS, P])
        V = sb("V", [P, V_END])
        ident = C[:, IDENT, :]
        mv = sb("mv", [P, TILES, 2])
        st6 = sb("st6", [P, TILES, 6])
        var = sb("var", [P, TILES])
        rstd = sb("rstd", [P, TILES])
        tmp = sb("tmp", [P, TILES])
        bo_b = sb("bo_b", [P, D])
        bout_b = sb("bout_b", [P, D])
        wr0 = sb("wr0", [P, E])
        br0 = sb("br0", [P, E])
        wr1 = sb("wr1", [P, E])
        fill = sb("fill", [P, ROW])
        plan_i = sb("plan_i", [P, TILES * 2], I32)
        expert_i = sb("expert_i", [1, 40], I32)
        start_i = sb("start_i", [1, 40], I32)
        cum = sb("cum", [P, E])

        wide = sb("wide", [P, 2 * HEADS * KEYS])
        kvqg = wide[:, :].rearrange("p (t c n) -> p t c n", t=TILES, c=4)
        Kq = wide[:, 0:HEADS * KEYS].rearrange("p (h k) -> p h k", h=HEADS)
        VW = wide[:, HEADS * KEYS:2 * HEADS * KEYS].rearrange("p (h t d) -> p h t d", h=HEADS, t=KT_N)

        slots = [nc.dram_tensor(f"slots{n}", [rows, ROW], F32, kind="Internal").ap()
                 for n, rows in enumerate((slot_tiles(1) * P, (E - 1) * REGION + slot_tiles(2) * P))]
        fills = [(n, r, min(r + 16 * P, slots[n].shape[0])) for n in range(2) for r in range(0, slots[n].shape[0], 16 * P)]
        byrow = [nc.dram_tensor(f"byrow{n}", [(n + 1) * TILES * P, D], F32, kind="Internal").ap()
                 for n in range(2)]

        chain = Chain(sem("s_chain"))
        s_x = sem("s_x")
        s_const = sem("s_const")
        s_w0 = sem("s_w0")
        s_ffn0 = sem("s_ffn0")
        s_fillz = sem("s_fillz")
        s_fill = sem("s_fill")
        s_attnw = sem("s_attnw")
        s_ffn1 = sem("s_ffn1")

        s_out = sem("s_out")
        norm = (st6, mv, var, rstd, tmp)

        kvx = ExitStack()
        keyvals = KeyValues(top, nc, bank, a, Kq, VW, bout_b)
        keyvals.place(alloc(kvx))

        ab = ExitStack()
        sa = alloc(ab)
        dec = sa("dec", [P, 3, TILES])
        beta = sa("beta", [P, TILES])
        la = sa("la", [P, TILES])
        rn = sa("rn", [P, TILES])
        bd = sa("bd", [P, TILES])
        wo = sa("wo", [P, D])

        with ExitStack() as ctx:
            s1 = alloc(ctx)
            wcat = s1("wcat", [P, 512])
            bcat = s1("bcat", [P, 512])
            wab = s1("wab", [P, 2])
            bab = s1("bab", [P, 2])
            xn = [s1(f"xn{i}", [P, 4, D]) for i in range(CHUNKS)]
            xnT = [s1(f"xnT{i}", [P, 512]) for i in range(CHUNKS)]
            nmr = s1("nmr", [P, TILES])
            z = s1("z", [P, TILES, 2])
            az = s1("az", [P, TILES, 2])
            ez = s1("ez", [P, TILES, 2])
            lz = s1("lz", [P, TILES, 2])
            lb = s1("lb", [P, TILES])
            junk = s1("junk", [P, D])
            ss = s1("ss", [P, TILES])
            s_ln = sem("a_ln")
            s_x1 = sem("a_x1")
            s_wp = sem("a_wp")
            s_xn = sem("a_xn")
            s_tr = sem("a_tr")
            s_xT = sem("a_xT")
            s_pj = sem("a_pj")
            s_ev = sem("a_ev")
            s_az = sem("a_az")
            s_lz = sem("a_lz")
            s_la = sem("a_la")
            s_cum = sem("a_cum")
            s_z = sem("a_z")
            s_sq = sem("a_sq")
            block = ctx.enter_context(nc.Block())

            @block.sync
            def _(sp):
                sp.dma_start(X[:, 0:4, :], a["x"][:, 0:4, :]).then_inc(s_x, 16)
                sp.dma_start(C[:, :, :], a["consts"]).then_inc(s_const, 16)
                sp.dma_start(X[:, 4:TILES, :], a["x"][:, 4:TILES, :]).then_inc(s_x1, 16)
                sp.dma_start(wab[:, :], a["wab"]).then_inc(s_wp, 16)
                sp.dma_start(wcat[:, :], a["wcat"]).then_inc(s_wp, 16)
                sp.dma_start(bcat[:, :], a["bcat"].partition_broadcast(P)).then_inc(s_wp, 16)
                sp.dma_start(bab[:, :], a["bab"].partition_broadcast(P)).then_inc(s_wp, 16)
                sp.dma_start(V[:, :], a["vecs"]).then_inc(s_const, 16)
                sp.dma_start(wo[:, :], a["wo"]).then_inc(s_w0, 16)
                sp.dma_start(bo_b[:, :], a["bo"].partition_broadcast(P)).then_inc(s_w0, 16)
                sp.dma_start(bout_b[:, :], a["bout"].partition_broadcast(P)).then_inc(s_w0, 16)
                sp.dma_start(wr0[:, :], a["wr0"]).then_inc(s_w0, 16)
                sp.dma_start(br0[:, :], a["br0"].partition_broadcast(P)).then_inc(s_w0, 16)
                sp.dma_start(wr1[:, :], a["wr1"]).then_inc(s_w0, 16)
                keyvals.sync(sp)
                sp.wait_ge(s_fillz, 2)
                for n, lo, hi in fills:
                    sp.dma_start(slots[n][lo:hi, :].rearrange("(a p) w -> p a w", p=P),
                                 mid_col(fill[:, :], (hi - lo) // P)).then_inc(s_fill, 16)

            @block.gpsimd
            def _(pool):
                pool.memset(fill[:, :], 0.0).then_inc(s_fillz, 1)
                pool.wait_ge(s_fillz, 1)
                pool.memset(fill[:, DEST:DEST + 1], FAR).then_inc(s_fillz, 1)

            @block.vector
            def _(dve):
                def norm(lo, hi):
                    moments(dve, chain, X, st6, mv, range(lo, hi))
                    deviations(dve, chain, mv[:, lo:hi, :], var[:, lo:hi], rstd[:, lo:hi], tmp[:, lo:hi])
                    dve.scalar_tensor_tensor(nmr[:, lo:hi], mv[:, lo:hi, 0], -1.0, rstd[:, lo:hi], ALU.mult, ALU.mult).then_inc(s_ln, 1)

                def evict(n):
                    dve.wait_ge(s_pj, n + 1)
                    dve.tensor_tensor(kvqg[:, n, :, :].rearrange("p c n -> p (c n)"),
                                      bank[2 + n % 4][:, :], bcat[:, :], ALU.add).then_inc(s_ev, 1)

                def normalize(g):
                    for k in range(4):
                        j = 4 * g + k
                        last = dve.tensor_scalar(xn[g][:, k, :], X[:, j, :], mv[:, j, 0:1], rstd[:, j:j + 1],
                                                 ALU.subtract, ALU.mult)
                    last.then_inc(s_xn, 1)

                dve.wait_ge(s_x, 16)
                moments(dve, chain, X, st6, mv, range(4))
                deviations(dve, chain, mv[:, 0:4, :], var[:, 0:4], rstd[:, 0:4], tmp[:, 0:4])
                normalize(0)
                dve.wait_ge(s_x1, 16)
                norm(4, TILES)
                normalize(1)
                dve.wait_ge(s_wp, 64)
                for n in range(4):
                    evict(n)
                dve.wait_ge(s_z, 1)
                chain.run(dve, dve.tensor_tensor(z[:, :, :], bank[6][:, 0:2 * TILES].rearrange("p (a n) -> p a n", n=2),
                                            mid_col(bab[:, :], TILES), ALU.add))
                dve.scalar_tensor_tensor(az[:, :, :], z[:, :, :], -1.0, z[:, :, :], ALU.mult, ALU.max).then_inc(s_az, 1)
                for n in range(4, 10):
                    evict(n)
                dve.wait_ge(s_lz, 2)
                dve.scalar_tensor_tensor(lb[:, :], z[:, :, 1], 0.0, lz[:, :, 1], ALU.min, ALU.subtract).then_inc(s_la, 1)
                dve.scalar_tensor_tensor(la[:, :], z[:, :, 0], 0.0, lz[:, :, 0], ALU.min, ALU.subtract).then_inc(s_la, 1)
                for n in range(10, TILES):
                    evict(n)
                dve.wait_ge(s_sq, TILES)
                chain.run(dve, dve.tensor_scalar(ss[:, :], ss[:, :], 1e-24, None, ALU.max))
                rsqrt(dve, chain, ss[:, :], rn[:, :], tmp[:, :])
                dve.wait_ge(s_w0, 16 * 6)

            @block.tensor
            def _(pe):
                def turn(g):
                    pe.wait_ge(s_xn, g + 1)
                    if g >= 2:
                        pe.wait_ge(s_xT, g - 1)
                    for k in range(4):
                        last = pe.transpose(bank[g % 2][:, k * P:(k + 1) * P], xn[g][:, k, :], ident)
                    last.then_inc(s_tr, 1)

                def gates(g):
                    pe.wait_ge(s_xT, g + 1)
                    for k in range(4):
                        n = 4 * g + k
                        last = pe.matmul(bank[6][:, n * 2:n * 2 + 2], xnT[g][:, k * P:(k + 1) * P], wab[:, :], start=True, stop=True)
                    return last

                def project(g):
                    for k in range(4):
                        if g:
                            pe.wait_ge(s_ev, 4 * g + k - 3)
                        pe.matmul(bank[2 + k][:, :], xnT[g][:, k * P:(k + 1) * P], wcat[:, :],
                                  start=True, stop=True).then_inc(s_pj, 1)

                pe.wait_ge(s_const, 32)
                turn(0)
                pe.wait_ge(s_wp, 64)
                gates(0)
                project(0)
                turn(1)
                turn(2)
                turn(3)
                gates(1)
                gates(2)
                gates(3).then_inc(s_z, 1)
                project(1)
                project(2)
                project(3)
                pe.wait_ge(s_la, 2)
                pe.matmul(bank[7][:, 0:16], C[:, TRI_INC, :], la[:, :], start=True, stop=True)
                pe.matmul(bank[7][:, 16:32], C[:, LOW_STRICT, :], la[:, :], start=True, stop=True)
                pe.matmul(bank[7][:, 32:48], C[:, ONES, :], la[:, :], start=True, stop=True).then_inc(s_cum, 1)
                pe.wait_ge(s_w0, 16 * 6)

            @block.scalar
            def _(act):
                def square(n):
                    act.wait_ge(s_ev, n + 1)
                    if n:
                        act.wait_ge(s_sq, n)
                    act.activation(junk[:, :], kvqg[:, n, 0, :], ACT.Square, accum_out=ss[:, n:n + 1]).then_inc(s_sq, 1)

                def turned(g):
                    act.wait_ge(s_tr, g + 1)
                    act.activation(xnT[g][:, :], bank[g % 2][:, :], ACT.Copy).then_inc(s_xT, 1)

                turned(0)
                act.wait_ge(s_ln, 1)
                for g in (2, 3):
                    act.wait_ge(s_xn, g)
                    for k in range(4):
                        j = 4 * g + k
                        last = act.activation(xn[g][:, k, :], X[:, j, :], ACT.Identity, bias=nmr[:, j:j + 1], scale=rstd[:, j:j + 1])
                    last.then_inc(s_xn, 1)
                for g in (1, 2, 3):
                    turned(g)
                act.wait_ge(s_az, 1)
                act.activation(ez[:, :, :], az[:, :, :], ACT.Exp, scale=-1.0).then_inc(s_lz, 1)
                act.wait_ge(s_lz, 1)
                act.activation(lz[:, :, :], ez[:, :, :], ACT.Ln, bias=1.0).then_inc(s_lz, 1)
                for n in range(8):
                    square(n)
                act.wait_ge(s_la, 1)
                act.activation(beta[:, :], lb[:, :], ACT.Exp)
                for n in range(8, TILES):
                    square(n)
                act.wait_ge(s_cum, 1)
                act.activation(dec[:, :, :].rearrange("p a n -> p (a n)"), bank[7][:, 0:48], ACT.Exp)
                act.activation(kvqg[:, :, 3, :], kvqg[:, :, 3, :], ACT.Sigmoid)

        with ExitStack() as ctx:
            s2 = alloc(ctx)
            bgK = s2("bgK", [P, TILES, P])
            EK = s2("EK", [P, TILES, P])
            QT = s2("QT", [P, TILES, P])
            gQT = s2("gQT", [P, TILES, P])
            gateT = s2("gateT", [P, TILES, P])
            DT = s2("DT", [P, TILES, P])
            AT = s2("AT", [P, TILES, P])
            AM = s2("AM", [P, TILES, P])
            XL = s2("XL", [P, TILES, P])
            TI = s2("TI", [P, TILES, P])
            RI = s2("RI", [P, TILES, P])
            t_a = s2("t_a", [P, 4, P])
            kb, gQ, rla = TI, XL, AM
            d_kn = sem("b_kn")
            d_kb = sem("b_kb")
            p_el = sem("b_el")
            p_dt = sem("b_dt")
            q_tr = sem("b_tr")
            q_lt = sem("b_lt")
            q_at = sem("b_at")
            a_ev = sem("b_aev")
            a_lt = sem("b_alt")
            d_ev = sem("b_dev")
            d_at = sem("b_dat")
            d_r0 = sem("b_r0")
            d_c = sem("b_dvec")
            q_t0 = sem("b_t0")
            a_t0 = sem("b_at0")
            p_am = sem("b_am")
            q_x = sem("b_x")
            a_x = sem("b_ax")
            q_y = sem("b_y")
            d_t = sem("b_t")
            q_r = sem("b_r")
            a_r = sem("b_ar")
            KTb = s2("KTb", [P, 4, P])
            kbTb = s2("kbTb", [P, 4, P])

            with nc.Block() as block:
                def grp(t, g):
                    return t[:, 4 * g:4 * g + 4, :]

                def col(t, g):
                    return last_col(t[:, 4 * g:4 * g + 4], P)

                def kv(g, c):
                    return kvqg[:, 4 * g:4 * g + 4, c, :]

                @block.vector
                def _(dve):
                    for g in range(CHUNKS):
                        dve.tensor_tensor(kv(g, 0), kv(g, 0), col(rn, g), ALU.mult).then_inc(d_kn, 1)
                        dve.wait_ge(d_kn, g + 1)
                        dve.tensor_tensor(grp(kb, g), kv(g, 0), col(beta, g), ALU.mult).then_inc(d_kb, 1)
                        dve.tensor_tensor(kv(g, 1), kv(g, 1), col(beta, g), ALU.mult).then_inc(d_kb, 1)
                    dve.tensor_tensor(bd[:, :], beta[:, :], dec[:, 0, :], ALU.mult).then_inc(d_kn, 1)
                    for g in range(CHUNKS):
                        dve.wait_ge(q_tr, 5 * g + 3)
                        dve.tensor_copy(grp(QT, g), quad(bank[2][:, :])).then_inc(d_ev, 1)
                        dve.wait_ge(q_tr, 5 * g + 5)
                        dve.tensor_copy(grp(gateT, g), quad(bank[4][:, :])).then_inc(d_ev, 1)
                        dve.wait_ge(q_at, g + 1)
                        dve.wait_ge(p_dt, g + 1)
                        dve.tensor_tensor(grp(AT, g), quad(bank[6][:, :]), grp(DT, g), ALU.mult).then_inc(d_at, 1)
                        dve.wait_ge(d_at, g + 1)
                        if g:
                            dve.wait_ge(d_r0, g)
                        dve.tensor_tensor(t_a[:, :, :], grp(AT, g), mid_col(C[:, PAIRS, :], 4), ALU.mult).then_inc(d_c, 1)
                        dve.wait_ge(d_c, g + 1)
                        dve.tensor_tensor(grp(RI, g), mid_col(ident, 4), t_a[:, :, :], ALU.subtract).then_inc(d_r0, 1)
                    chain.run(dve, dve.tensor_tensor(X[:, :, :], X[:, :, :], mid_col(bo_b[:, :], TILES), ALU.add))
                    with dve.Fori(1, LEVELS) as lv:
                        for g in range(CHUNKS):
                            dve.wait_ge(q_y, lv * 4 + (g + 1 - 4))
                            dve.tensor_tensor(grp(TI, g), grp(TI, g), quad(bank[4 + g][:, :]), ALU.subtract).then_inc(d_t, 1)

                @block.gpsimd
                def _(pool):
                    for g in range(CHUNKS):
                        pool.tensor_tensor(grp(rla, g), mid_col(C[:, TRI_INC, :], 4), col(la, g), ALU.mult).then_inc(p_el, 1)
                        pool.tensor_tensor(grp(gQ, g), kv(g, 2), last_col(dec[:, 0, 4 * g:4 * g + 4], P), ALU.mult).then_inc(p_el, 1)
                        pool.wait_ge(a_lt, g + 1)
                        pool.tensor_tensor(grp(DT, g), grp(DT, g), mid_col(C[:, TRI_INC, :], 4), ALU.mult).then_inc(p_dt, 1)
                    pool.wait_ge(q_lt, CHUNKS)
                    for lv in range(1, LEVELS):
                        for g in range(CHUNKS):
                            pool.wait_ge(d_at, g + 1)
                            pool.wait_ge(q_x, lv * 4 + (g + 1 - 4))
                            pool.tensor_tensor(grp(AM, g), grp(AT, g),
                                               mid_col(C[:, PAIRS + lv, :], 4),
                                               ALU.mult).then_inc(p_am, 1)
                        if lv <= CHUNKS:
                            g = lv - 1
                            pool.wait_ge(d_kn, CHUNKS + 1)
                            pool.tensor_tensor(grp(EK, g), kv(g, 0), last_col(dec[:, 1, 4 * g:4 * g + 4], P), ALU.mult)
                            pool.tensor_tensor(grp(bgK, g), kv(g, 0), col(bd, g), ALU.mult)

                @block.tensor
                def _(pe):
                    pe.sem_inc(q_x, 4)
                    for g in range(CHUNKS):
                        pe.wait_ge(p_el, 2 * g + 1)
                        if g:
                            pe.wait_ge(a_lt, g)
                        pe.matmul(bank[5][:, :], C[:, LOW_STRICT, :], grp(rla, g).rearrange("p a n -> p (a n)"),
                                  start=True, stop=True).then_inc(q_lt, 1)
                        pe.wait_ge(d_kb, 2 * g + 2)
                        pe.wait_ge(p_el, 2 * g + 2)
                        for i, src in enumerate((kv(g, 0), grp(kb, g), kv(g, 2), grp(gQ, g), kv(g, 3))):
                            if g:
                                if i in (2, 4):
                                    pe.wait_ge(d_ev, 2 * g - (1 if i == 2 else 0))
                                else:
                                    pe.wait_ge(a_ev, 3 * (g - 1) + {0: 1, 1: 2, 3: 3}[i])
                            for b in range(SEQS):
                                last = pe.transpose(bank[i][:, b * P:(b + 1) * P], src[:, b, :], ident)
                            last.then_inc(q_tr, 1)
                        pe.wait_ge(a_ev, 3 * g + 2)
                        if g:
                            pe.wait_ge(d_at, g)
                        for b in range(SEQS):
                            last = pe.matmul(bank[6][:, b * P:(b + 1) * P], KTb[:, b, :], kbTb[:, b, :], start=True, stop=True)
                        last.then_inc(q_at, 1)
                    for g in range(CHUNKS):
                        pe.wait_ge(d_r0, g + 1)
                        pe.wait_ge(a_lt, CHUNKS)
                        if g >= 2:
                            pe.wait_ge(a_t0, g - 1)
                        for b in range(SEQS):
                            last = pe.transpose(bank[7 - g % 2 * 2][:, b * P:(b + 1) * P], RI[:, 4 * g + b, :], ident)
                        last.then_inc(q_t0, 1)
                    pe.wait_ge(a_t0, CHUNKS)
                    pe.wait_ge(a_ev, 3 * CHUNKS)
                    pe.wait_ge(d_ev, 2 * CHUNKS)
                    with pe.Fori(1, LEVELS) as lv:
                        for g in range(CHUNKS):
                            pe.wait_ge(a_r, lv * 4 + (g + 1 - 4))
                            pe.wait_ge(p_am, lv * 4 + (g + 1 - 4))
                            for b in range(SEQS):
                                last = pe.matmul(bank[g][:, b * P:(b + 1) * P], AM[:, 4 * g + b, :], TI[:, 4 * g + b, :],
                                                 start=True, stop=True)
                            last.then_inc(q_x, 1)
                        for g in range(CHUNKS):
                            pe.wait_ge(a_x, lv * 4 + (g + 1 - 4))
                            for b in range(SEQS):
                                last = pe.matmul(bank[4 + g][:, b * P:(b + 1) * P], RI[:, 4 * g + b, :], XL[:, 4 * g + b, :],
                                                 start=True, stop=True)
                            last.then_inc(q_y, 1)
                        for g in range(CHUNKS):
                            pe.wait_ge(d_t, lv * 4 + (g + 1 - 4))
                            for b in range(SEQS):
                                last = pe.transpose(bank[g][:, b * P:(b + 1) * P], TI[:, 4 * g + b, :], ident)
                            last.then_inc(q_r, 1)

                @block.scalar
                def _(act):
                    act.sem_inc(a_r, 4)
                    for g in range(CHUNKS):
                        act.wait_ge(q_lt, g + 1)
                        act.activation(grp(DT, g), quad(bank[5][:, :]), ACT.Exp).then_inc(a_lt, 1)
                        act.wait_ge(q_tr, 5 * g + 1)
                        if g:
                            act.wait_ge(q_at, g)
                        act.activation(KTb[:, :, :], quad(bank[0][:, :]), ACT.Copy).then_inc(a_ev, 1)
                        act.wait_ge(q_tr, 5 * g + 2)
                        act.activation(kbTb[:, :, :], quad(bank[1][:, :]), ACT.Copy).then_inc(a_ev, 1)
                        act.wait_ge(q_tr, 5 * g + 4)
                        act.activation(grp(gQT, g), quad(bank[3][:, :]), ACT.Copy).then_inc(a_ev, 1)
                    for g in range(CHUNKS):
                        act.wait_ge(q_t0, g + 1)
                        act.activation(grp(TI, g), quad(bank[7 - g % 2 * 2][:, :]), ACT.Copy).then_inc(a_t0, 1)
                    with act.Fori(1, LEVELS) as lv:
                        for g in range(CHUNKS):
                            act.wait_ge(q_x, lv * 4 + (g + 1))
                            act.activation(grp(XL, g), quad(bank[g][:, :]), ACT.Copy).then_inc(a_x, 1)
                        for g in range(CHUNKS):
                            act.wait_ge(q_r, lv * 4 + (g + 1 - 4))
                            act.activation(grp(RI, g), quad(bank[g][:, :]), ACT.Copy).then_inc(a_r, 1)

            nZT, U, UT, M = AT, AM, XL, TI
            S = s2("S", [P, 4, P])
            ST = s2("ST", [P, 4, P])
            Sg = s2("Sg", [P, 4, P])
            STg = s2("STg", [P, 4, P])
            c_zt = sem("c_zt")
            c_nzt = sem("c_nzt")
            c_u = sem("c_u")
            c_ue = sem("c_ue")
            c_ut = sem("c_ut")
            c_ute = sem("c_ute")
            c_m = sem("c_m")
            c_me = sem("c_me")
            c_o = sem("c_o")
            c_oe = sem("c_oe")
            c_out = sem("c_out")
            c_x = sem("c_x")
            c_s = sem("c_s")
            c_st = sem("c_st")
            c_se = sem("c_se")
            c_g = sem("c_g")
            with nc.Block() as block:
                GO = bgK

                @block.tensor
                def _(pe):
                    def mm4(dst, pairs):
                        for b in range(SEQS):
                            for i, (l, r) in enumerate(pairs):
                                last = pe.matmul(dst[:, b * P:(b + 1) * P], l(b), r(b), start=(i == 0), stop=(i == len(pairs) - 1))
                        return last

                    def at(t, g):
                        return lambda b: t[:, 4 * g + b, :]

                    def kvb(g, c):
                        return lambda b: kvqg[:, 4 * g + b, c, :]

                    def zt(g):
                        if g:
                            pe.wait_ge(c_nzt, g)
                        mm4(bank[0], [(at(bgK, g), at(RI, g))]).then_inc(c_zt, 1)

                    def project(g):
                        pe.wait_ge(c_oe, g + 1)
                        if g:
                            pe.wait_ge(c_x, g)
                        mm4(bank[5], [(at(GO, g), lambda b: wo[:, :])]).then_inc(c_out, 1)

                    zt(0)
                    for g in range(CHUNKS):
                        pe.wait_ge(c_nzt, g + 1)
                        if g:
                            pe.wait_ge(c_se, 2 * g - 1)
                        old = [(at(nZT, g), lambda b: ST[:, b, :])] if g else []
                        old_t = [(lambda b: ST[:, b, :], at(nZT, g))] if g else []
                        mm4(bank[1], [(at(RI, g), kvb(g, 1))] + old).then_inc(c_u, 1)
                        mm4(bank[2], [(kvb(g, 1), at(RI, g))] + old_t).then_inc(c_ut, 1)
                        if g < CHUNKS - 1:
                            pe.wait_ge(c_ue, g + 1)
                            mm4(bank[6], [(at(EK, g), at(U, g))]).then_inc(c_st, 1)
                            mm4(bank[7], [(at(U, g), at(EK, g))]).then_inc(c_s, 1)
                        pe.wait_ge(c_ute, g + 1)
                        if g:
                            pe.wait_ge(c_me, g)
                        mm4(bank[3], [(at(UT, g), at(QT, g))]).then_inc(c_m, 1)
                        if g < CHUNKS - 1:
                            zt(g + 1)
                        if g:
                            project(g - 1)
                        pe.wait_ge(c_me, g + 1)
                        if g:
                            pe.wait_ge(c_se, 2 * g)
                        old_o = [(lambda b: S[:, b, :], at(gQT, g))] if g else []
                        mm4(bank[4], [(kvb(g, 0), at(M, g))] + old_o).then_inc(c_o, 1)
                    project(CHUNKS - 1)

                @block.scalar
                def _(act):
                    def nzt(g):
                        act.wait_ge(c_zt, g + 1)
                        act.activation(grp(nZT, g), quad(bank[0][:, :]), ACT.Copy, scale=-1.0).then_inc(c_nzt, 1)

                    nzt(0)
                    for g in range(CHUNKS):
                        act.wait_ge(c_ut, g + 1)
                        act.activation(grp(UT, g), quad(bank[2][:, :]), ACT.Copy).then_inc(c_ute, 1)
                        if g < CHUNKS - 1:
                            nzt(g + 1)

                @block.gpsimd
                def _(pool):
                    for g in range(1, CHUNKS - 1):
                        pool.wait_ge(c_se, 2 * g)
                        for src, dst in ((ST, STg), (S, Sg)):
                            pool.tensor_tensor(dst[:, :, :], src[:, :, :], last_col(dec[:, 2, 4 * g:4 * g + 4], P),
                                               ALU.mult).then_inc(c_g, 1)

                @block.vector
                def _(dve):
                    for g in range(CHUNKS):
                        dve.wait_ge(c_u, g + 1)
                        dve.tensor_copy(grp(U, g), quad(bank[1][:, :])).then_inc(c_ue, 1)
                        if g < CHUNKS - 1:
                            dve.wait_ge(c_st, g + 1)
                            dve.wait_ge(c_ut, g + 1)
                            if g:
                                dve.wait_ge(c_g, 2 * g)
                                dve.tensor_tensor(ST[:, :, :], STg[:, :, :], quad(bank[6][:, :]), ALU.add).then_inc(c_se, 1)
                            else:
                                dve.tensor_copy(ST[:, :, :], quad(bank[6][:, :])).then_inc(c_se, 1)
                        dve.wait_ge(c_m, g + 1)
                        dve.tensor_tensor(grp(M, g), quad(bank[3][:, :]), grp(DT, g), ALU.mult).then_inc(c_me, 1)
                        if g:
                            dve.wait_ge(c_out, g)
                            dve.tensor_tensor(grp(X, g - 1), grp(X, g - 1), quad(bank[5][:, :]), ALU.add).then_inc(c_x, 1)
                        dve.wait_ge(c_o, g + 1)
                        if g < CHUNKS - 1:
                            dve.wait_ge(c_s, g + 1)
                            if g:
                                dve.tensor_tensor(S[:, :, :], Sg[:, :, :], quad(bank[7][:, :]), ALU.add).then_inc(c_se, 1)
                            else:
                                dve.tensor_copy(S[:, :, :], quad(bank[7][:, :])).then_inc(c_se, 1)
                        dve.tensor_tensor(grp(GO, g), quad(bank[4][:, :]), grp(gateT, g), ALU.mult).then_inc(c_oe, 1)
                        if g:
                            dve.wait_ge(c_x, g)
                            moments(dve, chain, X, st6, mv, range(4 * g - 4, 4 * g))
                    g = CHUNKS - 1
                    dve.wait_ge(c_out, CHUNKS)
                    dve.tensor_tensor(grp(X, g), grp(X, g), quad(bank[5][:, :]), ALU.add).then_inc(c_x, 1)
        ab.close()

        ffn = ExitStack()
        sf = alloc(ffn)
        w1a = sf("w1a", [P, E * F])
        w2a = sf("w2a", [P, E * F])
        b1a = sf("b1a", [P, E * F])
        b2a = sf("b2a", [P, E * D])

        route(nc, top, chain, bank, a, X, C, V, wr0, br0, mv, st6, var, rstd, tmp, plan_i, expert_i, slots[0], s_fill, 16 * len(fills), keyvals,
              [(w1a, "w1a"), (w2a, "w2a"), (b1a, "b1a"), (b2a, "b2a")], s_ffn0)
        experts(nc, top, chain, bank, 0, X, C, (w1a, w2a, b1a, b2a, None, None), expert_i, slots[0], byrow[0], s_ffn0, 64, None, s_out)
        ffn.close()
        kvx.close()

        with ExitStack() as ctx1:
            s7 = alloc(ctx1)
            u1 = s7("u1", [P, E * F])
            ug = s7("ug", [P, E * F])
            u2 = s7("u2", [P, E * F])
            c1 = s7("c1", [P, E * F])
            cg = s7("cg", [P, E * F])
            c2 = s7("c2", [P, E * D])
            attention(nc, top, chain, bank, a, X, C, V, Kq, VW, wr1, norm, byrow[0], plan_i, cum, expert_i, start_i, slots[1],
                      [(u1, "w1b"), (ug, "wgb"), (u2, "w2b"), (c1, "b1b"), (cg, "bgb"), (c2, "b2b")], s_ffn1)
            experts(nc, top, chain, bank, 1, X, C, (u1, u2, c1, c2, ug, cg), expert_i, slots[1], byrow[1], s_ffn1, 96, out,
                    s_out, start_i)


def route(nc, top, chain, bank, a, X, C, V, wr, br, mv, st6, var, rstd, tmp, plan_i, expert_i, slots, s_fill, fill_count, keyvals, ffn_loads, s_ffn):
    NT = slot_tiles(1)
    ident = C[:, IDENT, :]

    def sem(name):
        return top.enter_context(nc.semaphore(f"r_{name}"))

    with ExitStack() as ctx:
        def sb(name, shape, dt=F32):
            return ctx.enter_context(nc.sbuf_tensor(f"r_{name}", shape, dt))

        rows = sb("rows", [P, TILES, ROW])
        xnT = [sb(f"xnT{i}", [P, 512]) for i in range(CHUNKS)]
        lg = sb("lg", [P, TILES, E])
        wk = sb("wk", [P, TILES, E])
        ex = sb("ex", [P, TILES, E])
        mx = sb("mx", [P, TILES])
        sm = sb("sm", [P, TILES])
        one = sb("one", [P, TILES, E])
        tot = sb("tot", [P, E, TILES])
        run = sb("run", [P, E, TILES])
        cnt = sb("cnt", [P, E, TILES])
        ntl = sb("ntl", [P, E])
        end = sb("end", [P, E])
        beg = sb("beg", [P, E])
        base = sb("base", [P, TILES, E])
        pos = sb("pos", [P, TILES])
        ew = sb("ew", [1, NT, E])
        ef = sb("ef", [1, NT])
        s_row, s_tr, s_xT, s_lg, s_ex, s_exd, s_one, s_rank, s_plan, s_sc = (
            sem(n) for n in ("row", "tr", "xT", "lg", "ex", "exd", "one", "rank", "plan", "sc"))
        block = ctx.enter_context(nc.Block())
        LG, WITHIN, TOTAL = bank[4][:, 0:P], bank[5][:, 0:P], bank[6][:, 0:P]

        keyvals.place_products(sb)

        @block.sync
        def _(sp):
            for t, name in ffn_loads:
                src = a[name]
                if len(src.shape) == 1:
                    src = src.partition_broadcast(P)
                sp.dma_start(t[:, :], src).then_inc(s_ffn, 16)

        def te(ap):
            return ap.rearrange("p (a n) -> p a n", n=E)

        @block.vector
        def _(dve):
            moments(dve, chain, X, st6, mv, range(TILES - 4, TILES))
            deviations(dve, chain, mv, var, rstd, tmp)
            for j in range(TILES):
                dve.tensor_scalar(rows[:, j, 0:D], X[:, j, :], mv[:, j, 0:1], rstd[:, j:j + 1],
                                  ALU.subtract, ALU.mult).then_inc(s_row, 1)
            dve.tensor_copy(rows[:, :, DEST:DEST + 1], V[:, V_ROW:V_ROW + TILES].unsqueeze(2))
            dve.wait_ge(s_lg, 1)
            chain.run(dve, dve.tensor_tensor(lg[:, :, :], te(LG), mid_col(br[:, :], TILES), ALU.add))
            chain.run(dve, dve.tensor_reduce(mx[:, :], lg[:, :, :], AX.X, ALU.max))
            dve.tensor_tensor(wk[:, :, :], lg[:, :, :], last_col(mx[:, :], E), ALU.subtract).then_inc(s_ex, 1)
            dve.wait_ge(s_exd, 1)
            chain.run(dve, dve.tensor_reduce(sm[:, :], ex[:, :, :], AX.X, ALU.add))
            chain.run(dve, dve.reciprocal(sm[:, :], sm[:, :]))
            chain.run(dve, dve.tensor_tensor(ex[:, :, :], ex[:, :, :], last_col(sm[:, :], E), ALU.mult))
            chain.run(dve, dve.tensor_reduce(mx[:, :], ex[:, :, :], AX.X, ALU.max))
            dve.tensor_tensor(wk[:, :, :], ex[:, :, :], last_col(mx[:, :], E), ALU.is_ge)
            chain.run(dve, dve.tensor_copy(rows[:, :, GATE:GATE + 1], mx[:, :].unsqueeze(2)))
            chain.run(dve, dve.tensor_tensor(wk[:, :, :], wk[:, :, :], mid_col(V[:, V_EM8:V_EM8 + E], TILES), ALU.mult))
            chain.run(dve, dve.tensor_reduce(sm[:, :], wk[:, :, :], AX.X, ALU.min))
            dve.tensor_tensor(one[:, :, :], mid_col(V[:, V_EM8:V_EM8 + E], TILES), last_col(sm[:, :], E),
                              ALU.is_equal).then_inc(s_one, 1)
            dve.wait_ge(s_rank, 1)
            chain.run(dve, dve.tensor_copy(tot[:, :, :], te(TOTAL).rearrange("p a n -> p n a")))
            chain.run(dve, dve.tensor_tensor_scan(run[:, :, :].rearrange("p a n -> p (a n)"), V[:, V_SCAN:V_SCAN + P],
                                             tot[:, :, :].rearrange("p a n -> p (a n)"), 0.0, ALU.mult, ALU.add))
            dve.tensor_tensor(cnt[:, :, :], run[:, :, TILES - 1:TILES].broadcast_to([P, E, TILES]),
                              mid_col(V[:, V_KTH:V_KTH + TILES], E), ALU.is_gt)
            chain.run(dve, dve.tensor_tensor(tot[:, :, :], run[:, :, :], tot[:, :, :], ALU.subtract))
            dve.tensor_reduce(ntl[:, :], cnt[:, :, :], AX.X, ALU.add)
            chain.run(dve, dve.tensor_tensor(base[:, :, :], te(WITHIN), tot[:, :, :].rearrange("p a n -> p n a"), ALU.add))
            chain.run(dve, dve.tensor_tensor_scan(end[:, :], C[:, ONES, 0:E], ntl[:, :], 0.0, ALU.mult, ALU.add))
            chain.run(dve, dve.tensor_tensor(beg[:, :], end[:, :], ntl[:, :], ALU.subtract))
            chain.run(dve, dve.scalar_tensor_tensor(base[:, :, :], mid_col(beg[:, :], TILES), float(P), base[:, :, :],
                                                    ALU.mult, ALU.add))
            dve.wait_ge(s_one, 1)
            chain.run(dve, dve.tensor_tensor(wk[:, :, :], base[:, :, :], one[:, :, :], ALU.mult))
            chain.run(dve, dve.tensor_reduce(pos[:, :], wk[:, :, :], AX.X, ALU.add))
            dve.tensor_copy(plan_i[:, 0:TILES], pos[:, :]).then_inc(s_plan, 1)
            chain.run(dve, dve.tensor_tensor(ew[:, :, 0:E - 1], last_col(V[0:1, V_TILE:V_TILE + NT], E - 1),
                                        mid_col(end[0:1, 0:E - 1], NT), ALU.is_ge))
            chain.run(dve, dve.tensor_reduce(ef[:, :], ew[:, :, 0:E - 1], AX.X, ALU.add))
            chain.run(dve, dve.tensor_copy(expert_i[:, 0:NT], ef[:, :]))
            keyvals.vector(dve)

        @block.tensor
        def _(pe):
            def turn(g):
                pe.wait_ge(s_row, 4 * g + 4)
                for k in range(4):
                    last = pe.transpose(bank[g][:, k * P:(k + 1) * P], rows[:, 4 * g + k, 0:D], ident)
                last.then_inc(s_tr, 1)

            def router(g):
                pe.wait_ge(s_xT, g + 1)
                for k in range(4):
                    n = 4 * g + k
                    last = pe.matmul(LG[:, n * E:(n + 1) * E], xnT[g][:, k * P:(k + 1) * P], wr[:, :], start=True, stop=True)
                return last

            keyvals.tensor(pe, 0, 1)
            for left in (keyvals.s_kte, keyvals.s_vte, keyvals.s_bq, keyvals.s_vwe):
                pe.wait_ge(left, 1)
            turn(0)
            for g in range(CHUNKS):
                if g < CHUNKS - 1:
                    turn(g + 1)
                last = router(g)
            last.then_inc(s_lg, 1)
            keyvals.tensor(pe, 1, 2)
            pe.wait_ge(s_one, 1)
            pe.matmul(WITHIN, C[:, UP_STRICT, :], one[:, :, :].rearrange("p a n -> p (a n)"), start=True, stop=True)
            pe.matmul(TOTAL, C[:, ONES, :], one[:, :, :].rearrange("p a n -> p (a n)"), start=True, stop=True).then_inc(s_rank, 1)
            keyvals.tensor(pe, 2, HEADS)

        @block.scalar
        def _(act):
            keyvals.scalar(act, 0, 1)
            for g in range(CHUNKS):
                act.wait_ge(s_tr, g + 1)
                act.activation(xnT[g][:, :], bank[g][:, :], ACT.Copy).then_inc(s_xT, 1)
            act.wait_ge(s_ex, 1)
            act.activation(ex[:, :, :], wk[:, :, :], ACT.Exp).then_inc(s_exd, 1)
            keyvals.scalar(act, 1, 2)
            keyvals.scalar(act, 2, HEADS)

        @block.gpsimd
        def _(pool):
            pool.wait_ge(s_fill, fill_count)
            pool.wait_ge(s_plan, 1)
            for n in range(TILES):
                pool.indirect_dma_start(out=slots, out_offset=bass.IndirectOffsetOnAxis(
                    ap=plan_i[:, n:n + 1].bitcast(U32), axis=0), in_=rows[:, n, :], in_offset=None).then_inc(s_sc, 16)
            pool.wait_ge(s_sc, 16 * TILES)


def experts(nc, top, chain, bank, layer, X, C, weights, expert_i, slots, byrow, s_w, w_count, out, s_out, start_i=None):
    w1, w2, b1, b2, wg, bg = weights
    K = layer + 1
    NT = slot_tiles(K)
    gated = wg is not None
    ident = C[:, IDENT, :]

    def sem(name):
        return top.enter_context(nc.semaphore(f"e{layer}_{name}"))

    with ExitStack() as ctx:
        def sb(name, shape, dt=F32):
            return ctx.enter_context(nc.sbuf_tensor(f"e{layer}_{name}", shape, dt))

        xs = [sb(f"xs{i}", [P, ROW]) for i in range(4)]
        xT = [sb(f"xT{i}", [P, P]) for i in range(2)]
        h = [sb(f"h{i}", [P, F]) for i in range(2)]
        hg = [sb(f"hg{i}", [P, F]) for i in range(2)] if gated else None
        hT = [sb(f"hT{i}", [P, F]) for i in range(2)]
        y = [sb(f"y{i}", [P, D]) for i in range(4)]
        dst = sb("dst", [P, NT], I32)
        gate = sb("gate", [P, NT])
        back = sb("back", [P, CHUNKS, K, 4, D]) if out is not None else None
        s_xs = [sem(f"xs{i}") for i in range(4)]
        s_sc = [sem(f"sc{i}") for i in range(4)]
        s_xt, s_xT, s_h, s_hs, s_t, s_hT, s_y, s_yb, s_yg, s_take, s_bk = (
            sem(n) for n in ("xt", "xT", "h", "hs", "t", "hT", "y", "yb", "yg", "take", "bk"))
        if gated:
            s_g, s_gs, s_ge, s_p = (sem(n) for n in ("g", "gs", "ge", "p"))
        block = ctx.enter_context(nc.Block())
        BX, BH, BG, BT, BY = bank[0], (bank[1], bank[7]), bank[2], bank[3:5], bank[5:7]
        Q = NT // 4

        def tiles(eng, body, weights=None, what=expert_i, most=E - 1):
            regs = [eng.alloc_register(f"expert{layer}_{j}") for j in range(6)] if weights else []

            def fetch(i, lo, n):
                if weights:
                    at = what[0:1, bass.ds(i + lo, n - lo)] if not isinstance(i, int) else what[0:1, i + lo:i + n]
                    eng.load(regs[lo + 1:n + 1], at)
                return [None] * (lo + 1) + [nc.snap(r).with_bounds(min_val=0, max_val=most) for r in regs[lo + 1:n + 1]] + [None] * 8

            e = fetch(0, 0, 5)
            if weights:
                weights(e[1])
            for i in range(4):
                body(i, i, e[i:])
            with eng.Fori(1, Q) as q:
                e = fetch(q * 4, -1, 5)
                for k in range(4):
                    body(q * 4 + k, k, e[k:])
            e = fetch(4 * Q, -1, NT - 4 * Q)
            for i in range(4 * Q, NT):
                body(i, i % 4, e[i % 4:])
            return e[NT % 4]

        def inside(i):
            return not isinstance(i, int) or 0 <= i < NT

        def later(i):
            return not isinstance(i, int) or i >= 4

        @block.sync
        def _(sp):
            def load(i, k, e):
                if later(i):
                    sp.wait_ge(s_xt, i - 3)
                    sp.wait_ge(s_take, i - 3)
                if start_i is not None:
                    src = slots[bass.ds(e[1], P), :]
                else:
                    src = slots[bass.ds(i * P, P), :] if not isinstance(i, int) else slots[i * P:(i + 1) * P, :]
                sp.dma_start(xs[k][:, :], src).then_inc(s_xs[k], 16)

            if start_i is not None:
                tiles(sp, load, lambda e: None, start_i, slots.shape[0] - P)
            else:
                tiles(sp, load)
            for k in range(4):
                sp.wait_ge(s_sc[k], 16 * len(range(k, NT, 4)))
            if out is not None:
                by_token = byrow.rearrange("(c p j) d -> p c j d", c=K, p=P)
                for g in range(CHUNKS):
                    sp.dma_start(back[:, g, :, :, :], by_token[:, :, 4 * g:4 * g + 4, :]).then_inc(s_xs[g], 16)
                for g in range(CHUNKS):
                    sp.wait_ge(s_bk, g + 1)
                    sp.dma_start(out[:, 4 * g:4 * g + 4, :], X[:, 4 * g:4 * g + 4, :]).then_inc(s_out, 16)
                sp.wait_ge(s_out, 16 * CHUNKS)

        @block.tensor
        def _(pe):
            def turn(i, k):
                if inside(i):
                    pe.wait_ge(s_xs[k], (i - k) * 4 + 16)
                    pe.wait_ge(s_xT, i + 1)
                    pe.transpose(BX[:, 0:P], xs[k][:, 0:D], ident).then_inc(s_xt, 1)

            def hidden_gate(i, k, e):
                if gated and inside(i):
                    pe.wait_ge(s_xT, i + 2)
                    pe.wait_ge(s_gs, i + 1)
                    pe.matmul(BG[:, :], xT[k % 2][:, :], wg[:, bass.ds(e * F, F)], start=True, stop=True).then_inc(s_g, 1)

            def hidden(i, k, e):
                if inside(i):
                    pe.wait_ge(s_xT, i + 2)
                    pe.wait_ge(s_hs, i + 1)
                    pe.matmul(BH[k % 2][:, :], xT[k % 2][:, :], w1[:, bass.ds(e * F, F)], start=True, stop=True).then_inc(s_h, 1)

            def turn_hidden(i, k):
                src = hg if gated else h
                if gated:
                    pe.wait_ge(s_p, i + 1)
                else:
                    pe.wait_ge(s_hs, i + 3)
                pe.wait_ge(s_hT, i + 1)
                for t in range(FT):
                    last = pe.transpose(BT[k % 2][:, t * P:(t + 1) * P], src[k % 2][:, t * P:(t + 1) * P], ident)
                last.then_inc(s_t, 1)

            def result(i, k, e):
                if inside(i):
                    pe.wait_ge(s_hT, i + 3)
                    pe.wait_ge(s_yb, i + 1)
                    for t in range(FT):
                        last = pe.matmul(BY[k % 2][:, 0:D], hT[k % 2][:, t * P:(t + 1) * P], w2[:, bass.ds(e * F + t * D, D)],
                                         start=(t == 0), stop=(t == FT - 1))
                    last.then_inc(s_y, 1)

            def body(i, k, e):
                if gated:
                    hidden_gate(i + 1, (k + 1) % 4, e[2])
                    turn(i + 2, (k + 2) % 4)
                    result(i - 1, (k - 1) % 4, e[0])
                    turn_hidden(i, k)
                    hidden(i + 1, (k + 1) % 4, e[2])
                else:
                    hidden(i + 1, (k + 1) % 4, e[2])
                    turn(i + 2, (k + 2) % 4)
                    result(i - 1, (k - 1) % 4, e[0])
                    turn_hidden(i, k)

            def first(e):
                turn(0, 0)
                hidden_gate(0, 0, e)
                hidden(0, 0, e)
                turn(1, 1)

            pe.wait_ge(s_w, w_count)
            e = tiles(pe, body, first)
            result(NT - 1, (NT - 1) % 4, e)

        @block.scalar
        def _(act):
            def turned(i, k):
                if inside(i):
                    act.wait_ge(s_xt, i + 1)
                    act.activation(xT[k % 2][:, :], BX[:, 0:P], ACT.Copy).then_inc(s_xT, 1)

            def gelu(i, k):
                if gated and inside(i):
                    act.wait_ge(s_gs, i + 2)
                    act.activation(hg[k % 2][:, :], hg[k % 2][:, :], ACT.Gelu).then_inc(s_ge, 1)

            def body(i, k, _):
                turned(i + 2, (k + 2) % 4)
                gelu(i + 1, (k + 1) % 4)
                act.wait_ge(s_t, i + 1)
                act.activation(hT[k % 2][:, :], BT[k % 2][:, :], ACT.Copy if gated else ACT.Relu).then_inc(s_hT, 1)

            act.sem_inc(s_xT, 1)
            act.sem_inc(s_hT, 2)
            turned(0, 0)
            gelu(0, 0)
            turned(1, 1)
            tiles(act, body)

        @block.vector
        def _(dve):
            def bias_gate(i, k, e):
                if gated and inside(i):
                    dve.wait_ge(s_g, i + 1)
                    dve.tensor_tensor(hg[k % 2][:, :], BG[:, :], bg[:, bass.ds(e * F, F)], ALU.add).then_inc(s_gs, 1)

            def bias(i, k, e):
                if inside(i):
                    dve.wait_ge(s_h, i + 1)
                    dve.tensor_tensor(h[k % 2][:, :], BH[k % 2][:, :], b1[:, bass.ds(e * F, F)], ALU.add).then_inc(s_hs, 1)

            def result(i, k, e):
                if inside(i):
                    if later(i):
                        dve.wait_ge(s_sc[k], (i - k) * 4)
                    dve.wait_ge(s_y, i + 1)
                    dve.tensor_tensor(y[k][:, :], BY[k % 2][:, 0:D], b2[:, bass.ds(e * D, D)], ALU.add).then_inc(s_yb, 1)
                    dve.wait_ge(s_yb, i + 3)
                    dve.wait_ge(s_take, i + 1)
                    g = gate[:, bass.ds(i, 1)] if not isinstance(i, int) else gate[:, i:i + 1]
                    dve.tensor_scalar(y[k][:, :], y[k][:, :], g, None, ALU.mult).then_inc(s_yg, 1)

            def body(i, k, e):
                if gated:
                    dve.wait_ge(s_ge, i + 1)
                    dve.wait_ge(s_hs, i + 3)
                    dve.tensor_tensor(hg[k % 2][:, :], hg[k % 2][:, :], h[k % 2][:, :], ALU.mult).then_inc(s_p, 1)
                    bias_gate(i + 1, (k + 1) % 4, e[2])
                    result(i - 1, (k - 1) % 4, e[0])
                    bias(i + 1, (k + 1) % 4, e[2])
                else:
                    bias(i + 1, (k + 1) % 4, e[2])
                    result(i - 1, (k - 1) % 4, e[0])

            def first(e):
                bias_gate(0, 0, e)
                bias(0, 0, e)

            dve.sem_inc(s_hs, 2)
            if gated:
                dve.sem_inc(s_gs, 1)
            dve.sem_inc(s_yb, 2)
            e = tiles(dve, body, first)
            result(NT - 1, (NT - 1) % 4, e)
            for g in range(CHUNKS if out is not None else 0):
                dve.wait_ge(s_xs[g], 16 * len(range(g, NT, 4)) + 16)
                xg = X[:, 4 * g:4 * g + 4, :]
                for c in range(K):
                    chain.run(dve, dve.tensor_tensor(xg, xg, back[:, g, c, :, :], ALU.add))
                dve.sem_inc(s_bk, 1)

        @block.gpsimd
        def _(pool):
            def take(i):
                pool.wait_ge(s_xs[i % 4], 16 * (i // 4) + 16)
                pool.tensor_copy(dst[:, i:i + 1], xs[i % 4][:, DEST:DEST + 1])
                pool.tensor_copy(gate[:, i:i + 1], xs[i % 4][:, GATE:GATE + 1]).then_inc(s_take, 1)

            take(0)
            take(1)
            for i in range(NT):
                k = i % 4
                if i + 2 < NT:
                    take(i + 2)
                pool.wait_ge(s_take, i + 1)
                pool.wait_ge(s_yg, i + 1)
                pool.indirect_dma_start(out=byrow, out_offset=bass.IndirectOffsetOnAxis(
                    ap=dst[:, i:i + 1].bitcast(U32), axis=0), in_=y[k][:, :], in_offset=None,
                    bounds_check=K * TILES * P - 1, oob_is_err=False).then_inc(s_sc[k], 16)


def attention(nc, top, chain, bank, a, X, C, V, Kq, VW, wr, norm, byrow, plan_i, cum, expert_i, start_i, slots, ffn_loads, s_ffn1):
    ident = C[:, IDENT, :]

    def sem(name):
        return top.enter_context(nc.semaphore(f"t_{name}"))

    with ExitStack() as ctx:
        def sb(name, shape, dt=F32):
            return ctx.enter_context(nc.sbuf_tensor(f"t_{name}", shape, dt))

        st6, mv, var, rstd, tmp = norm
        xnT = sb("xnT", [P, TILES * P])
        back = sb("back", [P, CHUNKS, 4, D])
        xn = [sb(f"xn{i}", [P, 4, D]) for i in range(2)]
        s_back = [sem(f"back{g}") for g in range(CHUNKS)]
        s_xn, s_tr, s_xT = (sem(n) for n in ("xn", "tr", "xT"))
        xq = [sb(f"xq{i}", [P, P]) for i in range(2)]
        Pr = [sb(f"Pr{i}", [P, KEYS]) for i in range(2)]
        PT = [sb(f"PT{i}", [P, KEYS]) for i in range(2)]
        nmx = sb("nmx", [P, 16])
        den = sb("den", [P, 16])
        rec = sb("rec", [P, 16])
        s_mo = sem("mo")
        s_q, s_s, s_m, s_e, s_t, s_pt, s_o, s_rc, s_acc = (
            sem(n) for n in ("q", "s", "m", "e", "t", "pt", "o", "rc", "acc"))
        UN = 2 * HEADS
        PAIRS_N = TILES // 2
        BS, BT, BO, BR = bank[0:4], bank[4:6], bank[6], bank[7]
        x1 = sb("x1", [P, D])
        pad = sb("pad", [P, 2])
        st1 = sb("st1", [P, 6])
        mv2 = sb("mv2", [P, 2, 2])
        var2, rs2, tmp2, mx2, sm2 = (sb(n, [P, 2]) for n in ("var2", "rs2", "tmp2", "mx2", "sm2"))
        pos2 = sb("pos2", [P, 2, 2])
        rows = [[sb(f"rows{c}{h}", [P, ROW]) for h in range(2)] for c in range(2)]
        last_rows = [[sb(f"last{c}{h}", [P, ROW]) for h in range(2)] for c in range(2)]
        xT2 = sb("xT2", [P, 2 * P])
        wk2, ex2, both2, base2 = (sb(n, [P, 2, E]) for n in ("wk2", "ex2", "both2", "base2"))
        pair2 = sb("pair2", [P, E])
        one2 = sb("one2", [P, 2, 2, E])
        wk4 = sb("wk4", [P, 2, 2, E])
        s_rx, s_rt, s_rxT, s_rl, s_rs, s_rex, s_rone, s_rr, s_plan, s_dup, s_free, s_sc, s_link, s_cum = (
            sem(n) for n in ("rx", "rt", "rxT", "rl", "rs", "rex", "rone", "rr", "plan", "dup", "free", "sc", "link", "cum"))
        LOGITS, WITHIN, TOTAL = BR[:, 256:256 + 2 * E], BR[:, 288:288 + 2 * E], BR[:, 320:320 + E]

        def pe2(ap):
            return ap.rearrange("p (a n) -> p a n", n=E)

        def at(i, n=1):
            return bass.ds(i, n) if not isinstance(i, int) else slice(i, i + n)

        def each_pair(eng, body):
            body(0, None)
            with eng.Fori(1, PAIRS_N) as tt:
                body(tt, tt - 1)

        NT = slot_tiles(2)
        num, ntl, end, skip = (sb(n, [1, E]) for n in ("num", "ntl", "end", "skip"))
        cnt = sb("cnt", [1, E, TILES])
        ew = sb("ew", [1, NT, E - 1])
        ef = sb("ef", [1, NT])

        def slot_table(dve):
            chain.run(dve, dve.scalar_tensor_tensor(num[:, :], V[0:1, V_EM8:V_EM8 + E], -float(REGION), cum[0:1, :], ALU.mult, ALU.add))
            chain.run(dve, dve.tensor_scalar(num[:, :], num[:, :], -float(E * REGION), None, ALU.add))
            chain.run(dve, dve.tensor_tensor(cnt[:, :, :], last_col(num[:, :], TILES), mid_col(V[0:1, V_KTH:V_KTH + TILES], E), ALU.is_gt))
            chain.run(dve, dve.tensor_reduce(ntl[:, :], cnt[:, :, :], AX.X, ALU.add))
            chain.run(dve, dve.tensor_tensor_scan(end[:, :], C[0:1, ONES, 0:E], ntl[:, :], 0.0, ALU.mult, ALU.add))
            chain.run(dve, dve.tensor_tensor(ew[:, :, :], last_col(V[0:1, V_TILE:V_TILE + NT], E - 1), mid_col(end[:, 0:E - 1], NT), ALU.is_ge))
            chain.run(dve, dve.tensor_reduce(ef[:, :], ew[:, :, :], AX.X, ALU.add))
            chain.run(dve, dve.tensor_copy(expert_i[:, 0:NT], ef[:, :]))
            chain.run(dve, dve.tensor_scalar(skip[:, :], ntl[:, :], -float(P), float(REGION), ALU.mult, ALU.add))
            chain.run(dve, dve.tensor_tensor(ew[:, :, :], ew[:, :, :], mid_col(skip[:, 0:E - 1], NT), ALU.mult))
            chain.run(dve, dve.tensor_reduce(ef[:, :], ew[:, :, :], AX.X, ALU.add))
            chain.run(dve, dve.scalar_tensor_tensor(ef[:, :], V[0:1, V_TILE:V_TILE + NT], float(P), ef[:, :], ALU.mult, ALU.add))
            chain.run(dve, dve.tensor_copy(start_i[:, 0:NT], ef[:, :]))

        with nc.Block() as block:
            @block.sync
            def _(sp):
                by_token = byrow.rearrange("(p j) d -> p j d", p=P)
                for g in range(CHUNKS):
                    sp.dma_start(back[:, g, :, :], by_token[:, 4 * g:4 * g + 4, :]).then_inc(s_back[g], 16)
                for t, name in ffn_loads:
                    src = a[name]
                    if len(src.shape) == 1:
                        src = src.partition_broadcast(P)
                    sp.dma_start(t[:, :], src).then_inc(s_ffn1, 16)

            @block.gpsimd
            def _(pool):
                def query(t, scored):
                    if scored:
                        pool.wait_ge(s_s, scored)
                    for step, (lo, _) in enumerate(NORMS):
                        if t == lo:
                            pool.wait_ge(s_xT, step + 1)
                    pool.tensor_copy(xq[t % 2][:, :], xnT[:, t % TILES * P:(t % TILES + 1) * P]).then_inc(s_q, 1)

                def send(r, rows):
                    pool.wait_ge(s_rx, r + 1)
                    for h in range(2):
                        pool.tensor_copy(rows[1][h][:, 0:D], rows[0][h][:, 0:D]).then_inc(s_dup, 1)
                    pool.wait_ge(s_dup, 2 * r + 2)
                    pool.wait_ge(s_plan, r + 1)
                    for c in range(2):
                        for h in range(2):
                            n = c * TILES + 2 * r + h
                            pool.indirect_dma_start(out=slots, out_offset=bass.IndirectOffsetOnAxis(
                                ap=plan_i[:, n:n + 1].bitcast(U32), axis=0), in_=rows[c][h][:, :], in_offset=None).then_inc(s_sc, 16)

                pool.sem_inc(s_free, 1)
                query(0, 0)
                for tt in range(PAIRS_N):
                    query(2 * tt + 1, 16 * tt + 1 if tt else 0)
                    if tt >= 2:
                        pool.wait_ge(s_sc, 64 * (tt - 1))
                        pool.sem_inc(s_free, 1)
                    query(2 * tt + 2, 16 * tt + HEADS + 1)
                    if tt:
                        send(tt - 1, rows)
                send(PAIRS_N - 1, last_rows)
                pool.wait_ge(s_sc, 64 * PAIRS_N)

            @block.tensor
            def _(pe):
                def score(n, u):
                    pe.wait_ge(s_e, n + 1)
                    hd = u % HEADS
                    pe.matmul(BS[u % 4][:, :], xq[u // HEADS][:, :], Kq[:, hd, :], start=True, stop=True).then_inc(s_s, 1)

                def turn_group(step):
                    pe.wait_ge(s_xn, step + 1)
                    if step:
                        pe.wait_ge(s_xT, step)
                    for j in range(*NORMS[step]):
                        k = j % 4
                        last = pe.transpose(BR[:, k * P:(k + 1) * P], xn[j // 4 % 2][:, k, :], ident)
                    last.then_inc(s_tr, 1)

                def turn(r, rows):
                    pe.wait_ge(s_rx, r + 1)
                    for h in range(2):
                        last = pe.transpose(BR[:, h * P:(h + 1) * P], rows[0][h][:, 0:D], ident)
                    last.then_inc(s_rt, 1)

                def router(r):
                    pe.wait_ge(s_rxT, r + 1)
                    for h in range(2):
                        last = pe.matmul(LOGITS[:, h * E:(h + 1) * E], xT2[:, h * P:(h + 1) * P], wr[:, :], start=True, stop=True)
                    last.then_inc(s_rl, 1)

                def rank(r):
                    pe.wait_ge(s_rone, r + 1)
                    up, ones = C[:, UP_STRICT, :], C[:, ONES, :]
                    pe.matmul(WITHIN, up, both2[:, :, :].rearrange("p a n -> p (a n)"), start=True, stop=False)
                    pe.matmul(WITHIN[:, E:2 * E], ones, both2[:, 0, :], start=False, stop=True)
                    pe.matmul(TOTAL, ones, pair2[:, :], start=True, stop=True).then_inc(s_rr, 1)

                def body(tt, r):
                    for u in range(UN):
                        n = tt * UN + u
                        nx = u + 2
                        if nx == HEADS:
                            pe.wait_ge(s_q, tt * 2 + 2)
                        if nx == UN:
                            pe.wait_ge(s_q, tt * 2 + 3)
                        pe.wait_ge(s_e, n + 5)
                        pe.wait_ge(s_pt, n + 1)
                        for t in range(KT_N):
                            last = pe.transpose(BT[u % 2][:, t * P:(t + 1) * P], Pr[u % 2][:, t * P:(t + 1) * P], ident)
                        last.then_inc(s_t, 1)
                        score(n + 2, nx % UN)
                        if r is None and u == 4:
                            turn_group(1)
                        if r is None and u >= 13:
                            turn_group(u - 11)
                        if r is not None and u == 5:
                            turn(r, rows)
                        if r is not None and u == 7:
                            router(r)
                        if r is not None and u == 14:
                            rank(r)
                        pe.wait_ge(s_pt, n + 3)
                        pe.wait_ge(s_acc, n + 2)
                        for t in range(KT_N):
                            last = pe.matmul(BO[:, 0:D], PT[u % 2][:, t * P:(t + 1) * P], VW[:, u % HEADS, t, :],
                                             start=(t == 0), stop=(t == KT_N - 1))
                        last.then_inc(s_o, 1)

                turn_group(0)
                pe.wait_ge(s_q, 1)
                score(0, 0)
                score(1, 1)
                each_pair(pe, body)
                r = PAIRS_N - 1
                turn(r, last_rows)
                router(r)
                rank(r)

            @block.scalar
            def _(act):
                def exps(n, u):
                    act.wait_ge(s_m, n + 1)
                    act.activation(Pr[u % 2][:, :], BS[u % 4][:, :], ACT.Exp, bias=nmx[:, u:u + 1],
                                   accum_out=den[:, u:u + 1]).then_inc(s_e, 1)

                act.sem_inc(s_e, 4)
                act.sem_inc(s_pt, 2)

                def turned_group(step):
                    lo, hi = NORMS[step]
                    act.wait_ge(s_tr, step + 1)
                    act.activation(xnT[:, lo * P:hi * P], BR[:, lo % 4 * P:(lo % 4 + hi - lo) * P], ACT.Copy).then_inc(s_xT, 1)

                turned_group(0)
                exps(0, 0)

                def turned(r):
                    act.wait_ge(s_rt, r + 1)
                    act.activation(xT2[:, :], BR[:, 0:2 * P], ACT.Copy).then_inc(s_rxT, 1)

                def softmax(r):
                    act.wait_ge(s_rs, r + 1)
                    act.activation(ex2[:, :, :], wk2[:, :, :], ACT.Exp).then_inc(s_rex, 1)

                def body(tt, r):
                    for u in range(UN):
                        n = tt * UN + u
                        act.wait_ge(s_t, n + 1)
                        act.activation(PT[u % 2][:, :], BT[u % 2][:, :], ACT.Copy).then_inc(s_pt, 1)
                        exps(n + 1, (u + 1) % UN)
                        if r is None and u == 4:
                            turned_group(1)
                        if r is None and u >= 13:
                            turned_group(u - 11)
                        if r is not None and u == 5:
                            turned(r)
                        if r is not None and u == 9:
                            softmax(r)

                each_pair(act, body)
                turned(PAIRS_N - 1)
                softmax(PAIRS_N - 1)

            @block.vector
            def _(dve):
                def top(n, u):
                    dve.wait_ge(s_s, n + 1)
                    dve.tensor_reduce(nmx[:, u:u + 1], BS[u % 4][:, :], AX.X, ALU.max, negate=True).then_inc(s_m, 1)

                count = 0

                def link(r, ins, beside=None):
                    nonlocal count
                    count += 1
                    ins.then_inc(s_link, 1)
                    if beside is not None:
                        beside()
                    dve.wait_ge(s_link, r * LINKS + count)

                def add_back(step):
                    lo, hi = NORMS[step]
                    g = lo // 4
                    dve.wait_ge(s_back[g], 16)
                    xg = X[:, lo:hi, :]
                    chain.run(dve, dve.tensor_tensor(xg, xg, back[:, g, lo - 4 * g:hi - 4 * g, :], ALU.add))

                def deviations_of(lo, hi):
                    deviations(dve, chain, mv[:, lo:hi, :], var[:, lo:hi], rstd[:, lo:hi], tmp[:, lo:hi])

                def normalize_group(step):
                    if step >= 3:
                        dve.wait_ge(s_tr, step - 1)
                    for j in range(*NORMS[step]):
                        last = dve.tensor_scalar(xn[j // 4 % 2][:, j % 4, :], X[:, j, :], mv[:, j, 0:1], rstd[:, j:j + 1],
                                                 ALU.subtract, ALU.mult)
                    last.then_inc(s_xn, 1)

                def first_turn(u):
                    if u == 0:
                        add_back(1)
                        moments(dve, chain, X, st6, mv, range(*NORMS[1]))
                    if u == 1:
                        deviations_of(*NORMS[1])
                    if u == 2:
                        normalize_group(1)
                    if 3 <= u < 6:
                        add_back(u - 1)
                    if 6 <= u < 9:
                        moments(dve, chain, X, st6, mv, range(*NORMS[u - 4]))
                    if u == 8:
                        chain.run(dve, dve.tensor_scalar(var[:, 4:TILES], mv[:, 4:TILES, 1], EPS, None, ALU.add))
                        rsqrt_seed(dve, chain, var[:, 4:TILES], rstd[:, 4:TILES])
                    if 9 <= u < 12:
                        rsqrt_step(dve, chain, var[:, 4:TILES], rstd[:, 4:TILES], tmp[:, 4:TILES])
                    if 11 <= u < 14:
                        normalize_group(u - 9)

                def moments_of(j, half, n):
                    dve.wait_ge(s_acc, n + 3)
                    dve.tensor_scalar(x1[:, :], X[:, at(j), :].rearrange("p a n -> p (a n)"), 1.0, None, ALU.mult).then_inc(s_mo, 1)
                    dve.wait_ge(s_mo, j * 3 + 1)
                    dve.tensor_scalar(pad[:, 0:1], ident[:, 0:1], 1.0, None, ALU.mult)
                    dve.bn_stats(st1[:, :], x1[:, :]).then_inc(s_mo, 1)
                    dve.wait_ge(s_mo, j * 3 + 2)
                    dve.tensor_scalar(pad[:, 1:2], ident[:, 0:1], 1.0, None, ALU.mult)
                    dve.bn_aggr(mv2[:, half, :], st1[:, :]).then_inc(s_mo, 1)

                def seed(r):
                    dve.wait_ge(s_mo, r * 6 + 6)
                    link(r, dve.tensor_scalar(var2[:, :], mv2[:, :, 1], EPS, None, ALU.add))
                    link(r, dve.tensor_scalar(rs2[:, :].bitcast(I32), var2[:, :].bitcast(I32), 1, None, ALU.logical_shift_right))
                    link(r, dve.tensor_scalar(rs2[:, :].bitcast(I32), rs2[:, :].bitcast(I32), -1.0, float(0x5F3759DF), ALU.mult, ALU.add))

                def newton(r):
                    link(r, dve.tensor_tensor(tmp2[:, :], rs2[:, :], rs2[:, :], ALU.mult))
                    link(r, dve.scalar_tensor_tensor(tmp2[:, :], tmp2[:, :], -0.5, var2[:, :], ALU.mult, ALU.mult))
                    link(r, dve.scalar_tensor_tensor(rs2[:, :], tmp2[:, :], 1.5, rs2[:, :], ALU.add, ALU.mult))

                def normalize(r, rows):
                    for h in range(2):
                        xj = X[:, at(r * 2 + h), :].rearrange("p a n -> p (a n)")
                        last = dve.tensor_scalar(rows[0][h][:, 0:D], xj, mv2[:, h, 0:1], rs2[:, h:h + 1], ALU.subtract, ALU.mult)
                    last.then_inc(s_rx, 1)
                    for c in range(2):
                        for h in range(2):
                            last = dve.tensor_scalar(rows[c][h][:, DEST:DEST + 1], V[:, at(r * 2 + (V_ROW + h))],
                                                     float(c * TILES * P), None, ALU.add)
                    link(r, last)

                def shift(r):
                    dve.wait_ge(s_rl, r + 1)
                    link(r, dve.tensor_reduce(mx2[:, :], pe2(LOGITS), AX.X, ALU.max))
                    dve.tensor_tensor(wk2[:, :, :], pe2(LOGITS), last_col(mx2[:, :], E), ALU.subtract).then_inc(s_rs, 1)

                def divide(r):
                    dve.wait_ge(s_rex, r + 1)
                    link(r, dve.tensor_reduce(sm2[:, :], ex2[:, :, :], AX.X, ALU.add))
                    link(r, dve.reciprocal(sm2[:, :], sm2[:, :]))
                    link(r, dve.tensor_tensor(ex2[:, :, :], ex2[:, :, :], last_col(sm2[:, :], E), ALU.mult))

                def choose(r, c, rows):
                    def gates():
                        for h in range(2):
                            dve.tensor_scalar(rows[c][h][:, GATE:GATE + 1], mx2[:, h:h + 1], 1.0, None, ALU.mult)

                    link(r, dve.tensor_reduce(mx2[:, :], ex2[:, :, :], AX.X, ALU.max))
                    link(r, dve.tensor_tensor(wk2[:, :, :], ex2[:, :, :], last_col(mx2[:, :], E), ALU.is_ge), gates)
                    link(r, dve.tensor_tensor(wk2[:, :, :], wk2[:, :, :], mid_col(V[:, V_EM8:V_EM8 + E], 2), ALU.mult))
                    link(r, dve.tensor_reduce(sm2[:, :], wk2[:, :, :], AX.X, ALU.min))
                    link(r, dve.tensor_tensor(one2[:, c, :, :], mid_col(V[:, V_EM8:V_EM8 + E], 2), last_col(sm2[:, :], E), ALU.is_equal))
                    if c == 0:
                        link(r, dve.scalar_tensor_tensor(ex2[:, :, :].rearrange("p a n -> p (a n)"),
                                                         one2[:, 0, :, :].rearrange("p a n -> p (a n)"), -2.0,
                                                         ex2[:, :, :].rearrange("p a n -> p (a n)"), ALU.mult, ALU.add))
                    else:
                        link(r, dve.tensor_tensor(both2[:, :, :], one2[:, 0, :, :], one2[:, 1, :, :], ALU.add))
                        dve.tensor_tensor(pair2[:, :], both2[:, 0, :], both2[:, 1, :], ALU.add).then_inc(s_rone, 1)

                def place(r):
                    dve.wait_ge(s_rr, r + 1)
                    link(r, dve.tensor_tensor(base2[:, :, :], pe2(WITHIN), mid_col(cum[:, :], 2), ALU.add))
                    link(r, dve.tensor_tensor(wk4[:, :, :, :], one2[:, :, :, :],
                                              base2[:, :, :].unsqueeze(1).broadcast_to([P, 2, 2, E]), ALU.mult))
                    link(r, dve.tensor_reduce(pos2[:, :, :], wk4[:, :, :, :], AX.X, ALU.add))
                    for c in range(2):
                        last = dve.tensor_scalar(plan_i[:, at(r * 2 + c * TILES, 2)], pos2[:, c, :], 1.0, None, ALU.mult)
                    last.then_inc(s_plan, 1)
                    link(r, dve.tensor_tensor(cum[:, :], cum[:, :], TOTAL, ALU.add))

                def body(tt, r):
                    nonlocal count
                    count = 0
                    for u in range(UN):
                        n = tt * UN + u
                        top(n + 2, (u + 2) % UN)
                        dve.wait_ge(s_e, n + 5)
                        dve.reciprocal(rec[:, u:u + 1], den[:, u:u + 1]).then_inc(s_rc, 1)
                        dve.wait_ge(s_rc, n + 1)
                        dve.wait_ge(s_o, n + 1)
                        j = tt * 2 + u // HEADS
                        xj = X[:, at(j), :].rearrange("p a n -> p (a n)")
                        dve.wait_ge(s_acc, n + 2)
                        dve.scalar_tensor_tensor(xj, BO[:, 0:D], rec[:, u:u + 1], xj, ALU.mult, ALU.add).then_inc(s_acc, 1)
                        if r is None:
                            first_turn(u)
                        else:
                            if u == 0:
                                seed(r)
                            if u in (1, 2, 3):
                                newton(r)
                            if u == 4:
                                dve.wait_ge(s_free, r + 1)
                                normalize(r, rows)
                            if u == 8:
                                shift(r)
                            if u == 10:
                                divide(r)
                            if u in (11, 12):
                                choose(r, u - 11, rows)
                            if u == 14:
                                place(r)
                        if u % HEADS == HEADS - 1:
                            moments_of(j, u // HEADS, n)

                dve.sem_inc(s_acc, 2)
                dve.tensor_scalar(cum[:, :], V[:, V_EM8:V_EM8 + E], float(E), float(REGION), ALU.add, ALU.mult).then_inc(s_cum, 1)
                dve.wait_ge(s_cum, 1)
                add_back(0)
                moments(dve, chain, X, st6, mv, range(*NORMS[0]))
                deviations_of(*NORMS[0])
                normalize_group(0)
                top(0, 0)
                top(1, 1)
                each_pair(dve, body)
                assert count == LINKS
                r, count = PAIRS_N - 1, 0
                seed(r)
                for _ in range(3):
                    newton(r)
                normalize(r, last_rows)
                shift(r)
                divide(r)
                choose(r, 0, last_rows)
                choose(r, 1, last_rows)
                place(r)
                slot_table(dve)


def kernel(**inp):
    import numpy as np
    import concourse.bacc as bacc
    from concourse import mybir as mb
    from concourse.bass_utils import run_bass_kernel_spmd as run

    g = {k: np.asarray(v) for k, v in inp.items()}
    f = np.float32
    r, c = np.arange(P)[:, None], np.arange(P)[None, :]
    planes = [r == c, r <= c, r > c, r < c, np.ones((P, P))]
    for lv in range(LEVELS):
        m = 1 << lv
        planes.append((r // (2 * m) == c // (2 * m)) & ((r // m) % 2 == 0) & ((c // m) % 2 == 1))
    vecs = np.zeros((P, V_END), f)
    vecs[:, V_EM8:V_EM8 + E] = np.arange(E) - E
    vecs[:, V_KTH:V_KTH + TILES] = P * np.arange(TILES)
    vecs[:, V_TILE:V_TILE + 40] = np.arange(40)
    vecs[:, V_ROW:V_ROW + TILES] = r * TILES + np.arange(TILES)
    vecs[:, V_SCAN:V_SCAN + P] = np.arange(P) % TILES != 0

    def pick(*names):
        return [g["L0_attn_" + n] for n in names]

    ex0, ex1 = g["L0_ffn_W1"], g["L1_ffn_w1_w"]
    arrays = {
        "x": g["L0_attn_x"].reshape(SEQS, CHUNKS, P, D).transpose(2, 1, 0, 3).reshape(P, TILES, D),
        "consts": np.stack(planes, 1).astype(f),
        "vecs": vecs,
        "wcat": np.concatenate(pick("Wk", "Wv", "Wq", "Wg"), 1),
        "bcat": np.concatenate(pick("bk", "bv", "bq", "bg")),
        "wab": np.concatenate(pick("Wa", "Wb"), 1),
        "bab": np.concatenate(pick("ba", "bb")),
        "wo": g["L0_attn_Wo"], "bo": g["L0_attn_bo"], "bout": g["L1_attn_bout"],
        "wr0": g["L0_ffn_Wr"], "br0": g["L0_ffn_br"], "wr1": g["L1_ffn_router_w"].T,
        "w1a": g["L0_ffn_W1"].transpose(1, 0, 2).reshape(D, E * F),
        "b1a": g["L0_ffn_b1"].reshape(-1),
        "w2a": g["L0_ffn_W2"].reshape(E, FT, P, D).transpose(2, 0, 1, 3).reshape(P, E * F),
        "b2a": g["L0_ffn_b2"].reshape(-1),
        "ctxT": g["L1_attn_context"].reshape(KEYS, CTX).T,
        "wk": g["L1_attn_Wk"], "wv": g["L1_attn_Wv"],
        "wqT": g["L1_attn_Wq"].reshape(D, HEADS, P).transpose(2, 1, 0),
        "wout": g["L1_attn_Wout"].reshape(HEADS, P, D).transpose(1, 0, 2),
        "w1b": g["L1_ffn_w1_w"].transpose(2, 0, 1).reshape(D, E * F),
        "wgb": g["L1_ffn_wg_w"].transpose(2, 0, 1).reshape(D, E * F),
        "w2b": g["L1_ffn_w2_w"].reshape(E, D, FT, P).transpose(3, 0, 2, 1).reshape(P, E * F),
        "b1b": g["L1_ffn_w1_b"].reshape(-1), "bgb": g["L1_ffn_wg_b"].reshape(-1), "b2b": g["L1_ffn_w2_b"].reshape(-1),
    }
    nc = bacc.Bacc("TRN2", target_bir_lowering=False, num_devices=1)
    feeds, aps = {}, {}
    for name, arr in arrays.items():
        arr = np.ascontiguousarray(arr)
        feeds[f"in_{name}"] = arr
        aps[name] = nc.dram_tensor(f"in_{name}", arr.shape, mb.dt.from_np(arr.dtype), kind="ExternalInput").ap()
    out = nc.dram_tensor("out_0", (P, TILES, D), F32, kind="ExternalOutput").ap()
    build(nc, aps, out)
    res = run(nc, [feeds], core_ids=[0]).results[0]["out_0"]
    return res.reshape(P, CHUNKS, SEQS, D).transpose(2, 1, 0, 3).reshape(SEQS, CHUNKS * P, D)
```
